# Optimizing a Trainium2 kernel written in Bass

```python
import numpy as np
import jax
import jax.numpy as jnp

def _softmax(x, axis=-1):
    return jax.nn.softmax(x, axis=axis)

def _gelu(x):
    return jax.nn.gelu(x, approximate=True)

def _silu(x):
    return jax.nn.silu(x)

def _sigmoid(x):
    return jax.nn.sigmoid(x)

def _layernorm(x, axis=-1, eps=1e-05):
    m = jnp.mean(x, axis=axis, keepdims=True)
    v = jnp.var(x, axis=axis, keepdims=True)
    return (x - m) / jnp.sqrt(v + eps)

def _scatter_add(tgt, idx, src, axis=0):
    return tgt.at[idx].add(src)

def _segment_sum(src, seg, n):
    return jax.ops.segment_sum(src, seg, n)
kernel_name = 'mk_gnn_resnorm_d4_gnn_r32_01cf53'

def setup_inputs(seed: int=0):
    np.random.seed(seed)
    _w = jnp.asarray

    def _rec_inputs():
        import jax
        import jax.numpy as jnp
        _gk = jax.random.key(seed)
        x = -0.0003929 + 0.9999 * jax.random.normal(jax.random.fold_in(_gk, 1), (1024, 512), jnp.float32)
        src = jax.random.randint(jax.random.fold_in(_gk, 2), (32768,), 0, 1024, jnp.int32)
        dst = jax.random.randint(jax.random.fold_in(_gk, 3), (32768,), 0, 1024, jnp.int32)
        _o = jnp.argsort(dst, stable=True)
        src = src[_o]
        dst = dst[_o]
        edge_attr_8 = -4.48278e-06 + 1.00019 * jax.random.normal(jax.random.fold_in(_gk, 13), (32768, 8), jnp.float32)
        return (x, src, dst, edge_attr_8)
    x, src, dst, edge_attr_8 = _rec_inputs()

    def _L0_gnn_setup():
        import jax, jax.numpy as jnp
        import numpy as np
        L, C, H, E = (1024, 512, 8, 32768)
        D = C // H
        HID = 1024
        EPS = 1e-05

        def _ln(x, g, b):
            mu = jnp.mean(x, axis=-1, keepdims=True)
            var = jnp.var(x, axis=-1, keepdims=True)
            return (x - mu) * jax.lax.rsqrt(var + EPS) * g + b

        def _sparse_attention(z, row, col, bias, Wq, bq, Wk, bk, Wv, bv, Wo, bo):
            q = (z @ Wq + bq).reshape(L, H, D)
            k = (z @ Wk + bk).reshape(L, H, D)
            v = (z @ Wv + bv).reshape(L, H, D)
            scale = 1.0 / jnp.sqrt(jnp.asarray(D, z.dtype))
            scores = jnp.einsum('ehd,ehd->eh', q[row], k[col]) * scale + bias
            m = jax.ops.segment_max(scores, row, num_segments=L)
            p = jnp.exp(scores - m[row])
            ssum = jax.ops.segment_sum(p, row, num_segments=L)
            alpha = p / ssum[row]
            out = jax.ops.segment_sum(alpha[:, :, None] * v[col], row, num_segments=L)
            return out.reshape(L, C) @ Wo + bo
        key = jax.random.key(seed)
        ks = jax.random.split(key, 12)
        s = 0.02
        inp = {'x': jax.random.normal(ks[0], (L, C), jnp.float32), 'row_index': jnp.sort(jax.random.randint(ks[1], (E,), 0, L)), 'col_index': jax.random.randint(ks[2], (E,), 0, L), 'att_bias': jax.random.normal(ks[3], (E, H), jnp.float32), 'Wq': jax.random.normal(ks[4], (C, C), jnp.float32) * s, 'bq': jnp.zeros((C,), jnp.float32), 'Wk': jax.random.normal(ks[5], (C, C), jnp.float32) * s, 'bk': jnp.zeros((C,), jnp.float32), 'Wv': jax.random.normal(ks[6], (C, C), jnp.float32) * s, 'bv': jnp.zeros((C,), jnp.float32), 'Wo': jax.random.normal(ks[7], (C, C), jnp.float32) * s, 'bo': jnp.zeros((C,), jnp.float32), 'ln1_g': jnp.ones((C,), jnp.float32), 'ln1_b': jnp.zeros((C,), jnp.float32), 'ln2_g': jnp.ones((C,), jnp.float32), 'ln2_b': jnp.zeros((C,), jnp.float32), 'W1': jax.random.normal(ks[8], (C, HID), jnp.float32) * s, 'b1': jnp.zeros((HID,), jnp.float32), 'W2': jax.random.normal(ks[9], (HID, C), jnp.float32) * s, 'b2': jnp.zeros((C,), jnp.float32)}
        return inp
    _L0_gnn_all = _L0_gnn_setup()
    _L0_gnn_in = {k: v for k, v in _L0_gnn_all.items() if k in ('Wq', 'bq', 'Wk', 'bk', 'Wv', 'bv', 'Wo', 'bo', 'ln1_g', 'ln1_b', 'ln2_g', 'ln2_b', 'W1', 'b1', 'W2', 'b2')}
    del _L0_gnn_all

    def _L1_gnn_setup():
        import jax, jax.numpy as jnp
        import numpy as np
        N_NODES = 50000
        N_EDGES = 150000
        D_IN = 512
        D_OUT = 512
        LN_EPS = 1e-05
        key = jax.random.key(seed)
        k_x, k_e, k_ws, k_wn = jax.random.split(key, 4)
        x = jax.random.normal(k_x, (N_NODES, D_IN), dtype=jnp.float32)
        edge_index = jax.random.randint(k_e, (2, N_EDGES), 0, N_NODES, dtype=jnp.int64)
        scale = 1.0 / np.sqrt(D_IN)
        w_self = jax.random.normal(k_ws, (D_OUT, D_IN), dtype=jnp.float32) * scale
        w_neigh = jax.random.normal(k_wn, (D_OUT, D_IN), dtype=jnp.float32) * scale
        bias = jnp.zeros((D_OUT,), dtype=jnp.float32)
        gamma = jnp.ones((D_OUT,), dtype=jnp.float32)
        beta = jnp.zeros((D_OUT,), dtype=jnp.float32)
        return {'x': x, 'edge_index': edge_index, 'w_self': w_self, 'w_neigh': w_neigh, 'bias': bias, 'gamma': gamma, 'beta': beta}
    _L1_gnn_all = _L1_gnn_setup()
    _L1_gnn_in = {k: v for k, v in _L1_gnn_all.items() if k in ('w_self', 'w_neigh', 'bias', 'gamma', 'beta')}
    del _L1_gnn_all

    def _L2_gnn_setup():
        import jax, jax.numpy as jnp
        import numpy as np
        N = 3125
        E = 25000
        D_IN = 512
        D_OUT = 512
        EPS = 1e-05
        key = jax.random.key(seed)
        k = jax.random.split(key, 7)
        x = jax.random.normal(k[0], (N, D_IN), dtype=jnp.float32)
        edge_index = jax.random.randint(k[1], (2, E), 0, N, dtype=jnp.int64)
        W_l = jax.random.normal(k[2], (D_OUT, D_IN), dtype=jnp.float32) * 0.02
        b_l = jnp.zeros((D_OUT,), dtype=jnp.float32)
        W_r = jax.random.normal(k[3], (D_OUT, D_IN), dtype=jnp.float32) * 0.02
        gamma = jnp.ones((D_OUT,), dtype=jnp.float32)
        beta = jnp.zeros((D_OUT,), dtype=jnp.float32)
        return {'x': x, 'edge_index': edge_index, 'W_l': W_l, 'b_l': b_l, 'W_r': W_r, 'gamma': gamma, 'beta': beta}
    _L2_gnn_all = _L2_gnn_setup()
    _L2_gnn_in = {k: v for k, v in _L2_gnn_all.items() if k in ('W_l', 'b_l', 'W_r', 'gamma', 'beta')}
    del _L2_gnn_all

    def _L3_gnn_setup():
        import jax, jax.numpy as jnp
        import numpy as np
        N_NODES = 10000
        N_EDGES = 5000
        IN_DIM = 512
        OUT_DIM = 512
        LN_EPS = 1e-05
        key = jax.random.key(seed)
        k_x, k_src, k_ws, k_wn = jax.random.split(key, 4)
        x = jax.random.normal(k_x, (N_NODES, IN_DIM), dtype=jnp.float32)
        edge_src = jax.random.randint(k_src, (N_EDGES,), 0, N_NODES, dtype=jnp.int32)
        edge_dst = jnp.repeat(jnp.arange(N_NODES, dtype=jnp.int32), N_EDGES // N_NODES)
        deg = jnp.full((N_NODES,), float(N_EDGES // N_NODES), dtype=jnp.float32)
        scale = 1.0 / np.sqrt(IN_DIM)
        W_self = jax.random.normal(k_ws, (OUT_DIM, IN_DIM), dtype=jnp.float32) * scale
        W_neigh = jax.random.normal(k_wn, (OUT_DIM, IN_DIM), dtype=jnp.float32) * scale
        bias = jnp.zeros((OUT_DIM,), dtype=jnp.float32)
        gamma = jnp.ones((OUT_DIM,), dtype=jnp.float32)
        beta = jnp.zeros((OUT_DIM,), dtype=jnp.float32)
        return {'x': x, 'edge_src': edge_src, 'edge_dst': edge_dst, 'deg': deg, 'W_self': W_self, 'W_neigh': W_neigh, 'bias': bias, 'gamma': gamma, 'beta': beta}
    _L3_gnn_all = _L3_gnn_setup()
    _L3_gnn_in = {k: v for k, v in _L3_gnn_all.items() if k in ('W_self', 'W_neigh', 'bias', 'gamma', 'beta')}
    del _L3_gnn_all
    return {'x': x, 'src': src, 'dst': dst, 'edge_attr_8': edge_attr_8, 'L0_gnn_Wq': _L0_gnn_in['Wq'], 'L0_gnn_bq': _L0_gnn_in['bq'], 'L0_gnn_Wk': _L0_gnn_in['Wk'], 'L0_gnn_bk': _L0_gnn_in['bk'], 'L0_gnn_Wv': _L0_gnn_in['Wv'], 'L0_gnn_bv': _L0_gnn_in['bv'], 'L0_gnn_Wo': _L0_gnn_in['Wo'], 'L0_gnn_bo': _L0_gnn_in['bo'], 'L0_gnn_ln1_g': _L0_gnn_in['ln1_g'], 'L0_gnn_ln1_b': _L0_gnn_in['ln1_b'], 'L0_gnn_ln2_g': _L0_gnn_in['ln2_g'], 'L0_gnn_ln2_b': _L0_gnn_in['ln2_b'], 'L0_gnn_W1': _L0_gnn_in['W1'], 'L0_gnn_b1': _L0_gnn_in['b1'], 'L0_gnn_W2': _L0_gnn_in['W2'], 'L0_gnn_b2': _L0_gnn_in['b2'], 'L1_gnn_w_self': _L1_gnn_in['w_self'], 'L1_gnn_w_neigh': _L1_gnn_in['w_neigh'], 'L1_gnn_bias': _L1_gnn_in['bias'], 'L1_gnn_gamma': _L1_gnn_in['gamma'], 'L1_gnn_beta': _L1_gnn_in['beta'], 'L2_gnn_W_l': _L2_gnn_in['W_l'], 'L2_gnn_b_l': _L2_gnn_in['b_l'], 'L2_gnn_W_r': _L2_gnn_in['W_r'], 'L2_gnn_gamma': _L2_gnn_in['gamma'], 'L2_gnn_beta': _L2_gnn_in['beta'], 'L3_gnn_W_self': _L3_gnn_in['W_self'], 'L3_gnn_W_neigh': _L3_gnn_in['W_neigh'], 'L3_gnn_bias': _L3_gnn_in['bias'], 'L3_gnn_gamma': _L3_gnn_in['gamma'], 'L3_gnn_beta': _L3_gnn_in['beta']}

def reference(x, src, dst, edge_attr_8, L0_gnn_Wq, L0_gnn_bq, L0_gnn_Wk, L0_gnn_bk, L0_gnn_Wv, L0_gnn_bv, L0_gnn_Wo, L0_gnn_bo, L0_gnn_ln1_g, L0_gnn_ln1_b, L0_gnn_ln2_g, L0_gnn_ln2_b, L0_gnn_W1, L0_gnn_b1, L0_gnn_W2, L0_gnn_b2, L1_gnn_w_self, L1_gnn_w_neigh, L1_gnn_bias, L1_gnn_gamma, L1_gnn_beta, L2_gnn_W_l, L2_gnn_b_l, L2_gnn_W_r, L2_gnn_gamma, L2_gnn_beta, L3_gnn_W_self, L3_gnn_W_neigh, L3_gnn_bias, L3_gnn_gamma, L3_gnn_beta):
    import jax
    import jax.numpy as jnp

    def _L0_gnn_ref(x, att_bias, Wq, bq, Wk, bk, Wv, bv, Wo, bo, ln1_g, ln1_b, ln2_g, ln2_b, W1, b1, W2, b2, row_index, col_index):
        import jax, jax.numpy as jnp
        import numpy as np
        L, C, H, E = (1024, 512, 8, 32768)
        D = C // H
        HID = 1024
        EPS = 1e-05

        def _ln(x, g, b):
            mu = jnp.mean(x, axis=-1, keepdims=True)
            var = jnp.var(x, axis=-1, keepdims=True)
            return (x - mu) * jax.lax.rsqrt(var + EPS) * g + b

        def _sparse_attention(z, row, col, bias, Wq, bq, Wk, bk, Wv, bv, Wo, bo):
            q = (z @ Wq + bq).reshape(L, H, D)
            k = (z @ Wk + bk).reshape(L, H, D)
            v = (z @ Wv + bv).reshape(L, H, D)
            scale = 1.0 / jnp.sqrt(jnp.asarray(D, z.dtype))
            scores = jnp.einsum('ehd,ehd->eh', q[row], k[col]) * scale + bias
            m = jax.ops.segment_max(scores, row, num_segments=L)
            p = jnp.exp(scores - m[row])
            ssum = jax.ops.segment_sum(p, row, num_segments=L)
            alpha = p / ssum[row]
            out = jax.ops.segment_sum(alpha[:, :, None] * v[col], row, num_segments=L)
            return out.reshape(L, C) @ Wo + bo
        z = _ln(x, ln1_g, ln1_b)
        att = _sparse_attention(z, row_index, col_index, att_bias, Wq, bq, Wk, bk, Wv, bv, Wo, bo)
        x = x + att
        z = _ln(x, ln2_g, ln2_b)
        ff = jax.nn.silu(z @ W1 + b1) @ W2 + b2
        return x + ff

    def _L1_gnn_ref(x, edge_index, w_self, w_neigh, bias, gamma, beta):
        import jax, jax.numpy as jnp
        import numpy as np
        N_NODES = 50000
        N_EDGES = 150000
        D_IN = 512
        D_OUT = 512
        LN_EPS = 1e-05
        n = x.shape[0]
        s, d = (edge_index[0], edge_index[1])
        agg = jax.ops.segment_sum(x[s], d, num_segments=n)
        cnt = jax.ops.segment_sum(jnp.ones(s.shape[0], x.dtype), d, num_segments=n)
        agg = agg / jnp.maximum(cnt, 1.0)[:, None]
        h = x @ w_self.T + agg @ w_neigh.T + bias
        mu = jnp.mean(h, axis=-1, keepdims=True)
        var = jnp.mean(jnp.square(h - mu), axis=-1, keepdims=True)
        hn = (h - mu) * jax.lax.rsqrt(var + LN_EPS) * gamma + beta
        return jax.nn.relu(hn)

    def _L2_gnn_ref(x, edge_index, W_l, b_l, W_r, gamma, beta):
        import jax, jax.numpy as jnp
        import numpy as np
        N = 3125
        E = 25000
        D_IN = 512
        D_OUT = 512
        EPS = 1e-05
        n = x.shape[0]
        src, dst = (edge_index[0], edge_index[1])
        summed = jax.ops.segment_sum(x[src], dst, num_segments=n)
        cnt = jax.ops.segment_sum(jnp.ones((src.shape[0],), x.dtype), dst, num_segments=n)
        aggr = summed / jnp.maximum(cnt, 1.0)[:, None]
        h = aggr @ W_l.T + b_l + x @ W_r.T
        mu = jnp.mean(h, axis=0)
        var = jnp.mean(jnp.square(h - mu), axis=0)
        h_norm = (h - mu) * jax.lax.rsqrt(var + EPS) * gamma + beta
        return jax.nn.relu(h_norm)

    def _L3_gnn_ref(x, edge_src, edge_dst, deg, W_self, W_neigh, bias, gamma, beta):
        import jax, jax.numpy as jnp
        import numpy as np
        N_NODES = 10000
        N_EDGES = 5000
        IN_DIM = 512
        OUT_DIM = 512
        LN_EPS = 1e-05
        n = x.shape[0]
        h_self = jnp.einsum('nd,od->no', x, W_self)
        neigh_sum = jax.ops.segment_sum(x[edge_src], edge_dst, num_segments=n)
        neigh_mean = neigh_sum / jnp.maximum(deg, 1.0)[:, None]
        h_neigh = jnp.einsum('nd,od->no', neigh_mean, W_neigh)
        h = h_self + h_neigh + bias
        mu = jnp.mean(h, axis=-1, keepdims=True)
        var = jnp.mean(jnp.square(h - mu), axis=-1, keepdims=True)
        h = (h - mu) * jax.lax.rsqrt(var + LN_EPS)
        return h * gamma + beta
    edge_index = jnp.stack([src, dst])
    deg = jnp.maximum(jax.ops.segment_sum(jnp.ones(dst.shape, jnp.float32), dst, num_segments=1024), 1.0)
    x = _layernorm(x + _L0_gnn_ref(x, edge_attr_8, L0_gnn_Wq, L0_gnn_bq, L0_gnn_Wk, L0_gnn_bk, L0_gnn_Wv, L0_gnn_bv, L0_gnn_Wo, L0_gnn_bo, L0_gnn_ln1_g, L0_gnn_ln1_b, L0_gnn_ln2_g, L0_gnn_ln2_b, L0_gnn_W1, L0_gnn_b1, L0_gnn_W2, L0_gnn_b2, src, dst), axis=-1)
    x = _layernorm(x + _L1_gnn_ref(x, edge_index, L1_gnn_w_self, L1_gnn_w_neigh, L1_gnn_bias, L1_gnn_gamma, L1_gnn_beta), axis=-1)
    x = _layernorm(x + _L2_gnn_ref(x, edge_index, L2_gnn_W_l, L2_gnn_b_l, L2_gnn_W_r, L2_gnn_gamma, L2_gnn_beta), axis=-1)
    x = _layernorm(x + _L3_gnn_ref(x, src, dst, deg, L3_gnn_W_self, L3_gnn_W_neigh, L3_gnn_bias, L3_gnn_gamma, L3_gnn_beta), axis=-1)
    return x

_drawn_inputs = setup_inputs


def setup_inputs(seed=0):
    import zlib

    import numpy as np

    out = dict(_drawn_inputs(seed))
    spreads = {'L0_gnn_bq': (0.0, 0.8),
     'L0_gnn_bk': (0.0, 0.8),
     'L0_gnn_bv': (0.0, 0.267),
     'L0_gnn_bo': (0.0, 0.1),
     'L0_gnn_ln1_g': (1.0, 0.6),
     'L0_gnn_ln1_b': (0.0, 0.666),
     'L0_gnn_ln2_g': (1.0, 0.6),
     'L0_gnn_ln2_b': (0.0, 0.8),
     'L0_gnn_b1': (0.0, 0.363),
     'L0_gnn_b2': (0.0, 0.1),
     'L1_gnn_bias': (0.0, 0.1),
     'L1_gnn_gamma': (1.0, 0.2),
     'L1_gnn_beta': (0.0, 0.1),
     'L2_gnn_b_l': (0.0, 0.8),
     'L2_gnn_gamma': (1.0, 0.2),
     'L2_gnn_beta': (0.0, 0.1),
     'L3_gnn_bias': (0.0, 0.1),
     'L3_gnn_gamma': (1.0, 0.2),
     'L3_gnn_beta': (0.0, 0.1)}
    factors = {'L0_gnn_Wq': 8.0, 'L0_gnn_Wk': 8.0}
    for name, (base, spread) in spreads.items():
        noise = np.random.default_rng([zlib.crc32(name.encode()), seed]).standard_normal(out[name].shape)
        drawn = base * np.exp(spread * noise) if base else spread * noise
        out[name] = jnp.asarray(drawn.astype(out[name].dtype))
    for name, factor in factors.items():
        out[name] = (out[name] * factor).astype(out[name].dtype)
    return out
```

```python
import concourse.bass as bass
from concourse import mybir
from contextlib import ExitStack

N = 1024
C = 512
E = 32768
H = 8
D = C // H
HID = 1024
P = 128
NB = N // P
KC = C // P
HC = HID // P
HALF = 512
EPP = E // P
GT = 4
GE = GT * P
NG = 72
NT = NG * GT
RW = 2 + H
EPS = 1e-5
NEG = -1.0e30
NBANK = 8


def gnn(nc, x, src, dst, edge_attr_8, Wq, bq, Wk, bk, Wv, bv, Wo, bo, ln1_g, ln1_b, ln2_g, ln2_b,
        W1, b1, W2, b2, l1_ws, l1_wn, l1_b, l1_g, l1_be, l2_wl, l2_bl, l2_wr, l2_g, l2_be,
        l3_ws, l3_wn, l3_b, l3_g, l3_be, kv_table, records, weights_t, out):
    f32 = mybir.dt.float32
    i32 = mybir.dt.int32
    i16 = mybir.dt.int16
    bf16 = mybir.dt.bfloat16
    ALU = mybir.AluOpType
    ACT = mybir.ActivationFunctionType
    AX = mybir.AxisListType

    with ExitStack() as ctx:
        def sb(name, shape, dt=f32):
            return ctx.enter_context(nc.sbuf_tensor(name, shape, dt))

        def sem(name):
            return ctx.enter_context(nc.semaphore(name))

        X = sb("X", [P, NB, C])
        HR = sb("HR", [P, NB, C])
        TR = sb("TR", [P, KC, N])
        W = sb("W", [P, 16, C])
        KV = sb("KV", [P, 8192])
        CT = sb("CT", [P, NB, N])
        recs = sb("recs", [P, NT, RW])
        PR = sb("PR", [P, 2048])
        PV = sb("PV", [P, EPP * RW])
        VEC = sb("VEC", [P, 8, C])
        iota_c = sb("iota_c", [P, N], i16)
        iota_pi = sb("iota_pi", [P, 1], i32)
        iota_p = sb("iota_p", [P, 1])
        iota_g = sb("iota_g", [P, NG])
        ident = sb("ident", [P, P])
        ident_b = sb("ident_b", [P, P], bf16)
        before = sb("before", [P, P])
        ones = sb("ones", [P, P])
        bcol = sb("bcol", [P, 2 * KC + HC])
        bq8 = sb("bq8", [P, KC])
        dst_i = sb("dst_i", [P, NT], i32)
        row_i = sb("row_i", [P, EPP], i32)
        small = sb("small", [P, 16, 8])
        pad_i = sb("pad_i", [P, 8], i32)
        gblk = sb("gblk", [P, NG])
        gblk_i = sb("gblk_i", [P, NG], i32)
        stage_rec = sb("stage_rec", [P, 2, 8, RW])
        stage_row = sb("stage_row", [P, 2, 8], i32)
        bmax = sb("bmax", [P, H])
        bmax_all = sb("bmax_all", [P, H])
        cmax = sb("cmax", [P, NB, H])
        shift = sb("shift", [P, NB, H], bf16)
        stats = sb("stats", [P, NB, 6])
        mv = sb("mv", [P, NB, 2])
        var_e = sb("var_e", [P, NB])
        std = sb("std", [P, NB])
        rstd = sb("rstd", [P, NB])
        oh_b = sb("oh_b", [P, 2, GT, P], bf16)
        oh_f = sb("oh_f", [P, 2, GT, P])
        ohT = sb("ohT", [P, 2, GT, P], bf16)
        idx = sb("idx", [P, 2, GT], i32)
        score = sb("score", [P, 2, GT * H])
        zsc = sb("zsc", [P, 2, GT * H])
        prob = sb("prob", [P, 2, GT, H])
        Lacc = sb("Lacc", [P, NB, H])

        Z = KV[:, 0:4096].rearrange("p (b c) -> p b c", b=NB)
        QT = KV[:, 0:4096].rearrange("p (k n) -> p k n", k=KC)
        KTr = KV[:, 4096:8192].rearrange("p (k n) -> p k n", k=KC)
        kvr = KV[:, :].rearrange("p (g j w) -> p g j w", g=2, j=GT)
        hidT = KV[:, :].rearrange("p (k n) -> p k n", k=HC)
        XT = KV[:, 0:4096].rearrange("p (k n) -> p k n", k=KC)
        SQ = KV[:, 4096:8192].rearrange("p (b c) -> p b c", b=NB)
        ctf = CT[:, :, :].rearrange("p b n -> p (b n)")
        attr = ctf[:, 0:2048]
        oh8 = ctf[:, 2048:4096].rearrange("p (b t) -> p b t", b=NB)
        oh8_f = ctf[:, 2048:4096]
        cum = ctf[:, 4096:6144].rearrange("p (b t) -> p b t", b=NB)
        cum_f = ctf[:, 4096:6144]
        pick = ctf[:, 6144:8192].rearrange("p (b t) -> p b t", b=NB)
        zeros_f = ctf[:, 6144:8192]
        rec_src = PV[:, :].rearrange("p (t r) -> p t r", r=RW)
        kvst = PR[:, :].rearrange("p (s w) -> p s w", s=2)
        mask = PR[:, :].rearrange("p (s w) -> p s w", s=2)
        ohd = [PR[:, :].bitcast(bf16).rearrange("p (j n) -> p j n", j=GT),
               PV[:, 0:2048].bitcast(bf16).rearrange("p (j n) -> p j n", j=GT)]
        prod = PR[:, :].rearrange("p (j c) -> p j c", j=GT)
        prod_h = PR[:, :].rearrange("p (a d) -> p a d", d=D)
        pv = PV[:, 0:2048].rearrange("p (j c) -> p j c", j=GT)
        pv_h = PV[:, 0:2048].rearrange("p (j h d) -> p j h d", j=GT, d=D)
        Qs = W[:, 4:16, :].rearrange("p s c -> p (s c)").bitcast(bf16).rearrange(
            "p (s b c) -> p s b c", s=3, b=NB)
        tmpq = recs[:, 0:205, :].rearrange("p t r -> p (t r)")
        src_i = TR[:, 0, 0:EPP].bitcast(i32)
        blk_i = TR[:, 0, EPP:2 * EPP].bitcast(i32)
        degrc = TR[:, 1, :]
        wnat = HR[:, 0:4, :]
        wtr = HR[:, 4:8, :]

        ps = ctx.enter_context(nc.psum_tensor("ps", [P, NBANK, C], f32))
        psb = ps[:, 6, :].bitcast(bf16)

        sums_ps = ps[:, 4, :]
        shift_ps = ps[:, 5, 0:GT * H]
        psum_ps = ps[:, 7, 0:H]

        def kv_count(g, a):
            return g * 8 + (16 - 8 * a)

        ld_edges, ld_x, ld_vec, ld_w = sem("ld_edges"), sem("ld_x"), sem("ld_vec"), sem("ld_w")
        ld_recs, filler_made, filler_stored = sem("ld_recs"), sem("filler_made"), sem("filler_stored")
        consts, dve_consts, attr_put = sem("consts"), sem("dve_consts"), sem("attr_put")
        dve_chain = sem("dve_chain")
        sort_n, sort_mm = sem("sort_n"), sem("sort_mm")
        rows_ready = sem("rows_ready")
        staged = sem("staged")
        scat = [sem("scat0"), sem("scat1")]
        bmax_in, bmax_out = sem("bmax_in"), sem("bmax_out")
        z_rows = sem("z_rows")
        ln_var, ln_std = sem("ln_var"), sem("ln_std")
        tile_full, dve_drained, act_drained = sem("tile_full"), sem("dve_drained"), sem("act_drained")
        q_split = sem("q_split")
        kv_stored = [sem("kv_stored0"), sem("kv_stored1")]
        wt_loaded, wt_stored = sem("wt_loaded"), sem("wt_stored")
        ct_zero, ct_ready, cn_ready = sem("ct_zero"), sem("ct_ready"), sem("cn_ready")
        recs_int = sem("recs_int")
        coh, cmm, cflush = sem("coh"), sem("cmm"), sem("cflush")
        gtab = sem("gtab")
        smm, smax = sem("smm"), sem("smax")
        shift_ready = sem("shift_ready")
        idx_ready, pool_go = sem("idx_ready"), sem("pool_go")
        kv_in = [[sem(f"kv_in{a}{j}") for j in range(GT)] for a in range(2)]
        oh_made, ohT_ps, ohT_sb, ohf_made = sem("oh_made"), sem("ohT_ps"), sem("ohT_sb"), sem("ohf_made")
        q_ps, c_ps, prod_done = sem("q_ps"), sem("c_ps"), sem("prod_done")
        summed, biased, z_made, p_made = sem("summed"), sem("biased"), sem("z_made"), sem("p_made")
        pv_made, agg_done, flushed, l_flushed = sem("pv_made"), sem("agg_done"), sem("flushed"), sem("l_flushed")
        acc_zero = sem("acc_zero")
        ld_wo, ld_w1, ld_w2a, ld_w2b = sem("ld_wo"), sem("ld_w1"), sem("ld_w2a"), sem("ld_w2b")
        ld_l = [sem("ld_l1"), sem("ld_l2"), sem("ld_l3")]
        ld_vec2, ld_vec3, ld_vec4 = sem("ld_vec2"), sem("ld_vec3"), sem("ld_vec4")
        onorm, z2_rows, x_rows, h_rows = sem("onorm"), sem("z2_rows"), sem("x_rows"), sem("h_rows")
        centred, squared, bn_var, bn_std = sem("centred"), sem("squared"), sem("bn_var"), sem("bn_std")
        rc_made = sem("rc_made")
        stored = sem("stored")

        order = []
        first = {}

        def part(name, count, engine):
            first[name] = len(order)
            order.extend([engine] * count)

        part("zT", 8, "act")
        part("K", 8, "dve")
        part("V", 8, "dve")
        part("KT", 8, "act")
        part("QT", 8, "act")
        part("Q", 8, "dve")
        part("WT", 24, "act")
        part("deg", 2, "dve")
        part("oT", 8, "act")
        part("wo", 8, "dve")
        part("z2T", 8, "act")
        part("hidT", 16, "act")
        part("ff", 8, "dve")
        for layer in (1, 2, 3):
            part(f"xT{layer}", 8, "act")
            part(f"aggT{layer}", 8, "act")
            part(f"h{layer}", 8, "dve")
            if layer == 2:
                part("bn_mean", 1, "dve")
                part("bn_var", 1, "dve")

        def drains(n):
            return order[:n + 1].count(order[n])

        def drained(n):
            return {"act": act_drained, "dve": dve_drained}[order[n]]

        def ln_sizes(which):
            return [(0, NB)] if which == "ln1" else [(0, NB // 2), (NB // 2, NB)]

        block = ctx.enter_context(nc.Block())

        @block.sync
        def _(sp):
            sp.dma_start(src_i[:, :], src.rearrange("(p t) -> p t", p=P)).then_inc(ld_edges, 16)
            sp.dma_start(blk_i[:, :], dst.rearrange("(p t) -> p t", p=P)).then_inc(ld_edges, 16)
            sp.dma_start(attr, edge_attr_8.rearrange("(p t) h -> p (t h)", p=P)).then_inc(ld_edges, 16)
            sp.dma_start(X[:, :, :], x.rearrange("(b p) c -> p b c", p=P)).then_inc(ld_x, 16)
            sp.wait_ge(filler_made, 1)
            sp.dma_start(records.rearrange("(p t) r -> p (t r)", p=P),
                         recs[:, :, :].rearrange("p t r -> p (t r)")).then_inc(filler_stored, 16)
            for s, v in enumerate((ln1_g, ln1_b, bk, bv, bq)):
                sp.dma_start(VEC[:, s, :], v.rearrange("(o c) -> o c", o=1).to_broadcast([P, C])).then_inc(ld_vec, 16)
            for at, v, k in ((0, bq, KC), (KC, bk, KC), (2 * KC, b1, HC)):
                sp.dma_start(bcol[:, at:at + k], v.rearrange("(k p) -> p k", p=P),
                             allow_slow_non_contiguous=True).then_inc(ld_vec, 16)
            for s, w in ((4, Wk), (8, Wv), (0, Wq)):
                sp.dma_start(W[:, s:s + 4, :], w.rearrange("(k p) c -> p k c", p=P)).then_inc(ld_w, 16)
            for b in range(NB):
                sp.wait_ge(dve_drained, drains(first["K"] + 2 * b + 1))
                sp.dma_start(kv_table[b * P:(b + 1) * P, :], kvst[:, b % 2, :]).then_inc(kv_stored[b % 2], 16)
            for m, w in enumerate((l1_ws, l1_wn, l2_wr, l2_wl, l3_ws, l3_wn)):
                if m:
                    sp.wait_ge(tile_full, first["WT"] + 4 * m)
                sp.dma_start(wnat, w.rearrange("(k p) c -> p k c", p=P)).then_inc(wt_loaded, 16)
                sp.wait_ge(act_drained, drains(first["WT"] + 4 * m + 3))
                sp.dma_start(weights_t[m].rearrange("(k p) c -> p k c", p=P), wtr).then_inc(wt_stored, 16)
            sp.wait_ge(q_split, NB)
            for s, v in enumerate((b2, l1_b, l1_g, l1_be, l2_bl, bo, ln2_g, ln2_b)):
                sp.dma_start(VEC[:, s, :], v.rearrange("(o c) -> o c", o=1).to_broadcast([P, C])).then_inc(ld_vec2, 16)
            sp.dma_start(W[:, 0:4, :], Wo.rearrange("(k p) c -> p k c", p=P)).then_inc(ld_wo, 16)
            for a in range(2):
                sp.wait_ge(scat[a], 16 * EPP // 2)
            sp.dma_start(recs[:, :, :].rearrange("p t r -> p (t r)"),
                         records.rearrange("(p t) r -> p (t r)", p=P)).then_inc(ld_recs, 16)
            sp.wait_ge(agg_done, NG)
            sp.dma_start(W[:, 4:12, :].rearrange("p (k a) c -> p k (a c)", k=KC),
                         W1.rearrange("(k p) c -> p k c", p=P)).then_inc(ld_w1, 16)
            w2v = W2.rearrange("(k p) c -> p k c", p=P)
            sp.dma_start(W[:, 12:16, :], w2v[:, 0:4, :]).then_inc(ld_w2a, 16)
            sp.wait_ge(tile_full, first["z2T"])
            sp.dma_start(W[:, 0:4, :], w2v[:, 4:8, :]).then_inc(ld_w2b, 16)
            sp.wait_ge(z2_rows, NB)
            for s, v in ((5, l2_g), (6, l2_be), (7, l3_b)):
                sp.dma_start(VEC[:, s, :], v.rearrange("(o c) -> o c", o=1).to_broadcast([P, C])).then_inc(ld_vec3, 16)
            sp.wait_ge(wt_stored, 96)

            def load_wt(layer, slots):
                for m, s in enumerate(slots):
                    sp.dma_start(W[:, s:s + 4, :], weights_t[2 * (layer - 1) + m].rearrange(
                        "(k p) c -> p k c", p=P)).then_inc(ld_l[layer - 1], 16)

            sp.wait_ge(tile_full, first["ff"])
            load_wt(1, (4, 8))
            sp.wait_ge(tile_full, first["ff"] + NB)
            load_wt(2, (12, 0))
            sp.wait_ge(tile_full, first["h1"] + NB)
            load_wt(3, (4, 8))
            sp.wait_ge(x_rows, 2 * NB)
            for s, v in ((1, l3_g), (2, l3_be)):
                sp.dma_start(VEC[:, s, :], v.rearrange("(o c) -> o c", o=1).to_broadcast([P, C])).then_inc(ld_vec4, 16)
            ov = out.rearrange("(b p) c -> p b c", p=P)
            for lo, hi in ln_sizes("out"):
                sp.wait_ge(x_rows, 3 * NB + hi)
                sp.dma_start(ov[:, lo:hi, :], X[:, lo:hi, :]).then_inc(stored, 16)
            sp.wait_ge(stored, 32)
            sp.wait_ge(filler_stored, 16)
            for a in range(2):
                sp.wait_ge(kv_stored[a], 16 * NB // 2)

        @block.gpsimd
        def _(pool):
            nc.gpsimd.memset(recs[:, :, :], 0.0).then_inc(consts, 1)
            nc.gpsimd.iota(iota_c[:, :], pattern=[[1, N]], base=0, channel_multiplier=0,
                           allow_small_or_imprecise_dtypes=True).then_inc(consts, 1)
            nc.gpsimd.iota(iota_pi[:, :], pattern=[[0, 1]], base=0, channel_multiplier=1).then_inc(consts, 1)
            nc.gpsimd.iota(iota_g[:, :], pattern=[[GE, NG]], base=0, channel_multiplier=0,
                           allow_small_or_imprecise_dtypes=True).then_inc(consts, 1)
            nc.gpsimd.memset(ones[:, :], 1.0).then_inc(consts, 1)
            pool.wait_ge(consts, 5)
            nc.gpsimd.memset(recs[:, :, 0:1], -1.0).then_inc(filler_made, 1)
            pool.wait_ge(bmax_in, 1)
            nc.gpsimd.partition_all_reduce(bmax_all[:, :], bmax[:, :], P, bass.bass_isa.ReduceOp.max).then_inc(bmax_out, 1)

            pool.wait_ge(rows_ready, 1)
            pool.wait_ge(attr_put, 1)
            pool.wait_ge(filler_stored, 16)

            def scatter_tiles(t0, a, k):
                nc.gpsimd.tensor_copy(stage_rec[:, a, :, :], rec_src[:, bass.ds(t0, 8), :]).then_inc(staged, 1)
                nc.gpsimd.tensor_copy(stage_row[:, a, :], row_i[:, bass.ds(t0, 8)]).then_inc(staged, 1)
                pool.wait_ge(staged, k)
                pool.sem_inc(pool_go, 1)
                for j in range(8):
                    nc.gpsimd.indirect_dma_start(
                        out=records[:, :], out_offset=bass.IndirectOffsetOnAxis(ap=stage_row[:, a, j:j + 1], axis=0),
                        in_=stage_rec[:, a, j, :], in_offset=None).then_inc(scat[a], 16)

            scatter_tiles(0, 0, 2)
            scatter_tiles(8, 1, 4)
            with pool.Fori(1, EPP // 16) as i:
                for a in range(2):
                    pool.wait_ge(scat[a], i * (16 * 8))
                    scatter_tiles(i * 16 + 8 * a, a, i * 4 + (2 * a + 2))

            nc.gpsimd.memset(CT[:, :, :], 0.0).then_inc(ct_zero, 1)
            pool.wait_ge(wt_stored, 96)
            nc.gpsimd.memset(HR[:, :, :], 0.0).then_inc(acc_zero, 1)
            nc.gpsimd.memset(Lacc[:, :, :], 0.0).then_inc(acc_zero, 1)

            def gather(g, a, k):
                nc.gpsimd.tensor_copy(idx[:, a, :], dst_i[:, bass.ds(g * GT, GT)]).then_inc(idx_ready, 1)
                pool.wait_ge(idx_ready, k)
                pool.sem_inc(pool_go, 1)
                for j in range(GT):
                    nc.gpsimd.indirect_dma_start(
                        out=kvr[:, a, j, :], out_offset=None, in_=kv_table[:, :],
                        in_offset=bass.IndirectOffsetOnAxis(ap=idx[:, a, j:j + 1], axis=0)).then_inc(kv_in[a][j], 16)

            for a in range(2):
                pool.wait_ge(kv_stored[a], 16 * NB // 2)
            pool.wait_ge(recs_int, 1)
            pool.wait_ge(smm, NB * H)
            gather(0, 0, 1)
            gather(1, 1, 2)
            with pool.Fori(2, NG - 1, 2) as g:
                for a in range(2):
                    pool.wait_ge(pv_made, g + (a - 1))
                    for j in range(GT):
                        pool.wait_ge(kv_in[a][j], g * 8)
                    gather(g + a, a, g + (a + 1))

            pool.wait_ge(rc_made, 1)
            for b in range(NB):
                last = nc.gpsimd.tensor_tensor(CT[:, b, :], CT[:, b, :], degrc[:, :], ALU.mult)
            last.then_inc(cn_ready, 1)

        @block.scalar
        def _(act):
            act.wait_ge(ld_edges, 48)
            nc.scalar.copy(rec_src[:, :, 2:RW], attr.rearrange("p (t h) -> p t h", h=H)).then_inc(attr_put, 1)
            roots = [0]

            def root(lo, hi):
                roots[0] += 1
                act.wait_ge(ln_var, roots[0])
                nc.scalar.activation(std[:, lo:hi], var_e[:, lo:hi], ACT.Sqrt).then_inc(ln_std, 1)

            def drain(n, dest, func=None, **kw):
                act.wait_ge(tile_full, n + 1)
                if func is None:
                    nc.scalar.copy(dest, ps[:, n % NBANK, :]).then_inc(act_drained, 1)
                else:
                    nc.scalar.activation(dest, ps[:, n % NBANK, :], func, **kw).then_inc(act_drained, 1)

            def drain_T(name, dest):
                for m in range(2 * KC):
                    half, k = m // KC, m % KC
                    drain(first[name] + m, dest[:, k, half * HALF:(half + 1) * HALF])

            root(0, NB)
            drain_T("zT", TR)
            act.wait_ge(ld_vec, 128)
            for name, dest, b0, scale in (("KT", KTr, bcol[:, KC:2 * KC], 1.0), ("QT", QT, bq8, float(D) ** -0.5)):
                if name == "QT":
                    act.wait_ge(dve_consts, 2)
                for m in range(2 * KC):
                    half, k = m // KC, m % KC
                    drain(first[name] + m, dest[:, k, half * HALF:(half + 1) * HALF], ACT.Identity,
                          bias=b0[:, k:k + 1], scale=scale)
            for m in range(24):
                if m >= 4 and m % 4 == 0:
                    act.wait_ge(wt_stored, 16 * (m // 4))
                drain(first["WT"] + m, wtr[:, m % 4, :])

            def onehots(g, a):
                act.wait_ge(ohT_ps, g + 1)
                nc.scalar.copy(ohT[:, a, :, :], psb[:, 0:GE].rearrange("p (j n) -> p j n", j=GT)).then_inc(ohT_sb, 1)

            def onehots_f(g, a, wait=True):
                if wait:
                    act.wait_ge(agg_done, g - 1)
                nc.scalar.copy(oh_f[:, a, :, :], oh_b[:, a, :, :]).then_inc(ohf_made, 1)

            def exps(g, a):
                act.wait_ge(z_made, g + 1)
                nc.scalar.activation(prob[:, a, :, :].rearrange("p j h -> p (j h)"), zsc[:, a, :],
                                     ACT.Exp).then_inc(p_made, 1)

            onehots(0, 0)
            onehots_f(0, 0, wait=False)
            exps(0, 0)
            onehots(1, 1)
            onehots_f(1, 1, wait=False)
            with act.Fori(1, NG - 2, 2) as g:
                for a in range(2):
                    exps(g + a, 1 - a)
                    onehots(g + (a + 1), a)
                    onehots_f(g + (a + 1), a)
            exps(NG - 1, 1)

            act.wait_ge(cn_ready, 1)
            drain_T("oT", TR)
            for lo, hi in ln_sizes("z2"):
                root(lo, hi)
            drain_T("z2T", TR)
            for m in range(2 * HC):
                half, k = m // HC, m % HC
                drain(first["hidT"] + m, hidT[:, k, half * HALF:(half + 1) * HALF], ACT.Silu,
                      bias=bcol[:, 2 * KC + k:2 * KC + k + 1])
            for lo, hi in ln_sizes("out"):
                root(lo, hi)
            for layer in (1, 2, 3):
                drain_T(f"xT{layer}", XT)
                drain_T(f"aggT{layer}", TR)
                if layer == 2:
                    for b in range(NB):
                        act.wait_ge(centred, b + 1)
                        nc.scalar.activation(SQ[:, b, :], HR[:, b, :], ACT.Square).then_inc(squared, 1)
                    act.wait_ge(bn_var, 1)
                    nc.scalar.activation(PR[:, 512:1024], PR[:, 0:512], ACT.Sqrt).then_inc(bn_std, 1)
                    for lo, hi in ln_sizes("out"):
                        root(lo, hi)
                else:
                    for lo, hi in ln_sizes("out"):
                        root(lo, hi)
                        root(lo, hi)

        @block.vector
        def _(dve):
            chain = [0]

            def link(ins):
                chain[0] += 1
                ins.then_inc(dve_chain, 1)
                dve.wait_ge(dve_chain, chain[0])

            vec = nc.vector
            dve.wait_ge(consts, 5)
            link(vec.tensor_copy(iota_p[:, :], iota_pi[:, :]))
            vec.tensor_scalar(ident[:, :], iota_c[:, 0:P], iota_p[:, 0:1], None, ALU.is_equal)
            vec.tensor_scalar(ident_b[:, :], iota_c[:, 0:P], iota_p[:, 0:1], None, ALU.is_equal)
            vec.tensor_scalar(before[:, :], iota_c[:, 0:P], iota_p[:, 0:1], None, ALU.is_gt).then_inc(dve_consts, 1)

            dve.wait_ge(ld_edges, 48)
            srcf = pick[:, 0, :]
            blkf = pick[:, 1, :]
            vec.tensor_copy(rec_src[:, :, 1:2].rearrange("p t o -> p (t o)"), blk_i[:, :])
            link(vec.tensor_copy(srcf, src_i[:, :]))
            link(vec.tensor_scalar(blk_i[:, :], src_i[:, :], 7, None, ALU.arith_shift_right))
            link(vec.tensor_copy(blkf, blk_i[:, :]))
            link(vec.scalar_tensor_tensor(rec_src[:, :, 0:1].rearrange("p t o -> p (t o)"), blkf, -float(P), srcf,
                                          ALU.mult, ALU.add))
            for b in range(NB):
                last = vec.tensor_scalar(oh8[:, b, :], blkf, float(b), None, ALU.is_equal)
            link(last)
            link(vec.memset(zeros_f, 0.0))
            link(vec.tensor_tensor_scan(cum_f, zeros_f, oh8_f, 0.0, ALU.add, ALU.add))
            last8, prev8, n8, tot8, end8, base8, off8 = (small[:, i, :] for i in range(7))
            link(vec.tensor_copy(last8, cum[:, :, EPP - 1:EPP].rearrange("p b o -> p (b o)")))
            vec.memset(prev8[:, 0:1], 0.0)
            link(vec.tensor_copy(prev8[:, 1:8], last8[:, 0:7]))
            vec.tensor_tensor(n8, last8, prev8, ALU.subtract).then_inc(sort_n, 1)
            dve.wait_ge(sort_mm, 1)
            link(vec.tensor_scalar(tot8, ps[:, 0, 8:16], float(GE - 1), None, ALU.add))
            link(vec.tensor_copy(pad_i[:, :], tot8))
            link(vec.tensor_scalar(pad_i[:, :], pad_i[:, :], -GE, None, ALU.bitwise_and))
            link(vec.tensor_copy(tot8, pad_i[:, :]))
            link(vec.tensor_tensor_scan(end8, zeros_f[:, 0:8], tot8, 0.0, ALU.add, ALU.add))
            link(vec.tensor_tensor(base8, end8, tot8, ALU.subtract))
            link(vec.tensor_tensor(off8, base8, ps[:, 0, 0:8], ALU.add))
            link(vec.scalar_tensor_tensor(off8, off8, -1.0, prev8, ALU.add, ALU.subtract))
            for b in range(NB):
                last = vec.scalar_tensor_tensor(pick[:, b, :], cum[:, b, :], off8[:, b:b + 1], oh8[:, b, :],
                                                ALU.add, ALU.mult)
            link(last)
            slot = cum[:, 0, :]
            tif, ppf = cum[:, 1, :], cum[:, 2, :]
            link(vec.tensor_reduce(slot, pick.rearrange("p b t -> p t b"), AX.X, ALU.add))
            link(vec.tensor_copy(row_i[:, :], slot))
            link(vec.tensor_scalar(blk_i[:, :], row_i[:, :], 7, None, ALU.arith_shift_right))
            link(vec.tensor_copy(tif, blk_i[:, :]))
            link(vec.tensor_scalar(blk_i[:, :], row_i[:, :], P - 1, None, ALU.bitwise_and))
            link(vec.tensor_copy(ppf, blk_i[:, :]))
            link(vec.scalar_tensor_tensor(ppf, ppf, float(NT), tif, ALU.mult, ALU.add))
            vec.tensor_copy(row_i[:, :], ppf).then_inc(rows_ready, 1)
            vec.tensor_reduce(bmax[:, :], attr.rearrange("p (t h) -> p h t", h=H), AX.X, ALU.max).then_inc(bmax_in, 1)
            link(vec.tensor_scalar(gblk[:, :], iota_g[:, :], end8[:, 0:1], None, ALU.is_ge))
            for b in range(1, NB - 1):
                link(vec.scalar_tensor_tensor(gblk[:, :], iota_g[:, :], end8[:, b:b + 1], gblk[:, :],
                                              ALU.is_ge, ALU.add))
            vec.tensor_copy(gblk_i[:, :], gblk[:, :]).then_inc(gtab, 1)

            roots = [0]

            def ln_stats(source, lo, hi):
                for b in range(lo, hi):
                    last = vec.bn_stats(stats[:, b, :], source[:, b, :])
                link(last)
                for b in range(lo, hi):
                    last = vec.bn_aggr(mv[:, b, :], stats[:, b, :])
                link(last)
                roots[0] += 1
                vec.tensor_scalar(var_e[:, lo:hi], mv[:, lo:hi, 1:2].rearrange("p b o -> p (b o)"), EPS, None,
                                  ALU.add).then_inc(ln_var, 1)
                dve.wait_ge(ln_std, roots[0])
                link(vec.reciprocal(rstd[:, lo:hi], std[:, lo:hi]))

            def ln_apply(dest, source, b):
                return vec.tensor_scalar(dest[:, b, :], source[:, b, :], mv[:, b, 0:1], rstd[:, b:b + 1],
                                         ALU.subtract, ALU.mult)

            def phased(lo, hi, *steps):
                for step in steps[:-1]:
                    for b in range(lo, hi):
                        last = step(b)
                    link(last)
                return steps[-1]

            dve.wait_ge(ld_x, 16)
            dve.wait_ge(ld_vec, 128)
            vec.tensor_scalar(bq8[:, :], bcol[:, 0:KC], float(D) ** -0.5, None, ALU.mult).then_inc(dve_consts, 1)
            ln_stats(X, 0, NB)
            last_step = phased(0, NB,
                               lambda b: ln_apply(Z, X, b),
                               lambda b: vec.tensor_tensor(Z[:, b, :], Z[:, b, :], VEC[:, 0, :], ALU.mult),
                               lambda b: vec.tensor_tensor(Z[:, b, :], Z[:, b, :], VEC[:, 1, :], ALU.add))
            for b in range(NB):
                last_step(b).then_inc(z_rows, 1)

            for b in range(NB):
                dve.wait_ge(tile_full, first["K"] + 2 * b + 1)
                if b >= 2:
                    dve.wait_ge(kv_stored[b % 2], 16 * (b // 2))
                vec.tensor_tensor(kvst[:, b % 2, 0:C], ps[:, (first["K"] + 2 * b) % NBANK, :], VEC[:, 2, :],
                                  ALU.add).then_inc(dve_drained, 1)
                dve.wait_ge(tile_full, first["K"] + 2 * b + 2)
                vec.tensor_tensor(kvst[:, b % 2, C:2 * C], ps[:, (first["K"] + 2 * b + 1) % NBANK, :], VEC[:, 3, :],
                                  ALU.add).then_inc(dve_drained, 1)
            dve.wait_ge(filler_stored, 16)
            for b in range(NB):
                n = first["Q"] + b
                q0, q1 = tmpq[:, 0:C], tmpq[:, C:2 * C]
                dve.wait_ge(tile_full, n + 1)
                chain[0] += 1
                vec.tensor_tensor(q0, ps[:, n % NBANK, :], VEC[:, 4, :], ALU.add).then_inc(dve_drained, 1)
                dve.wait_ge(dve_drained, drains(n))
                chain[0] -= 1
                link(vec.tensor_scalar(q0, q0, float(D) ** -0.5, None, ALU.mult))
                link(vec.tensor_copy(Qs[:, 0, b, :], q0))
                link(vec.tensor_tensor(q1, q0, Qs[:, 0, b, :], ALU.subtract))
                link(vec.tensor_copy(Qs[:, 1, b, :], q1))
                link(vec.tensor_tensor(q0, q1, Qs[:, 1, b, :], ALU.subtract))
                chain[0] += 1
                vec.tensor_copy(Qs[:, 2, b, :], q0).then_inc(dve_chain, 1)
                dve.wait_ge(dve_chain, chain[0])
                dve.sem_inc(q_split, 1)

            dve.wait_ge(ld_recs, 16)
            vec.tensor_copy(dst_i[:, :], recs[:, :, 1:2].rearrange("p t o -> p (t o)")).then_inc(recs_int, 1)
            dve.wait_ge(ct_zero, 1)
            dve.wait_ge(gtab, 1)
            for a in range(2):
                dve.wait_ge(kv_stored[a], 16 * NB // 2)

            def source_onehots(g, a, done):
                tiles = recs[:, bass.ds(g * GT, GT), :]
                for j in range(GT):
                    last = vec.tensor_scalar(oh_b[:, a, j, :], iota_c[:, 0:P], tiles[:, j, 0:1], None, ALU.is_equal)
                if done is not None:
                    last.then_inc(done, 1)

            def count_onehots(g, a, wait=True):
                if wait:
                    dve.wait_ge(cmm, g - 1)
                source_onehots(g, a, None)
                tiles = recs[:, bass.ds(g * GT, GT), :]
                for j in range(GT):
                    last = vec.tensor_scalar(ohd[a][:, j, :], iota_c[:, :], tiles[:, j, 1:2], None, ALU.is_equal)
                last.then_inc(coh, 1)

            def count_flush(g, a, wait=True):
                at = dve.value_load(gblk_i[0:1, bass.ds(g, 1)], min_val=0, max_val=NB - 1)
                dve.wait_ge(cmm, g + 1)
                if wait:
                    dve.wait_ge(cflush, g)
                vec.tensor_tensor(CT[:, at, :], CT[:, at, :],
                                  ps[:, 2 * a:2 * a + 2, :].rearrange("p a c -> p (a c)"), ALU.add).then_inc(cflush, 1)

            count_onehots(0, 0, wait=False)
            count_onehots(1, 1, wait=False)
            count_flush(0, 0, wait=False)
            with dve.Fori(1, NG - 2, 2) as g:
                for a in range(2):
                    count_onehots(g + (a + 1), a)
                    count_flush(g + a, 1 - a)
            count_flush(NG - 1, 1)
            dve.wait_ge(cflush, NG)
            dve.sem_inc(ct_ready, 1)

            for m in range(2):
                n = first["deg"] + m
                dve.wait_ge(tile_full, n + 1)
                vec.tensor_scalar(degrc[:, m * HALF:(m + 1) * HALF], ps[:, n % NBANK, :], 1.0, None,
                                  ALU.max).then_inc(dve_drained, 1)
            dve.wait_ge(dve_drained, drains(first["deg"] + 1))
            vec.reciprocal(degrc[:, :], degrc[:, :]).then_inc(rc_made, 1)

            for b in range(NB):
                if b >= 2:
                    dve.wait_ge(smax, H * (b - 1))
                link(vec.tensor_scalar(mask[:, b % 2, :], CT[:, b, :], 0.0, NEG, ALU.is_equal, ALU.mult))
                for h in range(H):
                    m = b * H + h
                    dve.wait_ge(smm, m + 1)
                    if m:
                        dve.wait_ge(smax, m)
                    bank = 2 * (m % 4)
                    vec.tensor_tensor_reduce(out=PV[:, 0:N], in0=ps[:, bank:bank + 2, :].rearrange("p a c -> p (a c)"),
                                             in1=mask[:, b % 2, :], scale=1.0, scalar=4 * NEG, op0=ALU.add,
                                             op1=ALU.max, accum_out=cmax[:, b, h:h + 1]).then_inc(smax, 1)
            dve.wait_ge(smax, NB * H)
            dve.wait_ge(bmax_out, 1)
            for b in range(NB):
                last = vec.tensor_tensor(shift[:, b, :], cmax[:, b, :], bmax_all[:, :], ALU.add)
            last.then_inc(shift_ready, 1)

            def edge_onehots(g, a, wait=True):
                if wait:
                    dve.wait_ge(ohf_made, g - 1)
                source_onehots(g, a, oh_made)

            def edge_scores(g, a, wait=True):
                for half in range(2):
                    dve.wait_ge(q_ps, g * 2 + (half + 1))
                    for j in (2 * half, 2 * half + 1):
                        dve.wait_ge(kv_in[a][j], kv_count(g, a))
                    if wait and half == 0:
                        dve.wait_ge(summed, g)
                    vec.tensor_tensor(prod[:, 2 * half:2 * half + 2, :], ps[:, 2 * half:2 * half + 2, :],
                                      kvr[:, a, 2 * half:2 * half + 2, 0:C], ALU.mult).then_inc(prod_done, 1)
                dve.wait_ge(prod_done, g * 2 + 2)
                vec.tensor_reduce(score[:, a, :], prod_h, AX.X, ALU.add).then_inc(summed, 1)
                dve.wait_ge(summed, g + 1)
                tiles = recs[:, bass.ds(g * GT, GT), :]
                vec.tensor_tensor(score[:, a, :].rearrange("p (j h) -> p j h", j=GT),
                                  score[:, a, :].rearrange("p (j h) -> p j h", j=GT),
                                  tiles[:, :, 2:RW], ALU.add).then_inc(biased, 1)
                dve.wait_ge(biased, g + 1)
                dve.wait_ge(c_ps, g + 1)
                vec.tensor_tensor(zsc[:, a, :], score[:, a, :], shift_ps, ALU.subtract).then_inc(z_made, 1)

            def edge_flush(g, a, wait=True):
                at = dve.value_load(gblk_i[0:1, bass.ds(g, 1)], min_val=0, max_val=NB - 1)
                dve.wait_ge(agg_done, g + 1)
                if wait:
                    dve.wait_ge(flushed, g)
                    dve.wait_ge(l_flushed, g)
                vec.tensor_tensor(Lacc[:, at, :], Lacc[:, at, :], psum_ps, ALU.add).then_inc(l_flushed, 1)
                vec.tensor_tensor(HR[:, at, :], HR[:, at, :], sums_ps, ALU.add).then_inc(flushed, 1)

            def edge_values(g, a, wait=True):
                dve.wait_ge(p_made, g + 1)
                if wait:
                    dve.wait_ge(agg_done, g)
                vec.tensor_tensor(pv_h, kvr[:, a, :, C:2 * C].rearrange("p j (h d) -> p j h d", d=D),
                                  prob[:, a, :, :].unsqueeze(3).to_broadcast([P, GT, H, D]), ALU.mult).then_inc(pv_made, 1)

            dve.wait_ge(cmm, NG)
            edge_onehots(0, 0, wait=False)
            edge_onehots(1, 1, wait=False)
            edge_scores(0, 0, wait=False)
            dve.wait_ge(acc_zero, 2)
            edge_onehots(2, 0)
            edge_values(0, 0, wait=False)
            edge_scores(1, 1)
            edge_flush(0, 0, wait=False)
            edge_onehots(3, 1)
            edge_values(1, 1)
            with dve.Fori(2, NG - 3, 2) as g:
                for a in range(2):
                    edge_scores(g + a, a)
                    edge_flush(g + (a - 1), 1 - a)
                    edge_onehots(g + (a + 2), a)
                    edge_values(g + a, a)
            for a in range(2):
                g = NG - 2 + a
                edge_scores(g, a)
                edge_flush(g - 1, 1 - a)
                edge_values(g, a)
            edge_flush(NG - 1, 1)
            dve.wait_ge(flushed, NG)
            dve.wait_ge(l_flushed, NG)

            rl = cmax
            link(vec.tensor_scalar(rl[:, :, :], Lacc[:, :, :], 1.0e-37, None, ALU.max))
            link(vec.reciprocal(rl[:, :, :], rl[:, :, :]))
            for b in range(NB):
                o = HR[:, b, :].rearrange("p (h d) -> p h d", d=D)
                vec.tensor_tensor(o, o, rl[:, b, :].unsqueeze(2).to_broadcast([P, H, D]), ALU.mult).then_inc(onorm, 1)
            dve.wait_ge(ld_vec2, 128)
            for lo, hi in ln_sizes("z2"):
                for b in range(lo, hi):
                    n = first["wo"] + b
                    dve.wait_ge(tile_full, n + 1)
                    last = vec.tensor_tensor(HR[:, b, :], ps[:, n % NBANK, :], X[:, b, :], ALU.add)
                    last.then_inc(dve_drained, 1)
                dve.wait_ge(dve_drained, drains(first["wo"] + hi - 1))
                for b in range(lo, hi):
                    last = vec.tensor_tensor(HR[:, b, :], HR[:, b, :], VEC[:, 5, :], ALU.add)
                link(last)
                ln_stats(HR, lo, hi)
                step = phased(lo, hi,
                              lambda b: ln_apply(Z, HR, b),
                              lambda b: vec.tensor_tensor(Z[:, b, :], Z[:, b, :], VEC[:, 6, :], ALU.mult),
                              lambda b: vec.tensor_tensor(Z[:, b, :], Z[:, b, :], VEC[:, 7, :], ALU.add))
                for b in range(lo, hi):
                    step(b).then_inc(z2_rows, 1)
            for b in range(NB):
                last = vec.tensor_tensor(X[:, b, :], X[:, b, :], HR[:, b, :], ALU.add)
            link(last)
            for b in range(NB):
                last = vec.tensor_tensor(X[:, b, :], X[:, b, :], VEC[:, 0, :], ALU.add)
            link(last)
            for lo, hi in ln_sizes("out"):
                for b in range(lo, hi):
                    n = first["ff"] + b
                    dve.wait_ge(tile_full, n + 1)
                    last = vec.tensor_tensor(HR[:, b, :], ps[:, n % NBANK, :], X[:, b, :], ALU.add)
                    last.then_inc(dve_drained, 1)
                dve.wait_ge(dve_drained, drains(first["ff"] + hi - 1))
                ln_stats(HR, lo, hi)
                for b in range(lo, hi):
                    ln_apply(X, HR, b).then_inc(x_rows, 1)

            def gain_relu_add(v_g, v_b, relu, pre):
                steps = list(pre)
                steps.append(lambda b: vec.tensor_tensor(HR[:, b, :], HR[:, b, :], v_g, ALU.mult))
                steps.append(lambda b: vec.tensor_tensor(HR[:, b, :], HR[:, b, :], v_b, ALU.add))
                if relu:
                    steps.append(lambda b: vec.scalar_tensor_tensor(HR[:, b, :], HR[:, b, :], 0.0, X[:, b, :],
                                                                    ALU.max, ALU.add))
                else:
                    steps.append(lambda b: vec.tensor_tensor(HR[:, b, :], HR[:, b, :], X[:, b, :], ALU.add))
                return steps

            def whole(lo, hi, steps):
                for step in steps:
                    for b in range(lo, hi):
                        last = step(b)
                    link(last)

            def take_h(layer, lo, hi, v_bias):
                for b in range(lo, hi):
                    n = first[f"h{layer}"] + b
                    dve.wait_ge(tile_full, n + 1)
                    vec.tensor_tensor(HR[:, b, :], ps[:, n % NBANK, :], v_bias, ALU.add).then_inc(dve_drained, 1)
                dve.wait_ge(dve_drained, drains(first[f"h{layer}"] + hi - 1))

            def finish(lo, hi):
                ln_stats(HR, lo, hi)
                for b in range(lo, hi):
                    ln_apply(X, HR, b).then_inc(x_rows, 1)

            def ln_layer(layer, v_bias, v_g, v_b, relu):
                for lo, hi in ln_sizes("out"):
                    take_h(layer, lo, hi, v_bias)
                    ln_stats(HR, lo, hi)
                    whole(lo, hi, gain_relu_add(v_g, v_b, relu, [lambda b: ln_apply(HR, HR, b)]))
                    finish(lo, hi)

            ln_layer(1, VEC[:, 1, :], VEC[:, 2, :], VEC[:, 3, :], True)

            dve.wait_ge(ld_vec3, 48)
            take_h(2, 0, NB, VEC[:, 4, :])
            dve.sem_inc(h_rows, 1)
            n = first["bn_mean"]
            dve.wait_ge(tile_full, n + 1)
            vec.tensor_scalar(PR[:, 0:C], ps[:, n % NBANK, :], 1.0 / N, None, ALU.mult).then_inc(dve_drained, 1)
            dve.wait_ge(dve_drained, drains(n))
            for b in range(NB):
                vec.tensor_tensor(HR[:, b, :], HR[:, b, :], PR[:, 0:C], ALU.subtract).then_inc(centred, 1)
            dve.wait_ge(centred, NB)
            n = first["bn_var"]
            dve.wait_ge(tile_full, n + 1)
            vec.tensor_scalar(PR[:, 0:C], ps[:, n % NBANK, :], 1.0 / N, EPS, ALU.mult, ALU.add).then_inc(dve_drained, 1)
            dve.wait_ge(dve_drained, drains(n))
            dve.sem_inc(bn_var, 1)
            dve.wait_ge(bn_std, 1)
            link(vec.reciprocal(PR[:, 0:C], PR[:, C:2 * C]))
            link(vec.tensor_tensor(PR[:, 0:C], PR[:, 0:C], VEC[:, 5, :], ALU.mult))
            for lo, hi in ln_sizes("out"):
                whole(lo, hi, gain_relu_add(PR[:, 0:C], VEC[:, 6, :], True, []))
                finish(lo, hi)

            dve.wait_ge(ld_vec4, 32)
            ln_layer(3, VEC[:, 7, :], VEC[:, 1, :], VEC[:, 2, :], False)

        @block.tensor
        def _(pe):
            mm = nc.tensor.matmul

            def free_bank(n):
                if n >= NBANK:
                    pe.wait_ge(drained(n - NBANK), drains(n - NBANK))
                return ps[:, n % NBANK, :]

            def transposes(name, source, rows, per):
                for m in range(2 * KC):
                    half, k = m // KC, m % KC
                    n = first[name] + m
                    pe.wait_ge(rows, per + (half + 1) * (NB // 2))
                    bank = free_bank(n)
                    for j in range(4):
                        last = nc.tensor.transpose(bank[:, j * P:(j + 1) * P],
                                                   source[:, 4 * half + j, k * P:(k + 1) * P], ident[:, :])
                    last.then_inc(tile_full, 1)

            pe.wait_ge(dve_consts, 1)
            pe.wait_ge(consts, 5)
            pe.wait_ge(sort_n, 1)
            mm(ps[:, 0, 0:8], before[:, :], small[:, 2, :], start=True, stop=True)
            mm(ps[:, 0, 8:16], ones[:, :], small[:, 2, :], start=True, stop=True).then_inc(sort_mm, 1)

            pe.wait_ge(rows_ready, 1)
            transposes("zT", Z, z_rows, 0)
            pe.wait_ge(ld_w, 48)

            for b in range(NB):
                for v in range(2):
                    n = first["K"] + 2 * b + v
                    pe.wait_ge(act_drained, drains(first["zT"] + KC * (b // 4) + KC - 1))
                    bank = free_bank(n)
                    for k in range(KC):
                        last = mm(bank, TR[:, k, b * P:(b + 1) * P], W[:, 4 + 4 * v + k, :],
                                  start=k == 0, stop=k == KC - 1)
                    last.then_inc(tile_full, 1)
            for name, w0 in (("KT", 4), ("QT", 0)):
                for m in range(2 * KC):
                    half, o = m // KC, m % KC
                    n = first[name] + m
                    bank = free_bank(n)
                    for k in range(KC):
                        last = mm(bank, W[:, w0 + k, o * P:(o + 1) * P], TR[:, k, half * HALF:(half + 1) * HALF],
                                  start=k == 0, stop=k == KC - 1)
                    last.then_inc(tile_full, 1)
            for b in range(NB):
                n = first["Q"] + b
                bank = free_bank(n)
                for k in range(KC):
                    last = mm(bank, TR[:, k, b * P:(b + 1) * P], W[:, k, :], start=k == 0, stop=k == KC - 1)
                last.then_inc(tile_full, 1)
            for m in range(24):
                n = first["WT"] + m
                pe.wait_ge(wt_loaded, 16 * (m // 4 + 1))
                bank = free_bank(n)
                for j in range(4):
                    last = nc.tensor.transpose(bank[:, j * P:(j + 1) * P], wnat[:, j, (m % 4) * P:(m % 4 + 1) * P],
                                               ident[:, :])
                last.then_inc(tile_full, 1)

            pe.wait_ge(act_drained, drains(first["WT"] + 23))
            pe.wait_ge(dve_drained, drains(first["Q"] + NB - 1))

            def count_mm(g, a, wait=True):
                pe.wait_ge(coh, g + 1)
                if wait:
                    pe.wait_ge(cflush, g - 1)
                for j in range(GT):
                    for half in range(2):
                        last = mm(ps[:, 2 * a + half, :], oh_b[:, a, j, :], ohd[a][:, j, half * HALF:(half + 1) * HALF],
                                  start=j == 0, stop=j == GT - 1)
                last.then_inc(cmm, 1)

            count_mm(0, 0, wait=False)
            count_mm(1, 1, wait=False)
            with pe.Fori(2, NG - 1, 2) as g:
                for a in range(2):
                    count_mm(g + a, a)

            pe.wait_ge(ct_ready, 1)
            for m in range(2):
                n = first["deg"] + m
                for b in range(NB):
                    last = mm(ps[:, n % NBANK, :], ones[:, :], CT[:, b, m * HALF:(m + 1) * HALF],
                              start=b == 0, stop=b == NB - 1)
                last.then_inc(tile_full, 1)
            pe.wait_ge(dve_drained, drains(first["deg"] + 1))
            for b in range(NB):
                for h in range(H):
                    m = b * H + h
                    bank = 2 * (m % 4)
                    if m >= 4:
                        pe.wait_ge(smax, m - 3)
                    lo = D * (h % 2)
                    for half in range(2):
                        last = mm(ps[:, bank + half, :], QT[lo:lo + D, h // 2, b * P:(b + 1) * P],
                                  KTr[lo:lo + D, h // 2, half * HALF:(half + 1) * HALF], start=True, stop=True)
                    last.then_inc(smm, 1)
            pe.wait_ge(shift_ready, 1)
            pe.wait_ge(q_split, NB)

            def edge_front(g, a, wait=True):
                at = pe.value_load(gblk_i[0:1, bass.ds(g, 1)], min_val=0, max_val=NB - 1)
                pe.wait_ge(oh_made, g + 1)
                if wait:
                    pe.wait_ge(ohT_sb, g)
                for j in range(GT):
                    last = nc.tensor.transpose(psb[:, j * P:(j + 1) * P], oh_b[:, a, j, :], ident_b[:, :])
                last.then_inc(ohT_ps, 1)
                pe.wait_ge(ohT_sb, g + 1)
                for half in range(2):
                    if wait:
                        pe.wait_ge(prod_done, g * 2 + (half - 1))
                    for j in (2 * half, 2 * half + 1):
                        for s in range(3):
                            last = mm(ps[:, j, :], ohT[:, a, j, :], Qs[:, s, at, :], start=s == 0, stop=s == 2)
                    last.then_inc(q_ps, 1)
                if wait:
                    pe.wait_ge(z_made, g)
                for j in range(GT):
                    last = mm(shift_ps[:, j * H:(j + 1) * H], ohT[:, a, j, :], shift[:, at, :], start=True, stop=True)
                last.then_inc(c_ps, 1)

            def edge_back(g, a, wait=True):
                pe.wait_ge(pv_made, g + 1)
                pe.wait_ge(ohf_made, g + 1)
                if wait:
                    pe.wait_ge(l_flushed, g)
                    pe.wait_ge(flushed, g)
                for j in range(GT):
                    mm(sums_ps, oh_f[:, a, j, :], pv[:, j, :], start=j == 0, stop=j == GT - 1)
                for j in range(GT):
                    last = mm(psum_ps, oh_f[:, a, j, :], prob[:, a, j, :], start=j == 0, stop=j == GT - 1)
                last.then_inc(agg_done, 1)

            pe.wait_ge(gtab, 1)
            edge_front(0, 0, wait=False)
            edge_front(1, 1)
            edge_back(0, 0, wait=False)
            edge_front(2, 0)
            edge_back(1, 1)
            with pe.Fori(2, NG - 3, 2) as g:
                for a in range(2):
                    edge_front(g + (a + 1), 1 - a)
                    edge_back(g + a, a)
            edge_front(NG - 1, 1)
            edge_back(NG - 2, 0)
            edge_back(NG - 1, 1)

            pe.wait_ge(flushed, NG)
            pe.wait_ge(l_flushed, NG)
            transposes("oT", HR, onorm, 0)
            pe.wait_ge(ld_wo, 16)
            for b in range(NB):
                n = first["wo"] + b
                pe.wait_ge(act_drained, drains(first["oT"] + KC * (b // 4) + KC - 1))
                bank = free_bank(n)
                for k in range(KC):
                    last = mm(bank, TR[:, k, b * P:(b + 1) * P], W[:, k, :], start=k == 0, stop=k == KC - 1)
                last.then_inc(tile_full, 1)
            transposes("z2T", Z, z2_rows, 0)
            pe.wait_ge(ld_w1, 16)
            w1 = W[:, 4:12, :].rearrange("p (k a) c -> p k (a c)", k=KC)
            for m in range(2 * HC):
                half, o = m // HC, m % HC
                n = first["hidT"] + m
                pe.wait_ge(act_drained, drains(first["z2T"] + 2 * KC - 1))
                bank = free_bank(n)
                for k in range(KC):
                    last = mm(bank, w1[:, k, o * P:(o + 1) * P], TR[:, k, half * HALF:(half + 1) * HALF],
                              start=k == 0, stop=k == KC - 1)
                last.then_inc(tile_full, 1)
            pe.wait_ge(ld_w2a, 16)
            pe.wait_ge(ld_w2b, 16)
            for b in range(NB):
                n = first["ff"] + b
                pe.wait_ge(act_drained, drains(first["hidT"] + HC * (b // 4) + HC - 1))
                bank = free_bank(n)
                for k in range(HC):
                    last = mm(bank, hidT[:, k, b * P:(b + 1) * P], W[:, (12 + k) % 16, :], start=k == 0, stop=k == HC - 1)
                last.then_inc(tile_full, 1)

            pe.wait_ge(cn_ready, 1)
            for layer, (ws, wn) in ((1, (4, 8)), (2, (12, 0)), (3, (4, 8))):
                transposes(f"xT{layer}", X, x_rows, (layer - 1) * NB)
                pe.wait_ge(x_rows, layer * NB)
                for m in range(2 * KC):
                    half, k = m // KC, m % KC
                    n = first[f"aggT{layer}"] + m
                    bank = free_bank(n)
                    for b in range(NB):
                        last = mm(bank, X[:, b, k * P:(k + 1) * P], CT[:, b, half * HALF:(half + 1) * HALF],
                                  start=b == 0, stop=b == NB - 1)
                    last.then_inc(tile_full, 1)
                pe.wait_ge(ld_l[layer - 1], 32)
                for b in range(NB):
                    n = first[f"h{layer}"] + b
                    pe.wait_ge(act_drained, drains(first[f"aggT{layer}"] + KC * (b // 4) + KC - 1))
                    bank = free_bank(n)
                    for k in range(KC):
                        mm(bank, XT[:, k, b * P:(b + 1) * P], W[:, ws + k, :], start=k == 0, stop=False)
                    for k in range(KC):
                        last = mm(bank, TR[:, k, b * P:(b + 1) * P], W[:, wn + k, :], start=False, stop=k == KC - 1)
                    last.then_inc(tile_full, 1)
                if layer == 2:
                    for name, source, ready, count in (("bn_mean", HR, h_rows, 1), ("bn_var", SQ, squared, NB)):
                        n = first[name]
                        pe.wait_ge(ready, count)
                        bank = free_bank(n)
                        for b in range(NB):
                            last = mm(bank, ones[:, :], source[:, b, :], start=b == 0, stop=b == NB - 1)
                        last.then_inc(tile_full, 1)


_INS = ['x', 'src', 'dst', 'edge_attr_8', 'L0_gnn_Wq', 'L0_gnn_bq', 'L0_gnn_Wk', 'L0_gnn_bk', 'L0_gnn_Wv', 'L0_gnn_bv',
        'L0_gnn_Wo', 'L0_gnn_bo', 'L0_gnn_ln1_g', 'L0_gnn_ln1_b', 'L0_gnn_ln2_g', 'L0_gnn_ln2_b', 'L0_gnn_W1',
        'L0_gnn_b1', 'L0_gnn_W2', 'L0_gnn_b2', 'L1_gnn_w_self', 'L1_gnn_w_neigh', 'L1_gnn_bias', 'L1_gnn_gamma',
        'L1_gnn_beta', 'L2_gnn_W_l', 'L2_gnn_b_l', 'L2_gnn_W_r', 'L2_gnn_gamma', 'L2_gnn_beta', 'L3_gnn_W_self',
        'L3_gnn_W_neigh', 'L3_gnn_bias', 'L3_gnn_gamma', 'L3_gnn_beta']


def kernel(**inputs):
    import numpy as _np
    import concourse.bacc as _bacc
    from concourse import mybir as _mybir
    from concourse.bass_utils import run_bass_kernel_spmd as _run

    nc = _bacc.Bacc("TRN2", target_bir_lowering=False, num_devices=1)
    f32 = _mybir.dt.float32
    arrays, args = {}, []
    for name in _INS:
        a = _np.ascontiguousarray(inputs[name])
        arrays[f"in_{name}"] = a
        args.append(nc.dram_tensor(f"in_{name}", a.shape, _mybir.dt.from_np(a.dtype), kind="ExternalInput").ap())
    args.append(nc.dram_tensor("kv_table", (N, 2 * C), f32).ap())
    args.append(nc.dram_tensor("records", (P * NT, RW), f32).ap())
    args.append(nc.dram_tensor("weights_t", (6, C, C), f32).ap())
    args.append(nc.dram_tensor("out", (N, C), f32, kind="ExternalOutput").ap())
    gnn(nc, *args)
    r = _run(nc, [arrays], core_ids=[0])
    return r.results[0]["out"]
```

```python
import concourse.bass as bass
from concourse import mybir
from contextlib import ExitStack

N = 1024
C = 512
E = 32768
H = 8
D = C // H
HID = 1024
P = 128
NB = N // P
KC = C // P
HC = HID // P
HALF = 512
EPP = E // P
GT = 4
GE = GT * P
NG = 72
NT = NG * GT
RW = 2 + H
EPS = 1e-5
NEG = -1.0e30
NBANK = 8
DVE_TILES = 2


def gnn(nc, x, src, dst, edge_attr_8, Wq, bq, Wk, bk, Wv, bv, Wo, bo, ln1_g, ln1_b, ln2_g, ln2_b,
        W1, b1, W2, b2, l1_ws, l1_wn, l1_b, l1_g, l1_be, l2_wl, l2_bl, l2_wr, l2_g, l2_be,
        l3_ws, l3_wn, l3_b, l3_g, l3_be, kv_table, records, weights_t, out):
    f32 = mybir.dt.float32
    i32 = mybir.dt.int32
    i16 = mybir.dt.int16
    bf16 = mybir.dt.bfloat16
    ALU = mybir.AluOpType
    ACT = mybir.ActivationFunctionType
    AX = mybir.AxisListType

    with ExitStack() as ctx:
        def sb(name, shape, dt=f32):
            return ctx.enter_context(nc.sbuf_tensor(name, shape, dt))

        def sem(name):
            return ctx.enter_context(nc.semaphore(name))

        X = sb("X", [P, NB, C])
        HR = sb("HR", [P, NB, C])
        TR = sb("TR", [P, KC, N])
        W = sb("W", [P, 16, C])
        KV = sb("KV", [P, 8192])
        CT = sb("CT", [P, NB, N])
        recs = sb("recs", [P, NT, RW])
        PR = sb("PR", [P, 2048])
        PV = sb("PV", [P, EPP * RW])
        VEC = sb("VEC", [P, 8, C])
        iota_c = sb("iota_c", [P, N], i16)
        iota_pi = sb("iota_pi", [P, 1], i32)
        iota_p = sb("iota_p", [P, 1])
        iota_g = sb("iota_g", [P, NG])
        ident = sb("ident", [P, P])
        ident_b = sb("ident_b", [P, P], bf16)
        ones = sb("ones", [P, P])
        bcol = sb("bcol", [P, 2 * KC + HC])
        bq8 = sb("bq8", [P, KC])
        dst_i = sb("dst_i", [P, NT], i32)
        row_i = sb("row_i", [P, EPP], i32)
        small = sb("small", [P, 16, 8])
        pad_i = sb("pad_i", [P, 8], i32)
        gblk = sb("gblk", [P, NG])
        gblk_i = sb("gblk_i", [P, NG], i32)
        stage_rec = sb("stage_rec", [P, 2, 8, RW])
        stage_row = sb("stage_row", [P, 2, 8], i32)
        bmax = sb("bmax", [P, H])
        bmax_all = sb("bmax_all", [P, H])
        cmax = sb("cmax", [P, NB, H])
        shift = sb("shift", [P, NB, H], bf16)
        stats = sb("stats", [P, NB, 6])
        mv = sb("mv", [P, NB, 2])
        var_e = sb("var_e", [P, NB])
        std = sb("std", [P, NB])
        rstd = sb("rstd", [P, NB])
        oh_b = sb("oh_b", [P, 2, GT, P], bf16)
        oh_f = sb("oh_f", [P, 2, GT, P])
        ohT = sb("ohT", [P, 2, GT, P], bf16)
        idx = sb("idx", [P, 2, GT], i32)
        score = sb("score", [P, 2, GT * H])
        zsc = sb("zsc", [P, 2, GT * H])
        prob = sb("prob", [P, 2, GT, H])
        Lacc = sb("Lacc", [P, NB, H])

        Z = KV[:, 0:4096].rearrange("p (b c) -> p b c", b=NB)
        QT = KV[:, 4096:6144].bitcast(bf16).rearrange("p (k n) -> p k n", k=KC)
        KTr = KV[:, 6144:8192].bitcast(bf16).rearrange("p (k n) -> p k n", k=KC)
        kvr = KV[:, :].rearrange("p (g j w) -> p g j w", g=2, j=GT)
        hidT = KV[:, :].rearrange("p (k n) -> p k n", k=HC)
        XT = KV[:, 0:4096].rearrange("p (k n) -> p k n", k=KC)
        SQ = KV[:, 4096:8192].rearrange("p (b c) -> p b c", b=NB)
        ctf = CT[:, :, :].rearrange("p b n -> p (b n)")
        attr = ctf[:, 0:2048]
        oh8 = ctf[:, 2048:4096].rearrange("p (b t) -> p b t", b=NB)
        oh8_f = ctf[:, 2048:4096]
        cum = ctf[:, 4096:6144].rearrange("p (b t) -> p b t", b=NB)
        cum_f = ctf[:, 4096:6144]
        pick = ctf[:, 6144:8192].rearrange("p (b t) -> p b t", b=NB)
        zeros_f = ctf[:, 6144:8192]
        rec_src = PV[:, :].rearrange("p (t r) -> p t r", r=RW)
        kvst = PR[:, :].rearrange("p (s w) -> p s w", s=2)
        mask = PR[:, :].rearrange("p (s w) -> p s w", s=2)
        ohd = [PR[:, :].bitcast(bf16).rearrange("p (j n) -> p j n", j=GT),
               PV[:, 0:2048].bitcast(bf16).rearrange("p (j n) -> p j n", j=GT)]
        prod = PR[:, :].rearrange("p (j c) -> p j c", j=GT)
        prod_h = PR[:, :].rearrange("p (a d) -> p a d", d=D)
        pv = [PV[:, 0:2048].rearrange("p (j c) -> p j c", j=GT), W[:, 0:4, :]]
        Qs = W[:, 4:16, :].rearrange("p s c -> p (s c)").bitcast(bf16).rearrange(
            "p (s b c) -> p s b c", s=3, b=NB)
        tmpq = recs[:, 0:205, :].rearrange("p t r -> p (t r)")
        src_i = TR[:, 0, 0:EPP].bitcast(i32)
        blk_i = TR[:, 0, EPP:2 * EPP].bitcast(i32)
        before = TR[:, 2, 0:P]
        dist = PV[:, 2048:2304].bitcast(bf16).rearrange("p (j n) -> p j n", j=GT)
        degrc = TR[:, 1, :]
        wnat = HR[:, 0:4, :]
        wtr = HR[:, 4:8, :]

        ps = ctx.enter_context(nc.psum_tensor("ps", [P, NBANK, C], f32))
        psb = ps[:, 6, :].bitcast(bf16)

        sums_ps = ps[:, 4, :]
        shift_ps = ps[:, 5, 0:GT * H]
        psum_ps = ps[:, 7, 0:H]

        def kv_count(g, a):
            return g * 8 + (16 - 8 * a)

        ld_edges, ld_x, ld_vec, ld_w = sem("ld_edges"), sem("ld_x"), sem("ld_vec"), sem("ld_w")
        ld_recs, filler_made, filler_stored = sem("ld_recs"), sem("filler_made"), sem("filler_stored")
        consts, dve_consts, attr_put = sem("consts"), sem("dve_consts"), sem("attr_put")
        dve_chain = sem("dve_chain")
        sort_n, sort_mm = sem("sort_n"), sem("sort_mm")
        rows_ready = sem("rows_ready")
        staged = sem("staged")
        scat = [sem("scat0"), sem("scat1")]
        bmax_in, bmax_out = sem("bmax_in"), sem("bmax_out")
        z_rows = sem("z_rows")
        ln_var, ln_std = sem("ln_var"), sem("ln_std")
        tile_full, dve_drained, act_drained = sem("tile_full"), sem("dve_drained"), sem("act_drained")
        q_split = sem("q_split")
        kv_stored = [sem("kv_stored0"), sem("kv_stored1")]
        wt_loaded, wt_stored = sem("wt_loaded"), sem("wt_stored")
        ct_zero, ct_ready, cn_ready = sem("ct_zero"), sem("ct_ready"), sem("cn_ready")
        recs_int = sem("recs_int")
        coh, cmm, cflush = sem("coh"), sem("cmm"), sem("cflush")
        csrc_dist, csrc_oh, src_dist = sem("csrc_dist"), sem("csrc_oh"), sem("src_dist")
        deg_full = sem("deg_full")
        act_pv_made = sem("act_pv_made")
        gtab = sem("gtab")
        smm, smax = sem("smm"), sem("smax")
        shift_ready = sem("shift_ready")
        idx_ready, pool_go = sem("idx_ready"), sem("pool_go")
        kv_in = [[sem(f"kv_in{a}{j}") for j in range(GT)] for a in range(2)]
        oh_made, ohf_made, ohT_ps, ohT_sb = sem("oh_made"), sem("ohf_made"), sem("ohT_ps"), sem("ohT_sb")
        q_ps, c_ps, prod_done = sem("q_ps"), sem("c_ps"), sem("prod_done")
        summed, biased, z_made, p_made = sem("summed"), sem("biased"), sem("z_made"), sem("p_made")
        pv_made, agg_done, flushed, l_flushed = sem("pv_made"), sem("agg_done"), sem("flushed"), sem("l_flushed")
        acc_zero = sem("acc_zero")
        ld_wo, ld_w1, ld_w2a, ld_w2b = sem("ld_wo"), sem("ld_w1"), sem("ld_w2a"), sem("ld_w2b")
        ld_l = [sem("ld_l1"), sem("ld_l2"), sem("ld_l3")]
        ld_vec2, ld_vec3, ld_vec4 = sem("ld_vec2"), sem("ld_vec3"), sem("ld_vec4")
        onorm, z2_rows, x_rows, h_rows = sem("onorm"), sem("z2_rows"), sem("x_rows"), sem("h_rows")
        centred, squared, bn_var, bn_std = sem("centred"), sem("squared"), sem("bn_var"), sem("bn_std")
        rc_made = sem("rc_made")
        stored = sem("stored")

        order = []
        first = {}

        def part(name, count, engine):
            first[name] = len(order)
            order.extend([engine] * count)

        part("zT", 8, "act")
        part("K", 8, "dve")
        part("V", 8, "dve")
        part("KT", 8, "act")
        part("QT", 8, "act")
        part("Q", 8, "dve")
        part("WT", 24, "act")
        part("oT", 8, "act")
        part("wo", 8, "dve")
        part("z2T", 8, "act")
        part("hidT", 16, "act")
        part("ff", 8, "dve")
        for layer in (1, 2, 3):
            part(f"xT{layer}", 8, "act")
            part(f"aggT{layer}", 8, "act")
            part(f"h{layer}", 8, "dve")
            if layer == 2:
                part("bn_mean", 1, "dve")
                part("bn_var", 1, "dve")

        def drains(n):
            return order[:n + 1].count(order[n])

        def drained(n):
            return {"act": act_drained, "dve": dve_drained}[order[n]]

        def ln_sizes(which):
            return [(0, NB)] if which == "ln1" else [(0, NB // 2), (NB // 2, NB)]

        block = ctx.enter_context(nc.Block())

        @block.sync
        def _(sp):
            sp.dma_start(src_i[:, :], src.rearrange("(p t) -> p t", p=P)).then_inc(ld_edges, 16)
            sp.dma_start(blk_i[:, :], dst.rearrange("(p t) -> p t", p=P)).then_inc(ld_edges, 16)
            sp.dma_start(attr, edge_attr_8.rearrange("(p t) h -> p (t h)", p=P)).then_inc(ld_edges, 16)
            sp.dma_start(X[:, :, :], x.rearrange("(b p) c -> p b c", p=P)).then_inc(ld_x, 16)
            sp.wait_ge(filler_made, 1)
            sp.dma_start(records.rearrange("(p t) r -> p (t r)", p=P),
                         recs[:, :, :].rearrange("p t r -> p (t r)")).then_inc(filler_stored, 16)
            for s, v in enumerate((ln1_g, ln1_b, bk, bv, bq)):
                sp.dma_start(VEC[:, s, :], v.rearrange("(o c) -> o c", o=1).to_broadcast([P, C])).then_inc(ld_vec, 16)
            for at, v, k in ((0, bq, KC), (KC, bk, KC), (2 * KC, b1, HC)):
                sp.dma_start(bcol[:, at:at + k], v.rearrange("(k p) -> p k", p=P),
                             allow_slow_non_contiguous=True).then_inc(ld_vec, 16)
            for s, w in ((4, Wk), (8, Wv), (0, Wq)):
                sp.dma_start(W[:, s:s + 4, :], w.rearrange("(k p) c -> p k c", p=P)).then_inc(ld_w, 16)
            for b in range(NB):
                sp.wait_ge(dve_drained, drains(first["K"] + 2 * b + 1))
                sp.dma_start(kv_table[b * P:(b + 1) * P, :], kvst[:, b % 2, :]).then_inc(kv_stored[b % 2], 16)
            for m, w in enumerate((l1_ws, l1_wn, l2_wr, l2_wl, l3_ws, l3_wn)):
                if m:
                    sp.wait_ge(tile_full, first["WT"] + 4 * m)
                sp.dma_start(wnat, w.rearrange("(k p) c -> p k c", p=P)).then_inc(wt_loaded, 16)
                sp.wait_ge(act_drained, drains(first["WT"] + 4 * m + 3))
                sp.dma_start(weights_t[m].rearrange("(k p) c -> p k c", p=P), wtr).then_inc(wt_stored, 16)
            sp.wait_ge(q_split, NB)
            for s, v in enumerate((b2, l1_b, l1_g, l1_be, l2_bl, bo, ln2_g, ln2_b)):
                sp.dma_start(VEC[:, s, :], v.rearrange("(o c) -> o c", o=1).to_broadcast([P, C])).then_inc(ld_vec2, 16)
            for a in range(2):
                sp.wait_ge(scat[a], 16 * EPP // 2)
            sp.dma_start(recs[:, :, :].rearrange("p t r -> p (t r)"),
                         records.rearrange("(p t) r -> p (t r)", p=P)).then_inc(ld_recs, 16)
            sp.wait_ge(agg_done, NG)
            sp.dma_start(W[:, 0:4, :], Wo.rearrange("(k p) c -> p k c", p=P)).then_inc(ld_wo, 16)
            sp.dma_start(W[:, 4:12, :].rearrange("p (k a) c -> p k (a c)", k=KC),
                         W1.rearrange("(k p) c -> p k c", p=P)).then_inc(ld_w1, 16)
            w2v = W2.rearrange("(k p) c -> p k c", p=P)
            sp.dma_start(W[:, 12:16, :], w2v[:, 0:4, :]).then_inc(ld_w2a, 16)
            sp.wait_ge(tile_full, first["z2T"])
            sp.dma_start(W[:, 0:4, :], w2v[:, 4:8, :]).then_inc(ld_w2b, 16)
            sp.wait_ge(z2_rows, NB)
            for s, v in ((5, l2_g), (6, l2_be), (7, l3_b)):
                sp.dma_start(VEC[:, s, :], v.rearrange("(o c) -> o c", o=1).to_broadcast([P, C])).then_inc(ld_vec3, 16)
            sp.wait_ge(wt_stored, 96)

            def load_wt(layer, slots):
                for m, s in enumerate(slots):
                    sp.dma_start(W[:, s:s + 4, :], weights_t[2 * (layer - 1) + m].rearrange(
                        "(k p) c -> p k c", p=P)).then_inc(ld_l[layer - 1], 16)

            sp.wait_ge(tile_full, first["ff"])
            load_wt(1, (4, 8))
            sp.wait_ge(tile_full, first["ff"] + NB)
            load_wt(2, (12, 0))
            sp.wait_ge(tile_full, first["h1"] + NB)
            load_wt(3, (4, 8))
            sp.wait_ge(x_rows, 2 * NB)
            for s, v in ((1, l3_g), (2, l3_be)):
                sp.dma_start(VEC[:, s, :], v.rearrange("(o c) -> o c", o=1).to_broadcast([P, C])).then_inc(ld_vec4, 16)
            ov = out.rearrange("(b p) c -> p b c", p=P)
            for lo, hi in ln_sizes("out"):
                sp.wait_ge(x_rows, 3 * NB + hi)
                sp.dma_start(ov[:, lo:hi, :], X[:, lo:hi, :]).then_inc(stored, 16)
            sp.wait_ge(stored, 32)
            sp.wait_ge(filler_stored, 16)
            for a in range(2):
                sp.wait_ge(kv_stored[a], 16 * NB // 2)

        @block.gpsimd
        def _(pool):
            nc.gpsimd.memset(recs[:, :, :], 0.0).then_inc(consts, 1)
            nc.gpsimd.iota(iota_c[:, :], pattern=[[1, N]], base=0, channel_multiplier=0,
                           allow_small_or_imprecise_dtypes=True).then_inc(consts, 1)
            nc.gpsimd.iota(iota_pi[:, :], pattern=[[0, 1]], base=0, channel_multiplier=1).then_inc(consts, 1)
            nc.gpsimd.iota(iota_g[:, :], pattern=[[GE, NG]], base=0, channel_multiplier=0,
                           allow_small_or_imprecise_dtypes=True).then_inc(consts, 1)
            nc.gpsimd.memset(ones[:, :], 1.0).then_inc(consts, 1)
            pool.wait_ge(consts, 5)
            nc.gpsimd.memset(recs[:, :, 0:1], 1.0).then_inc(filler_made, 1)
            pool.wait_ge(bmax_in, 1)
            nc.gpsimd.partition_all_reduce(bmax_all[:, :], bmax[:, :], P, bass.bass_isa.ReduceOp.max).then_inc(bmax_out, 1)

            pool.wait_ge(rows_ready, 1)
            pool.wait_ge(attr_put, 1)
            pool.wait_ge(filler_stored, 16)

            def scatter_tiles(t0, a, k):
                nc.gpsimd.tensor_copy(stage_rec[:, a, :, :], rec_src[:, bass.ds(t0, 8), :]).then_inc(staged, 1)
                nc.gpsimd.tensor_copy(stage_row[:, a, :], row_i[:, bass.ds(t0, 8)]).then_inc(staged, 1)
                pool.wait_ge(staged, k)
                pool.sem_inc(pool_go, 1)
                for j in range(8):
                    nc.gpsimd.indirect_dma_start(
                        out=records[:, :], out_offset=bass.IndirectOffsetOnAxis(ap=stage_row[:, a, j:j + 1], axis=0),
                        in_=stage_rec[:, a, j, :], in_offset=None).then_inc(scat[a], 16)

            scatter_tiles(0, 0, 2)
            scatter_tiles(8, 1, 4)
            with pool.Fori(1, EPP // 16) as i:
                for a in range(2):
                    pool.wait_ge(scat[a], i * (16 * 8))
                    scatter_tiles(i * 16 + 8 * a, a, i * 4 + (2 * a + 2))

            nc.gpsimd.memset(CT[:, :, :], 0.0).then_inc(ct_zero, 1)
            pool.wait_ge(wt_stored, 96)
            nc.gpsimd.memset(HR[:, :, :], 0.0).then_inc(acc_zero, 1)
            nc.gpsimd.memset(Lacc[:, :, :], 0.0).then_inc(acc_zero, 1)

            def gather(g, a, k, wait=True):
                if wait:
                    for j in range(GT):
                        pool.wait_ge(kv_in[a][j], (g - a) * 8)
                nc.gpsimd.tensor_copy(idx[:, a, :], dst_i[:, bass.ds(g * GT, GT)]).then_inc(idx_ready, 1)
                pool.wait_ge(idx_ready, k)
                pool.sem_inc(pool_go, 1)
                for j in range(GT):
                    if wait and j == 0:
                        pool.wait_ge(pv_made, g - 1)
                        pool.sem_inc(pool_go, 1)
                    if wait and j >= DVE_TILES:
                        pool.wait_ge(act_pv_made, (g - 2) * (GT - DVE_TILES) + (j - DVE_TILES + 1))
                        pool.sem_inc(pool_go, 1)
                    nc.gpsimd.indirect_dma_start(
                        out=kvr[:, a, j, :], out_offset=None, in_=kv_table[:, :],
                        in_offset=bass.IndirectOffsetOnAxis(ap=idx[:, a, j:j + 1], axis=0)).then_inc(kv_in[a][j], 16)

            for a in range(2):
                pool.wait_ge(kv_stored[a], 16 * NB // 2)
            pool.wait_ge(recs_int, 1)
            pool.wait_ge(tile_full, first["WT"])
            gather(0, 0, 1, wait=False)
            pool.wait_ge(smm, NB * H)
            gather(1, 1, 2, wait=False)
            with pool.Fori(2, NG - 1, 2) as g:
                for a in range(2):
                    gather(g + a, a, g + (a + 1))

            pool.wait_ge(rc_made, 1)
            for b in range(NB):
                last = nc.gpsimd.tensor_tensor(CT[:, b, :], CT[:, b, :], degrc[:, :], ALU.mult)
            last.then_inc(cn_ready, 1)

        @block.scalar
        def _(act):
            act.wait_ge(ld_edges, 48)
            nc.scalar.copy(rec_src[:, :, 2:RW], attr.rearrange("p (t h) -> p t h", h=H)).then_inc(attr_put, 1)
            roots = [0]

            def root(lo, hi):
                roots[0] += 1
                act.wait_ge(ln_var, roots[0])
                nc.scalar.activation(std[:, lo:hi], var_e[:, lo:hi], ACT.Sqrt).then_inc(ln_std, 1)

            def drain(n, dest, func=None, **kw):
                act.wait_ge(tile_full, n + 1)
                if func is None:
                    nc.scalar.copy(dest, ps[:, n % NBANK, :]).then_inc(act_drained, 1)
                else:
                    nc.scalar.activation(dest, ps[:, n % NBANK, :], func, **kw).then_inc(act_drained, 1)

            def drain_T(name, dest):
                for m in range(2 * KC):
                    half, k = m // KC, m % KC
                    drain(first[name] + m, dest[:, k, half * HALF:(half + 1) * HALF])

            root(0, NB)
            drain_T("zT", TR)
            act.wait_ge(ld_vec, 128)
            for name, dest, b0, scale in (("KT", KTr, bcol[:, KC:2 * KC], 1.0), ("QT", QT, bq8, float(D) ** -0.5)):
                if name == "QT":
                    act.wait_ge(dve_consts, 2)
                for m in range(2 * KC):
                    half, k = m // KC, m % KC
                    drain(first[name] + m, dest[:, k, half * HALF:(half + 1) * HALF], ACT.Identity,
                          bias=b0[:, k:k + 1], scale=scale)
            for m in range(24):
                if m >= 4 and m % 4 == 0:
                    act.wait_ge(wt_stored, 16 * (m // 4))
                drain(first["WT"] + m, wtr[:, m % 4, :])

            def distances(g, done, used):
                if used is not None:
                    act.wait_ge(used, g)
                tiles = recs[:, bass.ds(g * GT, GT), :]
                for j in range(GT):
                    last = nc.scalar.activation(dist[:, j, :], iota_c[:, 0:P], ACT.Abs, bias=tiles[:, j, 0:1], scale=1.0)
                last.then_inc(done, 1)
                act.wait_ge(done, g + 1)

            act.wait_ge(recs_int, 1)

            def count_sources(g, a, wait=True, late=True):
                distances(g, csrc_dist, csrc_oh if late else None)
                if wait:
                    act.wait_ge(cmm, g - 1)
                nc.scalar.activation(oh_b[:, a, :, :], dist[:, :, :], ACT.Relu, bias=1.0, scale=-1.0).then_inc(csrc_oh, 1)

            count_sources(0, 0, wait=False, late=False)
            count_sources(1, 1, wait=False)
            with act.Fori(2, NG - 1, 2) as g:
                for a in range(2):
                    count_sources(g + a, a)

            def edge_sources(g, a, wait=True, first=False):
                distances(g, src_dist, None if first else oh_made)
                if wait:
                    act.wait_ge(ohf_made, g - 1)
                nc.scalar.activation(oh_b[:, a, :, :], dist[:, :, :], ACT.Relu, bias=1.0, scale=-1.0).then_inc(oh_made, 1)

            def sources_f(g, a, wait=True):
                if wait:
                    act.wait_ge(agg_done, g - 1)
                nc.scalar.copy(oh_f[:, a, :, :], oh_b[:, a, :, :]).then_inc(ohf_made, 1)

            def onehots(g, a):
                act.wait_ge(ohT_ps, g + 1)
                nc.scalar.copy(ohT[:, a, :, :], psb[:, 0:GE].rearrange("p (j n) -> p j n", j=GT)).then_inc(ohT_sb, 1)

            def exps(g, a):
                act.wait_ge(z_made, g + 1)
                nc.scalar.activation(prob[:, a, :, :].rearrange("p j h -> p (j h)"), zsc[:, a, :],
                                     ACT.Exp).then_inc(p_made, 1)

            def act_values(g, a):
                act.wait_ge(p_made, g + 1)
                for j in range(DVE_TILES, GT):
                    for h in range(H):
                        last = nc.scalar.activation(pv[a][:, j, h * D:(h + 1) * D], kvr[:, a, j, C + h * D:C + (h + 1) * D],
                                                    ACT.Copy, scale=prob[:, a, j, h:h + 1])
                    last.then_inc(act_pv_made, 1)

            act.wait_ge(cmm, NG)
            act.wait_ge(csrc_oh, NG)
            edge_sources(0, 0, wait=False, first=True)
            edge_sources(1, 1, wait=False)
            onehots(0, 0)

            def edge_step(g, a, wait=True, copies=True, sources=True):
                if copies:
                    onehots(g + 1, 1 - a)
                sources_f(g, a, wait)
                if sources:
                    edge_sources(g + 2, a)
                exps(g, a)
                act_values(g, a)

            edge_step(0, 0, wait=False)
            edge_step(1, 1, wait=False)
            with act.Fori(2, NG - 3, 2) as g:
                for a in range(2):
                    edge_step(g + a, a)
            edge_step(NG - 2, 0, sources=False)
            edge_step(NG - 1, 1, copies=False, sources=False)

            act.wait_ge(cn_ready, 1)
            drain_T("oT", TR)
            for lo, hi in ln_sizes("z2"):
                root(lo, hi)
            drain_T("z2T", TR)
            for m in range(2 * HC):
                half, k = m // HC, m % HC
                drain(first["hidT"] + m, hidT[:, k, half * HALF:(half + 1) * HALF], ACT.Silu,
                      bias=bcol[:, 2 * KC + k:2 * KC + k + 1])
            for lo, hi in ln_sizes("out"):
                root(lo, hi)
            for layer in (1, 2, 3):
                drain_T(f"xT{layer}", XT)
                drain_T(f"aggT{layer}", TR)
                if layer == 2:
                    for b in range(NB):
                        act.wait_ge(centred, b + 1)
                        nc.scalar.activation(SQ[:, b, :], HR[:, b, :], ACT.Square).then_inc(squared, 1)
                    act.wait_ge(bn_var, 1)
                    nc.scalar.activation(PR[:, 512:1024], PR[:, 0:512], ACT.Sqrt).then_inc(bn_std, 1)
                    for lo, hi in ln_sizes("out"):
                        root(lo, hi)
                else:
                    for lo, hi in ln_sizes("out"):
                        root(lo, hi)
                        root(lo, hi)

        @block.vector
        def _(dve):
            chain = [0]

            def link(ins):
                chain[0] += 1
                ins.then_inc(dve_chain, 1)
                dve.wait_ge(dve_chain, chain[0])

            vec = nc.vector
            dve.wait_ge(consts, 5)
            link(vec.tensor_copy(iota_p[:, :], iota_pi[:, :]))
            vec.tensor_scalar(ident[:, :], iota_c[:, 0:P], iota_p[:, 0:1], None, ALU.is_equal)
            vec.tensor_scalar(ident_b[:, :], iota_c[:, 0:P], iota_p[:, 0:1], None, ALU.is_equal)
            vec.tensor_scalar(before, iota_c[:, 0:P], iota_p[:, 0:1], None, ALU.is_gt).then_inc(dve_consts, 1)

            dve.wait_ge(ld_edges, 48)
            srcf = pick[:, 0, :]
            blkf = pick[:, 1, :]
            vec.tensor_copy(rec_src[:, :, 1:2].rearrange("p t o -> p (t o)"), blk_i[:, :])
            link(vec.tensor_copy(srcf, src_i[:, :]))
            link(vec.tensor_scalar(blk_i[:, :], src_i[:, :], 7, None, ALU.arith_shift_right))
            link(vec.tensor_copy(blkf, blk_i[:, :]))
            link(vec.scalar_tensor_tensor(rec_src[:, :, 0:1].rearrange("p t o -> p (t o)"), blkf, float(P), srcf,
                                          ALU.mult, ALU.subtract))
            for b in range(NB):
                last = vec.tensor_scalar(oh8[:, b, :], blkf, float(b), None, ALU.is_equal)
            link(last)
            link(vec.memset(zeros_f, 0.0))
            link(vec.tensor_tensor_scan(cum_f, zeros_f, oh8_f, 0.0, ALU.add, ALU.add))
            last8, prev8, n8, tot8, end8, base8, off8 = (small[:, i, :] for i in range(7))
            link(vec.tensor_copy(last8, cum[:, :, EPP - 1:EPP].rearrange("p b o -> p (b o)")))
            vec.memset(prev8[:, 0:1], 0.0)
            link(vec.tensor_copy(prev8[:, 1:8], last8[:, 0:7]))
            vec.tensor_tensor(n8, last8, prev8, ALU.subtract).then_inc(sort_n, 1)
            dve.wait_ge(sort_mm, 1)
            link(vec.tensor_scalar(tot8, ps[:, 0, 8:16], float(GE - 1), None, ALU.add))
            link(vec.tensor_copy(pad_i[:, :], tot8))
            link(vec.tensor_scalar(pad_i[:, :], pad_i[:, :], -GE, None, ALU.bitwise_and))
            link(vec.tensor_copy(tot8, pad_i[:, :]))
            link(vec.tensor_tensor_scan(end8, zeros_f[:, 0:8], tot8, 0.0, ALU.add, ALU.add))
            link(vec.tensor_tensor(base8, end8, tot8, ALU.subtract))
            link(vec.tensor_tensor(off8, base8, ps[:, 0, 0:8], ALU.add))
            link(vec.scalar_tensor_tensor(off8, off8, -1.0, prev8, ALU.add, ALU.subtract))
            for b in range(NB):
                last = vec.scalar_tensor_tensor(pick[:, b, :], cum[:, b, :], off8[:, b:b + 1], oh8[:, b, :],
                                                ALU.add, ALU.mult)
            link(last)
            slot = cum[:, 0, :]
            tif, ppf = cum[:, 1, :], cum[:, 2, :]
            link(vec.tensor_reduce(slot, pick.rearrange("p b t -> p t b"), AX.X, ALU.add))
            link(vec.tensor_copy(row_i[:, :], slot))
            link(vec.tensor_scalar(blk_i[:, :], row_i[:, :], 7, None, ALU.arith_shift_right))
            link(vec.tensor_copy(tif, blk_i[:, :]))
            link(vec.tensor_scalar(blk_i[:, :], row_i[:, :], P - 1, None, ALU.bitwise_and))
            link(vec.tensor_copy(ppf, blk_i[:, :]))
            link(vec.scalar_tensor_tensor(ppf, ppf, float(NT), tif, ALU.mult, ALU.add))
            vec.tensor_copy(row_i[:, :], ppf).then_inc(rows_ready, 1)
            vec.tensor_reduce(bmax[:, :], attr.rearrange("p (t h) -> p h t", h=H), AX.X, ALU.max).then_inc(bmax_in, 1)
            link(vec.tensor_scalar(gblk[:, :], iota_g[:, :], end8[:, 0:1], None, ALU.is_ge))
            for b in range(1, NB - 1):
                link(vec.scalar_tensor_tensor(gblk[:, :], iota_g[:, :], end8[:, b:b + 1], gblk[:, :],
                                              ALU.is_ge, ALU.add))
            vec.tensor_copy(gblk_i[:, :], gblk[:, :]).then_inc(gtab, 1)

            roots = [0]

            def ln_stats(source, lo, hi):
                for b in range(lo, hi):
                    last = vec.bn_stats(stats[:, b, :], source[:, b, :])
                link(last)
                for b in range(lo, hi):
                    last = vec.bn_aggr(mv[:, b, :], stats[:, b, :])
                link(last)
                roots[0] += 1
                vec.tensor_scalar(var_e[:, lo:hi], mv[:, lo:hi, 1:2].rearrange("p b o -> p (b o)"), EPS, None,
                                  ALU.add).then_inc(ln_var, 1)
                dve.wait_ge(ln_std, roots[0])
                link(vec.reciprocal(rstd[:, lo:hi], std[:, lo:hi]))

            def ln_apply(dest, source, b):
                return vec.tensor_scalar(dest[:, b, :], source[:, b, :], mv[:, b, 0:1], rstd[:, b:b + 1],
                                         ALU.subtract, ALU.mult)

            def phased(lo, hi, *steps):
                for step in steps[:-1]:
                    for b in range(lo, hi):
                        last = step(b)
                    link(last)
                return steps[-1]

            dve.wait_ge(ld_x, 16)
            dve.wait_ge(ld_vec, 128)
            vec.tensor_scalar(bq8[:, :], bcol[:, 0:KC], float(D) ** -0.5, None, ALU.mult).then_inc(dve_consts, 1)
            ln_stats(X, 0, NB)
            last_step = phased(0, NB,
                               lambda b: ln_apply(Z, X, b),
                               lambda b: vec.tensor_tensor(Z[:, b, :], Z[:, b, :], VEC[:, 0, :], ALU.mult),
                               lambda b: vec.tensor_tensor(Z[:, b, :], Z[:, b, :], VEC[:, 1, :], ALU.add))
            for b in range(NB):
                last_step(b).then_inc(z_rows, 1)

            for b in range(NB):
                dve.wait_ge(tile_full, first["K"] + 2 * b + 1)
                if b >= 2:
                    dve.wait_ge(kv_stored[b % 2], 16 * (b // 2))
                vec.tensor_tensor(kvst[:, b % 2, 0:C], ps[:, (first["K"] + 2 * b) % NBANK, :], VEC[:, 2, :],
                                  ALU.add).then_inc(dve_drained, 1)
                dve.wait_ge(tile_full, first["K"] + 2 * b + 2)
                vec.tensor_tensor(kvst[:, b % 2, C:2 * C], ps[:, (first["K"] + 2 * b + 1) % NBANK, :], VEC[:, 3, :],
                                  ALU.add).then_inc(dve_drained, 1)
            dve.wait_ge(filler_stored, 16)
            for b in range(NB):
                n = first["Q"] + b
                q0, q1 = tmpq[:, 0:C], tmpq[:, C:2 * C]
                dve.wait_ge(tile_full, n + 1)
                chain[0] += 1
                vec.tensor_tensor(q0, ps[:, n % NBANK, :], VEC[:, 4, :], ALU.add).then_inc(dve_drained, 1)
                dve.wait_ge(dve_drained, drains(n))
                chain[0] -= 1
                link(vec.tensor_scalar(q0, q0, float(D) ** -0.5, None, ALU.mult))
                link(vec.tensor_copy(Qs[:, 0, b, :], q0))
                link(vec.tensor_tensor(q1, q0, Qs[:, 0, b, :], ALU.subtract))
                link(vec.tensor_copy(Qs[:, 1, b, :], q1))
                link(vec.tensor_tensor(q0, q1, Qs[:, 1, b, :], ALU.subtract))
                chain[0] += 1
                vec.tensor_copy(Qs[:, 2, b, :], q0).then_inc(dve_chain, 1)
                dve.wait_ge(dve_chain, chain[0])
                dve.sem_inc(q_split, 1)

            dve.wait_ge(ld_recs, 16)
            vec.tensor_copy(dst_i[:, :], recs[:, :, 1:2].rearrange("p t o -> p (t o)")).then_inc(recs_int, 1)
            dve.wait_ge(ct_zero, 1)
            dve.wait_ge(gtab, 1)
            for a in range(2):
                dve.wait_ge(kv_stored[a], 16 * NB // 2)

            def count_onehots(g, a, wait=True):
                if wait:
                    dve.wait_ge(cmm, g - 1)
                tiles = recs[:, bass.ds(g * GT, GT), :]
                for j in range(GT):
                    last = vec.tensor_scalar(ohd[a][:, j, :], iota_c[:, :], tiles[:, j, 1:2], None, ALU.is_equal)
                last.then_inc(coh, 1)

            def count_flush(g, a, wait=True):
                at = dve.value_load(gblk_i[0:1, bass.ds(g, 1)], min_val=0, max_val=NB - 1)
                dve.wait_ge(cmm, g + 1)
                if wait:
                    dve.wait_ge(cflush, g)
                vec.tensor_tensor(CT[:, at, :], CT[:, at, :],
                                  ps[:, 2 * a:2 * a + 2, :].rearrange("p a c -> p (a c)"), ALU.add).then_inc(cflush, 1)

            count_onehots(0, 0, wait=False)
            count_onehots(1, 1, wait=False)
            count_flush(0, 0, wait=False)
            with dve.Fori(1, NG - 2, 2) as g:
                for a in range(2):
                    count_onehots(g + (a + 1), a)
                    count_flush(g + a, 1 - a)
            count_flush(NG - 1, 1)
            dve.wait_ge(cflush, NG)
            dve.sem_inc(ct_ready, 1)

            for b in range(NB):
                if b >= 2:
                    dve.wait_ge(smax, H * (b - 1))
                link(vec.tensor_scalar(mask[:, b % 2, :], CT[:, b, :], 0.0, NEG, ALU.is_equal, ALU.mult))
                for h in range(H):
                    m = b * H + h
                    dve.wait_ge(smm, m + 1)
                    if m >= 2:
                        dve.wait_ge(smax, m - 1)
                    bank = 2 * (m % 3)
                    vec.tensor_tensor_reduce(out=PV[:, (m % 2) * N:(m % 2 + 1) * N], in0=ps[:, bank:bank + 2, :].rearrange("p a c -> p (a c)"),
                                             in1=mask[:, b % 2, :], scale=1.0, scalar=4 * NEG, op0=ALU.add,
                                             op1=ALU.max, accum_out=cmax[:, b, h:h + 1]).then_inc(smax, 1)
            dve.wait_ge(smax, NB * H)
            dve.wait_ge(deg_full, 1)
            link(vec.tensor_scalar(degrc, ps[:, 6:8, :].rearrange("p a c -> p (a c)"), 1.0, None, ALU.max))
            dve.wait_ge(bmax_out, 1)
            for b in range(NB):
                last = vec.tensor_tensor(shift[:, b, :], cmax[:, b, :], bmax_all[:, :], ALU.add)
            last.then_inc(shift_ready, 1)
            vec.reciprocal(degrc, degrc).then_inc(rc_made, 1)

            def edge_scores(g, a, wait=True):
                for half in range(2):
                    dve.wait_ge(q_ps, g * 2 + (half + 1))
                    for j in (2 * half, 2 * half + 1):
                        dve.wait_ge(kv_in[a][j], kv_count(g, a))
                    if wait and half == 0:
                        dve.wait_ge(summed, g)
                    vec.tensor_tensor(prod[:, 2 * half:2 * half + 2, :], ps[:, 2 * half:2 * half + 2, :],
                                      kvr[:, a, 2 * half:2 * half + 2, 0:C], ALU.mult).then_inc(prod_done, 1)
                dve.wait_ge(prod_done, g * 2 + 2)
                vec.tensor_reduce(score[:, a, :], prod_h, AX.X, ALU.add).then_inc(summed, 1)
                dve.wait_ge(summed, g + 1)
                tiles = recs[:, bass.ds(g * GT, GT), :]
                vec.tensor_tensor(score[:, a, :].rearrange("p (j h) -> p j h", j=GT),
                                  score[:, a, :].rearrange("p (j h) -> p j h", j=GT),
                                  tiles[:, :, 2:RW], ALU.add).then_inc(biased, 1)
                dve.wait_ge(biased, g + 1)
                dve.wait_ge(c_ps, g + 1)
                vec.tensor_tensor(zsc[:, a, :], score[:, a, :], shift_ps, ALU.subtract).then_inc(z_made, 1)

            def block_of(g):
                return dve.value_load(gblk_i[0:1, bass.ds(g, 1)], min_val=0, max_val=NB - 1)

            def edge_flush(g, a, at, wait=True):
                dve.wait_ge(agg_done, g + 1)
                if wait:
                    dve.wait_ge(flushed, g)
                    dve.wait_ge(l_flushed, g)
                vec.tensor_tensor(Lacc[:, at, :], Lacc[:, at, :], psum_ps, ALU.add).then_inc(l_flushed, 1)
                vec.tensor_tensor(HR[:, at, :], HR[:, at, :], sums_ps, ALU.add).then_inc(flushed, 1)

            def edge_values(g, a):
                dve.wait_ge(p_made, g + 1)
                n = DVE_TILES
                vec.tensor_tensor(pv[a][:, 0:n, :].rearrange("p j (h d) -> p j h d", d=D),
                                  kvr[:, a, 0:n, C:2 * C].rearrange("p j (h d) -> p j h d", d=D),
                                  prob[:, a, 0:n, :].unsqueeze(3).to_broadcast([P, n, H, D]), ALU.mult).then_inc(pv_made, 1)

            dve.wait_ge(acc_zero, 2)
            at = block_of(0)
            edge_scores(0, 0, wait=False)
            edge_values(0, 0)
            edge_scores(1, 1)
            edge_values(1, 1)
            edge_flush(0, 0, at, wait=False)
            with dve.Fori(2, NG - 1, 2) as g:
                for a in range(2):
                    at = block_of(g + (a - 1))
                    edge_scores(g + a, a)
                    edge_flush(g + (a - 1), 1 - a, at)
                    edge_values(g + a, a)
            edge_flush(NG - 1, 1, block_of(NG - 1))
            dve.wait_ge(flushed, NG)
            dve.wait_ge(l_flushed, NG)

            rl = cmax
            link(vec.tensor_scalar(rl[:, :, :], Lacc[:, :, :], 1.0e-37, None, ALU.max))
            link(vec.reciprocal(rl[:, :, :], rl[:, :, :]))
            for b in range(NB):
                o = HR[:, b, :].rearrange("p (h d) -> p h d", d=D)
                vec.tensor_tensor(o, o, rl[:, b, :].unsqueeze(2).to_broadcast([P, H, D]), ALU.mult).then_inc(onorm, 1)
            dve.wait_ge(ld_vec2, 128)
            for lo, hi in ln_sizes("z2"):
                for b in range(lo, hi):
                    n = first["wo"] + b
                    dve.wait_ge(tile_full, n + 1)
                    last = vec.tensor_tensor(HR[:, b, :], ps[:, n % NBANK, :], X[:, b, :], ALU.add)
                    last.then_inc(dve_drained, 1)
                dve.wait_ge(dve_drained, drains(first["wo"] + hi - 1))
                for b in range(lo, hi):
                    last = vec.tensor_tensor(HR[:, b, :], HR[:, b, :], VEC[:, 5, :], ALU.add)
                link(last)
                ln_stats(HR, lo, hi)
                step = phased(lo, hi,
                              lambda b: ln_apply(Z, HR, b),
                              lambda b: vec.tensor_tensor(Z[:, b, :], Z[:, b, :], VEC[:, 6, :], ALU.mult),
                              lambda b: vec.tensor_tensor(Z[:, b, :], Z[:, b, :], VEC[:, 7, :], ALU.add))
                for b in range(lo, hi):
                    step(b).then_inc(z2_rows, 1)
            for b in range(NB):
                last = vec.tensor_tensor(X[:, b, :], X[:, b, :], HR[:, b, :], ALU.add)
            link(last)
            for b in range(NB):
                last = vec.tensor_tensor(X[:, b, :], X[:, b, :], VEC[:, 0, :], ALU.add)
            link(last)
            for lo, hi in ln_sizes("out"):
                for b in range(lo, hi):
                    n = first["ff"] + b
                    dve.wait_ge(tile_full, n + 1)
                    last = vec.tensor_tensor(HR[:, b, :], ps[:, n % NBANK, :], X[:, b, :], ALU.add)
                    last.then_inc(dve_drained, 1)
                dve.wait_ge(dve_drained, drains(first["ff"] + hi - 1))
                ln_stats(HR, lo, hi)
                for b in range(lo, hi):
                    ln_apply(X, HR, b).then_inc(x_rows, 1)

            def gain_relu_add(v_g, v_b, relu, pre):
                steps = list(pre)
                steps.append(lambda b: vec.tensor_tensor(HR[:, b, :], HR[:, b, :], v_g, ALU.mult))
                steps.append(lambda b: vec.tensor_tensor(HR[:, b, :], HR[:, b, :], v_b, ALU.add))
                if relu:
                    steps.append(lambda b: vec.scalar_tensor_tensor(HR[:, b, :], HR[:, b, :], 0.0, X[:, b, :],
                                                                    ALU.max, ALU.add))
                else:
                    steps.append(lambda b: vec.tensor_tensor(HR[:, b, :], HR[:, b, :], X[:, b, :], ALU.add))
                return steps

            def whole(lo, hi, steps):
                for step in steps:
                    for b in range(lo, hi):
                        last = step(b)
                    link(last)

            def take_h(layer, lo, hi, v_bias):
                for b in range(lo, hi):
                    n = first[f"h{layer}"] + b
                    dve.wait_ge(tile_full, n + 1)
                    vec.tensor_tensor(HR[:, b, :], ps[:, n % NBANK, :], v_bias, ALU.add).then_inc(dve_drained, 1)
                dve.wait_ge(dve_drained, drains(first[f"h{layer}"] + hi - 1))

            def finish(lo, hi):
                ln_stats(HR, lo, hi)
                for b in range(lo, hi):
                    ln_apply(X, HR, b).then_inc(x_rows, 1)

            def ln_layer(layer, v_bias, v_g, v_b, relu):
                for lo, hi in ln_sizes("out"):
                    take_h(layer, lo, hi, v_bias)
                    ln_stats(HR, lo, hi)
                    whole(lo, hi, gain_relu_add(v_g, v_b, relu, [lambda b: ln_apply(HR, HR, b)]))
                    finish(lo, hi)

            ln_layer(1, VEC[:, 1, :], VEC[:, 2, :], VEC[:, 3, :], True)

            dve.wait_ge(ld_vec3, 48)
            take_h(2, 0, NB, VEC[:, 4, :])
            dve.sem_inc(h_rows, 1)
            n = first["bn_mean"]
            dve.wait_ge(tile_full, n + 1)
            vec.tensor_scalar(PR[:, 0:C], ps[:, n % NBANK, :], 1.0 / N, None, ALU.mult).then_inc(dve_drained, 1)
            dve.wait_ge(dve_drained, drains(n))
            for b in range(NB):
                vec.tensor_tensor(HR[:, b, :], HR[:, b, :], PR[:, 0:C], ALU.subtract).then_inc(centred, 1)
            dve.wait_ge(centred, NB)
            n = first["bn_var"]
            dve.wait_ge(tile_full, n + 1)
            vec.tensor_scalar(PR[:, 0:C], ps[:, n % NBANK, :], 1.0 / N, EPS, ALU.mult, ALU.add).then_inc(dve_drained, 1)
            dve.wait_ge(dve_drained, drains(n))
            dve.sem_inc(bn_var, 1)
            dve.wait_ge(bn_std, 1)
            link(vec.reciprocal(PR[:, 0:C], PR[:, C:2 * C]))
            link(vec.tensor_tensor(PR[:, 0:C], PR[:, 0:C], VEC[:, 5, :], ALU.mult))
            for lo, hi in ln_sizes("out"):
                whole(lo, hi, gain_relu_add(PR[:, 0:C], VEC[:, 6, :], True, []))
                finish(lo, hi)

            dve.wait_ge(ld_vec4, 32)
            ln_layer(3, VEC[:, 7, :], VEC[:, 1, :], VEC[:, 2, :], False)

        @block.tensor
        def _(pe):
            mm = nc.tensor.matmul

            def free_bank(n):
                if n >= NBANK:
                    pe.wait_ge(drained(n - NBANK), drains(n - NBANK))
                return ps[:, n % NBANK, :]

            def transposes(name, source, rows, per):
                for m in range(2 * KC):
                    half, k = m // KC, m % KC
                    n = first[name] + m
                    pe.wait_ge(rows, per + (half + 1) * (NB // 2))
                    bank = free_bank(n)
                    for j in range(4):
                        last = nc.tensor.transpose(bank[:, j * P:(j + 1) * P],
                                                   source[:, 4 * half + j, k * P:(k + 1) * P], ident[:, :])
                    last.then_inc(tile_full, 1)

            pe.wait_ge(dve_consts, 1)
            pe.wait_ge(consts, 5)
            pe.wait_ge(sort_n, 1)
            mm(ps[:, 0, 0:8], before, small[:, 2, :], start=True, stop=True)
            mm(ps[:, 0, 8:16], ones[:, :], small[:, 2, :], start=True, stop=True).then_inc(sort_mm, 1)

            pe.wait_ge(rows_ready, 1)
            transposes("zT", Z, z_rows, 0)
            pe.wait_ge(ld_w, 48)

            for b in range(NB):
                for v in range(2):
                    n = first["K"] + 2 * b + v
                    pe.wait_ge(act_drained, drains(first["zT"] + KC * (b // 4) + KC - 1))
                    bank = free_bank(n)
                    for k in range(KC):
                        last = mm(bank, TR[:, k, b * P:(b + 1) * P], W[:, 4 + 4 * v + k, :],
                                  start=k == 0, stop=k == KC - 1)
                    last.then_inc(tile_full, 1)
            for name, w0 in (("KT", 4), ("QT", 0)):
                for m in range(2 * KC):
                    half, o = m // KC, m % KC
                    n = first[name] + m
                    bank = free_bank(n)
                    for k in range(KC):
                        last = mm(bank, W[:, w0 + k, o * P:(o + 1) * P], TR[:, k, half * HALF:(half + 1) * HALF],
                                  start=k == 0, stop=k == KC - 1)
                    last.then_inc(tile_full, 1)
            for b in range(NB):
                n = first["Q"] + b
                bank = free_bank(n)
                for k in range(KC):
                    last = mm(bank, TR[:, k, b * P:(b + 1) * P], W[:, k, :], start=k == 0, stop=k == KC - 1)
                last.then_inc(tile_full, 1)
            for m in range(24):
                n = first["WT"] + m
                pe.wait_ge(wt_loaded, 16 * (m // 4 + 1))
                bank = free_bank(n)
                for j in range(4):
                    last = nc.tensor.transpose(bank[:, j * P:(j + 1) * P], wnat[:, j, (m % 4) * P:(m % 4 + 1) * P],
                                               ident[:, :])
                last.then_inc(tile_full, 1)

            pe.wait_ge(act_drained, drains(first["WT"] + 23))
            pe.wait_ge(dve_drained, drains(first["Q"] + NB - 1))

            def count_mm(g, a, wait=True):
                pe.wait_ge(coh, g + 1)
                pe.wait_ge(csrc_oh, g + 1)
                if wait:
                    pe.wait_ge(cflush, g - 1)
                for j in range(GT):
                    for half in range(2):
                        last = mm(ps[:, 2 * a + half, :], oh_b[:, a, j, :], ohd[a][:, j, half * HALF:(half + 1) * HALF],
                                  start=j == 0, stop=j == GT - 1)
                last.then_inc(cmm, 1)

            count_mm(0, 0, wait=False)
            count_mm(1, 1, wait=False)
            with pe.Fori(2, NG - 1, 2) as g:
                for a in range(2):
                    count_mm(g + a, a)

            pe.wait_ge(ct_ready, 1)
            for b in range(NB):
                for h in range(H):
                    m = b * H + h
                    bank = 2 * (m % 3)
                    if m >= 3:
                        pe.wait_ge(smax, m - 2)
                    lo = D * (h % 2)
                    for half in range(2):
                        last = mm(ps[:, bank + half, :], QT[lo:lo + D, h // 2, b * P:(b + 1) * P],
                                  KTr[lo:lo + D, h // 2, half * HALF:(half + 1) * HALF], start=True, stop=True)
                    last.then_inc(smm, 1)
                for m in range(2):
                    last = mm(ps[:, 6 + m, :], ones[:, :], CT[:, b, m * HALF:(m + 1) * HALF],
                              start=b == 0, stop=b == NB - 1)
            last.then_inc(deg_full, 1)
            pe.wait_ge(shift_ready, 1)
            pe.wait_ge(q_split, NB)

            def edge_transposes(g, a, wait=True):
                pe.wait_ge(oh_made, g + 1)
                if wait:
                    pe.wait_ge(ohT_sb, g)
                for j in range(GT):
                    last = nc.tensor.transpose(psb[:, j * P:(j + 1) * P], oh_b[:, a, j, :], ident_b[:, :])
                last.then_inc(ohT_ps, 1)

            def edge_front(g, a, at, wait=True):
                pe.wait_ge(ohT_sb, g + 1)
                for half in range(2):
                    if wait:
                        pe.wait_ge(prod_done, g * 2 + (half - 1))
                    for j in (2 * half, 2 * half + 1):
                        for s in range(3):
                            last = mm(ps[:, j, :], ohT[:, a, j, :], Qs[:, s, at, :], start=s == 0, stop=s == 2)
                    last.then_inc(q_ps, 1)
                if wait:
                    pe.wait_ge(z_made, g)
                for j in range(GT):
                    last = mm(shift_ps[:, j * H:(j + 1) * H], ohT[:, a, j, :], shift[:, at, :], start=True, stop=True)
                last.then_inc(c_ps, 1)

            def edge_back(g, a, wait=True):
                pe.wait_ge(p_made, g + 1)
                if wait:
                    pe.wait_ge(l_flushed, g)
                    pe.wait_ge(flushed, g)
                for j in range(GT):
                    mm(psum_ps, oh_f[:, a, j, :], prob[:, a, j, :], start=j == 0, stop=j == GT - 1)
                for j in range(GT):
                    if j == 0:
                        pe.wait_ge(pv_made, g + 1)
                    if j >= DVE_TILES:
                        pe.wait_ge(act_pv_made, g * (GT - DVE_TILES) + (j - DVE_TILES + 1))
                    last = mm(sums_ps, oh_f[:, a, j, :], pv[a][:, j, :], start=j == 0, stop=j == GT - 1)
                last.then_inc(agg_done, 1)

            def block_of(g):
                return pe.value_load(gblk_i[0:1, bass.ds(g, 1)], min_val=0, max_val=NB - 1)

            pe.wait_ge(gtab, 1)
            edge_transposes(0, 0, wait=False)
            edge_front(0, 0, block_of(0), wait=False)
            edge_transposes(1, 1)
            edge_front(1, 1, block_of(1))
            edge_transposes(2, 0)
            edge_back(0, 0, wait=False)
            with pe.Fori(1, NG - 4, 2) as g:
                for a in range(2):
                    at = block_of(g + (a + 1))
                    edge_front(g + (a + 1), a, at)
                    edge_transposes(g + (a + 2), 1 - a)
                    edge_back(g + a, 1 - a)
            edge_front(NG - 2, 0, block_of(NG - 2))
            edge_transposes(NG - 1, 1)
            edge_back(NG - 3, 1)
            edge_front(NG - 1, 1, block_of(NG - 1))
            edge_back(NG - 2, 0)
            edge_back(NG - 1, 1)

            pe.wait_ge(flushed, NG)
            pe.wait_ge(l_flushed, NG)
            transposes("oT", HR, onorm, 0)
            pe.wait_ge(ld_wo, 16)
            for b in range(NB):
                n = first["wo"] + b
                pe.wait_ge(act_drained, drains(first["oT"] + KC * (b // 4) + KC - 1))
                bank = free_bank(n)
                for k in range(KC):
                    last = mm(bank, TR[:, k, b * P:(b + 1) * P], W[:, k, :], start=k == 0, stop=k == KC - 1)
                last.then_inc(tile_full, 1)
            transposes("z2T", Z, z2_rows, 0)
            pe.wait_ge(ld_w1, 16)
            w1 = W[:, 4:12, :].rearrange("p (k a) c -> p k (a c)", k=KC)
            for m in range(2 * HC):
                half, o = m // HC, m % HC
                n = first["hidT"] + m
                pe.wait_ge(act_drained, drains(first["z2T"] + 2 * KC - 1))
                bank = free_bank(n)
                for k in range(KC):
                    last = mm(bank, w1[:, k, o * P:(o + 1) * P], TR[:, k, half * HALF:(half + 1) * HALF],
                              start=k == 0, stop=k == KC - 1)
                last.then_inc(tile_full, 1)
            pe.wait_ge(ld_w2a, 16)
            pe.wait_ge(ld_w2b, 16)
            for b in range(NB):
                n = first["ff"] + b
                pe.wait_ge(act_drained, drains(first["hidT"] + HC * (b // 4) + HC - 1))
                bank = free_bank(n)
                for k in range(HC):
                    last = mm(bank, hidT[:, k, b * P:(b + 1) * P], W[:, (12 + k) % 16, :], start=k == 0, stop=k == HC - 1)
                last.then_inc(tile_full, 1)

            pe.wait_ge(cn_ready, 1)
            for layer, (ws, wn) in ((1, (4, 8)), (2, (12, 0)), (3, (4, 8))):
                transposes(f"xT{layer}", X, x_rows, (layer - 1) * NB)
                pe.wait_ge(x_rows, layer * NB)
                for m in range(2 * KC):
                    half, k = m // KC, m % KC
                    n = first[f"aggT{layer}"] + m
                    bank = free_bank(n)
                    for b in range(NB):
                        last = mm(bank, X[:, b, k * P:(k + 1) * P], CT[:, b, half * HALF:(half + 1) * HALF],
                                  start=b == 0, stop=b == NB - 1)
                    last.then_inc(tile_full, 1)
                pe.wait_ge(ld_l[layer - 1], 32)
                for b in range(NB):
                    n = first[f"h{layer}"] + b
                    pe.wait_ge(act_drained, drains(first[f"aggT{layer}"] + KC * (b // 4) + KC - 1))
                    bank = free_bank(n)
                    for k in range(KC):
                        mm(bank, XT[:, k, b * P:(b + 1) * P], W[:, ws + k, :], start=k == 0, stop=False)
                    for k in range(KC):
                        last = mm(bank, TR[:, k, b * P:(b + 1) * P], W[:, wn + k, :], start=False, stop=k == KC - 1)
                    last.then_inc(tile_full, 1)
                if layer == 2:
                    for name, source, ready, count in (("bn_mean", HR, h_rows, 1), ("bn_var", SQ, squared, NB)):
                        n = first[name]
                        pe.wait_ge(ready, count)
                        bank = free_bank(n)
                        for b in range(NB):
                            last = mm(bank, ones[:, :], source[:, b, :], start=b == 0, stop=b == NB - 1)
                        last.then_inc(tile_full, 1)


_INS = ['x', 'src', 'dst', 'edge_attr_8', 'L0_gnn_Wq', 'L0_gnn_bq', 'L0_gnn_Wk', 'L0_gnn_bk', 'L0_gnn_Wv', 'L0_gnn_bv',
        'L0_gnn_Wo', 'L0_gnn_bo', 'L0_gnn_ln1_g', 'L0_gnn_ln1_b', 'L0_gnn_ln2_g', 'L0_gnn_ln2_b', 'L0_gnn_W1',
        'L0_gnn_b1', 'L0_gnn_W2', 'L0_gnn_b2', 'L1_gnn_w_self', 'L1_gnn_w_neigh', 'L1_gnn_bias', 'L1_gnn_gamma',
        'L1_gnn_beta', 'L2_gnn_W_l', 'L2_gnn_b_l', 'L2_gnn_W_r', 'L2_gnn_gamma', 'L2_gnn_beta', 'L3_gnn_W_self',
        'L3_gnn_W_neigh', 'L3_gnn_bias', 'L3_gnn_gamma', 'L3_gnn_beta']


def kernel(**inputs):
    import numpy as _np
    import concourse.bacc as _bacc
    from concourse import mybir as _mybir
    from concourse.bass_utils import run_bass_kernel_spmd as _run

    nc = _bacc.Bacc("TRN2", target_bir_lowering=False, num_devices=1)
    f32 = _mybir.dt.float32
    arrays, args = {}, []
    for name in _INS:
        a = _np.ascontiguousarray(inputs[name])
        arrays[f"in_{name}"] = a
        args.append(nc.dram_tensor(f"in_{name}", a.shape, _mybir.dt.from_np(a.dtype), kind="ExternalInput").ap())
    args.append(nc.dram_tensor("kv_table", (N, 2 * C), f32).ap())
    args.append(nc.dram_tensor("records", (P * NT, RW), f32).ap())
    args.append(nc.dram_tensor("weights_t", (6, C, C), f32).ap())
    args.append(nc.dram_tensor("out", (N, C), f32, kind="ExternalOutput").ap())
    gnn(nc, *args)
    r = _run(nc, [arrays], core_ids=[0])
    return r.results[0]["out"]
```

```python
import concourse.bass as bass
from concourse import mybir
from contextlib import ExitStack

N = 1024
C = 512
E = 32768
H = 8
D = C // H
HID = 1024
P = 128
NB = N // P
KC = C // P
HC = HID // P
HALF = 512
EPP = E // P
GT = 4
GE = GT * P
NG = 72
NT = NG * GT
RW = 2 + H
EPS = 1e-5
NEG = -1.0e30
NBANK = 8
KT_LAG = 3
DVE_TILES = 2


def gnn(nc, x, src, dst, edge_attr_8, Wq, bq, Wk, bk, Wv, bv, Wo, bo, ln1_g, ln1_b, ln2_g, ln2_b,
        W1, b1, W2, b2, l1_ws, l1_wn, l1_b, l1_g, l1_be, l2_wl, l2_bl, l2_wr, l2_g, l2_be,
        l3_ws, l3_wn, l3_b, l3_g, l3_be, kv_table, records, weights_t, out):
    f32 = mybir.dt.float32
    i32 = mybir.dt.int32
    i16 = mybir.dt.int16
    bf16 = mybir.dt.bfloat16
    ALU = mybir.AluOpType
    ACT = mybir.ActivationFunctionType
    AX = mybir.AxisListType

    with ExitStack() as ctx:
        def sb(name, shape, dt=f32):
            return ctx.enter_context(nc.sbuf_tensor(name, shape, dt))

        def sem(name):
            return ctx.enter_context(nc.semaphore(name))

        X = sb("X", [P, NB, C])
        HR = sb("HR", [P, NB, C])
        TR = sb("TR", [P, KC, N])
        W = sb("W", [P, 16, C])
        KV = sb("KV", [P, 8192])
        CT = sb("CT", [P, NB, N])
        recs = sb("recs", [P, NT, RW])
        PR = sb("PR", [P, 2048])
        PV = sb("PV", [P, EPP * RW])
        VEC = sb("VEC", [P, 8, C])
        iota_c = sb("iota_c", [P, N], i16)
        iota_pi = sb("iota_pi", [P, 1], i32)
        iota_p = sb("iota_p", [P, 1])
        iota_g = sb("iota_g", [P, NG])
        ident = sb("ident", [P, P])
        ident_b = sb("ident_b", [P, P], bf16)
        ones = sb("ones", [P, P])
        b1_col = sb("b1_col", [P, HC])
        dst_i = sb("dst_i", [P, NT], i32)
        row_i = sb("row_i", [P, EPP], i32)
        small = sb("small", [P, 16, 8])
        pad_i = sb("pad_i", [P, 8], i32)
        gblk = sb("gblk", [P, NG])
        gblk_i = sb("gblk_i", [P, NG], i32)
        order_i = sb("order_i", [1, 2 * NG], i32)
        stage_rec = sb("stage_rec", [P, 2, 8, RW])
        stage_row = sb("stage_row", [P, 2, 8], i32)
        bmax = sb("bmax", [P, H])
        bmax_all = sb("bmax_all", [P, H])
        cmax = sb("cmax", [P, NB, H])
        shift = sb("shift", [P, NB, H], bf16)
        stats = sb("stats", [P, NB, 6])
        mv = sb("mv", [P, NB, 2])
        var_e = sb("var_e", [P, NB])
        std = sb("std", [P, NB])
        rstd = sb("rstd", [P, NB])
        oh_b = sb("oh_b", [P, 2, GT, P], bf16)
        oh_f = sb("oh_f", [P, 2, GT, P])
        ohT = sb("ohT", [P, 2, GT, P], bf16)
        idx = sb("idx", [P, 2, GT], i32)
        score = sb("score", [P, 2, GT * H])
        zsc = sb("zsc", [P, 2, GT * H])
        prob = sb("prob", [P, 2, GT, H])
        Lacc = sb("Lacc", [P, NB, H])

        Z = KV[:, 0:4096].rearrange("p (b c) -> p b c", b=NB)
        QT = KV[:, 0:2048].bitcast(bf16).rearrange("p (k n) -> p k n", k=KC)
        KTr = KV[:, 2048:4096].bitcast(bf16).rearrange("p (k n) -> p k n", k=KC)
        kvr = [KV[:, 4096:8192].rearrange("p (j w) -> p j w", j=GT), KV[:, 0:4096].rearrange("p (j w) -> p j w", j=GT)]
        hidT = KV[:, :].rearrange("p (k n) -> p k n", k=HC)
        XT = KV[:, 0:4096].rearrange("p (k n) -> p k n", k=KC)
        SQ = KV[:, 4096:8192].rearrange("p (b c) -> p b c", b=NB)
        ctf = CT[:, :, :].rearrange("p b n -> p (b n)")
        attr = ctf[:, 0:2048]
        oh8 = ctf[:, 2048:3072].bitcast(bf16).rearrange("p (b t) -> p b t", b=NB)
        cum = ctf[:, 4096:6144].rearrange("p (b t) -> p b t", b=NB)
        cum_f = ctf[:, 4096:6144]
        pick = ctf[:, 6144:8192].rearrange("p (b t) -> p b t", b=NB)
        pick_f = ctf[:, 6144:8192]
        rec_src = PV[:, :].rearrange("p (t r) -> p t r", r=RW)
        kvst = PR[:, :].rearrange("p (s w) -> p s w", s=2)
        mask = PR[:, :].rearrange("p (s w) -> p s w", s=2)
        ohd = [PR[:, :].bitcast(bf16).rearrange("p (j n) -> p j n", j=GT),
               W[:, 0:4, :].rearrange("p s c -> p (s c)").bitcast(bf16).rearrange("p (j n) -> p j n", j=GT)]
        prod = PR[:, :].rearrange("p (j c) -> p j c", j=GT)
        prod_h = PR[:, :].rearrange("p (a d) -> p a d", d=D)
        z2 = [PR[:, :].rearrange("p (b c) -> p b c", c=C), PV[:, 0:2048].rearrange("p (b c) -> p b c", c=C)]
        pv = [PV[:, 0:2048].rearrange("p (j c) -> p j c", j=GT), W[:, 0:4, :]]
        Qs = W[:, 4:16, :].rearrange("p s c -> p (s c)").bitcast(bf16).rearrange(
            "p (s b c) -> p s b c", s=3, b=NB)
        tmpq = recs[:, 0:205, :].rearrange("p t r -> p (t r)")
        src_i = TR[:, 0, 0:EPP].bitcast(i32)
        blk_i = TR[:, 0, EPP:2 * EPP].bitcast(i32)
        ones_b = TR[:, 2, 0:P // 2].bitcast(bf16)
        upto_b = TR[:, 2, P // 2:P].bitcast(bf16)
        dist = TR[:, 3, 0:256].bitcast(bf16).rearrange("p (j n) -> p j n", j=GT)
        inv_degree = TR[:, 1, :]
        w_stage = KV[:, 4096:8192].rearrange("p (k c) -> p k c", c=C)
        wnat = [HR[:, 0:4, :], w_stage[:, 0:4, :]]
        wtr = [HR[:, 4:8, :], w_stage[:, 4:8, :]]

        ps = ctx.enter_context(nc.psum_tensor("ps", [P, NBANK, C], f32))
        psb = ps[:, 6, :].bitcast(bf16)

        sums_ps = ps[:, 4, :]
        shift_ps = ps[:, 5, 0:GT * H]
        psum_ps = ps[:, 7, 0:H]

        def kv_count(g, a):
            return g * 8 + (16 - 8 * a)

        ld_edges, ld_x, ld_vec, ld_w = sem("ld_edges"), sem("ld_x"), sem("ld_vec"), sem("ld_w")
        group_in = [sem("group_in0"), sem("group_in1")]
        filler_made, filler_stored, order_made = sem("filler_made"), sem("filler_stored"), sem("order_made")
        consts, dve_consts, attr_put = sem("consts"), sem("dve_consts"), sem("attr_put")
        dve_chain = sem("dve_chain")
        sort_n, sort_mm = sem("sort_n"), sem("sort_mm")
        rows_ready = sem("rows_ready")
        staged = sem("staged")
        scat = [sem("scat0"), sem("scat1")]
        bmax_in, bmax_out = sem("bmax_in"), sem("bmax_out")
        z_rows = sem("z_rows")
        ln_var, ln_std = sem("ln_var"), sem("ln_std")
        tile_full, dve_drained, act_drained = sem("tile_full"), sem("dve_drained"), sem("act_drained")
        q_split = sem("q_split")
        kv_stored = [sem("kv_stored0"), sem("kv_stored1")]
        wt_loaded, wt_stored = [sem("wt_loaded0"), sem("wt_loaded1")], [sem("wt_stored0"), sem("wt_stored1")]
        ct_ready, cn_ready = sem("ct_ready"), sem("cn_ready")
        recs_int = sem("recs_int")
        coh, cmm, cflush = sem("coh"), sem("cmm"), sem("cflush")
        csrc_dist, csrc_oh, src_dist = sem("csrc_dist"), sem("csrc_oh"), sem("src_dist")
        deg_full = sem("deg_full")
        act_pv_made = sem("act_pv_made")
        gtab = sem("gtab")
        smm, smax = sem("smm"), sem("smax")
        shift_ready = sem("shift_ready")
        idx_ready, pool_go = sem("idx_ready"), sem("pool_go")
        kv_in = [[sem(f"kv_in{a}{j}") for j in range(GT)] for a in range(2)]
        oh_made, ohf_made, ohT_ps, ohT_sb = sem("oh_made"), sem("ohf_made"), sem("ohT_ps"), sem("ohT_sb")
        q_ps, c_ps, prod_done = sem("q_ps"), sem("c_ps"), sem("prod_done")
        summed, biased, z_made, p_made = sem("summed"), sem("biased"), sem("z_made"), sem("p_made")
        pv_made, agg_done, flushed, l_flushed = sem("pv_made"), sem("agg_done"), sem("flushed"), sem("l_flushed")
        acc_zero = sem("acc_zero")
        ld_wo, ld_w1, ld_w2a, ld_w2b = sem("ld_wo"), sem("ld_w1"), sem("ld_w2a"), sem("ld_w2b")
        ld_l = [sem("ld_l1"), sem("ld_l2"), sem("ld_l3")]
        ld_vec2, ld_vec3, ld_vec4 = sem("ld_vec2"), sem("ld_vec3"), sem("ld_vec4")
        onorm, z2_rows, x_rows, mean_drained = sem("onorm"), sem("z2_rows"), sem("x_rows"), sem("mean_drained")
        centred, squared, bn_var, bn_std = sem("centred"), sem("squared"), sem("bn_var"), sem("bn_std")
        x_biased, q_scaled = sem("x_biased"), sem("q_scaled")
        rc_made, degree_put, bn_sums = sem("rc_made"), sem("degree_put"), sem("bn_sums")
        stored = sem("stored")

        order = []
        first = {}

        def part(name, count, engine):
            first[name] = len(order)
            order.extend([engine] * count)

        part("WT0", 12, "act")
        part("zT", 8, "act")
        part("WT12", 4, "act")
        for b in range(NB + KT_LAG):
            if b < NB:
                part(f"K{b}", 1, "dve")
                part(f"V{b}", 1, "dve")
            if b >= KT_LAG:
                part(f"KT{b - KT_LAG}", 1, "act")
        part("WT16", 8, "act")
        part("order", 1, "dve")
        for b in range(NB + 1):
            if b < NB:
                part(f"Q{b}", 1, "dve")
            if b:
                part(f"QT{b - 1}", 1, "act")
        part("oT", 8, "act")
        part("wo", 8, "dve")
        for half in range(2):
            part(f"z2T{half}", 4, "act")
            part(f"hidT{half}", 8, "act")
        part("ff", 8, "dve")
        for layer in (1, 2, 3):
            part(f"aggT{layer}", 8, "act")
            part(f"xT{layer}", 8, "act")
            if layer == 2:
                part("h2", 1, "dve")
                part("bn_mean", 1, "mean")
                part("h2_rest", 7, "dve")
                part("bn_var", 1, "dve")
            else:
                part(f"h{layer}", 8, "dve")

        def wt_tile(m):
            start = 0 if m < 12 else 12 if m < 16 else 16
            return first[f"WT{start}"] + m - start

        def h_tile(layer, b):
            return first["h2_rest"] + b - 1 if layer == 2 and b else first[f"h{layer}"] + b

        def drains(n):
            return order[:n + 1].count(order[n])

        def drained(n):
            return {"act": act_drained, "dve": dve_drained, "mean": mean_drained}[order[n]]

        def ln_sizes(which):
            return {"out2": [(0, 2), (2, 4), (4, 6), (6, 8)], "out3": [(0, 2), (2, 4), (4, 6), (6, 7), (7, 8)]}.get(
                which, [(0, NB // 2), (NB // 2, NB)])

        block = ctx.enter_context(nc.Block())

        @block.sync
        def _(sp):
            sp.dma_start(src_i[:, :], src.rearrange("(p t) -> p t", p=P)).then_inc(ld_edges, 16)
            sp.dma_start(blk_i[:, :], dst.rearrange("(p t) -> p t", p=P)).then_inc(ld_edges, 16)
            sp.dma_start(attr, edge_attr_8.rearrange("(p t) h -> p (t h)", p=P)).then_inc(ld_edges, 16)
            sp.dma_start(X[:, :, :], x.rearrange("(b p) c -> p b c", p=P)).then_inc(ld_x, 16)
            def load_natural(m):
                w = (l1_ws, l1_wn, l2_wr, l2_wl, l3_ws, l3_wn)[m]
                sp.dma_start(wnat[m % 2], w.rearrange("(k p) c -> p k c", p=P)).then_inc(wt_loaded[m % 2], 16)

            load_natural(0)
            load_natural(1)
            sp.wait_ge(filler_made, 1)
            sp.dma_start(records.rearrange("(p t) r -> p (t r)", p=P),
                         recs[:, :, :].rearrange("p t r -> p (t r)")).then_inc(filler_stored, 16)
            for s, v in enumerate((ln1_g, ln1_b, bk, bv, bq)):
                sp.dma_start(VEC[:, s, :], v.rearrange("(o c) -> o c", o=1).to_broadcast([P, C])).then_inc(ld_vec, 16)
            sp.dma_start(b1_col[:, :], b1.rearrange("(k p) -> p k", p=P), allow_slow_non_contiguous=True).then_inc(ld_vec, 16)
            for s, w in ((4, Wk), (8, Wv), (0, Wq)):
                sp.dma_start(W[:, s:s + 4, :], w.rearrange("(k p) c -> p k c", p=P)).then_inc(ld_w, 16)
            def store_transposed(m):
                sp.wait_ge(act_drained, drains(wt_tile(4 * m + 3)))
                sp.dma_start(weights_t[m].rearrange("(k p) c -> p k c", p=P), wtr[m % 2]).then_inc(wt_stored[m % 2], 16)

            for m in range(4):
                store_transposed(m)
                load_natural(m + 2)
            for b in range(NB):
                sp.wait_ge(dve_drained, drains(first[f"V{b}"]))
                sp.dma_start(kv_table[b * P:(b + 1) * P, :], kvst[:, b % 2, :]).then_inc(kv_stored[b % 2], 16)
            store_transposed(4)
            store_transposed(5)
            sp.wait_ge(q_split, NB)
            sp.wait_ge(tile_full, first[f"QT{NB - 1}"] + 1)
            sp.wait_ge(dve_drained, drains(first["order"]))

            def load_group(k, a, wait=True):
                g = sp.value_load(order_i[0:1, bass.ds(k, 1)], min_val=0, max_val=NG - 1)
                if wait:
                    sp.wait_ge(group_in[a], (k - a) * 8)
                sp.dma_start(recs[:, bass.ds(g * GT, GT), :],
                             records.rearrange("(p t) r -> p t r", p=P)[:, bass.ds(g * GT, GT), :]).then_inc(group_in[a], 16)

            def load_four(i, wait=True):
                for k in range(4):
                    sp.wait_ge(scat[0], (i + (2 if k == 0 else 3)) * (16 * 8))
                    sp.wait_ge(scat[1], (i + (3 if k == 3 else 2)) * (16 * 8))
                    load_group(i * 4 + k, k % 2, wait or k >= 2)

            load_four(0, wait=False)
            with sp.Fori(1, EPP // 16 - 2) as i:
                load_four(i)
            with sp.Fori((EPP // 16 - 2) * 4, NG - 1, 2) as k:
                for a in range(2):
                    load_group(k + a, a)
            for s, v in enumerate((b2, l1_b, l1_g, l1_be, l2_bl, bo, ln2_g, ln2_b)):
                sp.dma_start(VEC[:, s, :], v.rearrange("(o c) -> o c", o=1).to_broadcast([P, C])).then_inc(ld_vec2, 16)
            sp.wait_ge(agg_done, NG)
            sp.dma_start(W[:, 0:4, :], Wo.rearrange("(k p) c -> p k c", p=P)).then_inc(ld_wo, 16)
            sp.dma_start(W[:, 4:12, :].rearrange("p (k a) c -> p k (a c)", k=KC),
                         W1.rearrange("(k p) c -> p k c", p=P)).then_inc(ld_w1, 16)
            w2v = W2.rearrange("(k p) c -> p k c", p=P)
            sp.dma_start(W[:, 12:16, :], w2v[:, 0:4, :]).then_inc(ld_w2a, 16)
            sp.wait_ge(tile_full, first["z2T0"])
            sp.dma_start(W[:, 0:4, :], w2v[:, 4:8, :]).then_inc(ld_w2b, 16)
            sp.wait_ge(z2_rows, NB)
            for s, v in ((5, l2_g), (6, l2_be), (7, l3_b)):
                sp.dma_start(VEC[:, s, :], v.rearrange("(o c) -> o c", o=1).to_broadcast([P, C])).then_inc(ld_vec3, 16)
            for a in range(2):
                sp.wait_ge(wt_stored[a], 48)

            def load_wt(layer, slots):
                for m, s in enumerate(slots):
                    sp.dma_start(W[:, s:s + 4, :], weights_t[2 * (layer - 1) + m].rearrange(
                        "(k p) c -> p k c", p=P)).then_inc(ld_l[layer - 1], 16)

            sp.wait_ge(tile_full, first["ff"])
            load_wt(1, (4, 8))
            sp.wait_ge(tile_full, first["ff"] + NB)
            load_wt(2, (12, 0))
            sp.wait_ge(tile_full, h_tile(1, NB - 1) + 1)
            load_wt(3, (4, 8))
            sp.wait_ge(x_rows, 2 * NB)
            for s, v in ((1, l3_g), (2, l3_be)):
                sp.dma_start(VEC[:, s, :], v.rearrange("(o c) -> o c", o=1).to_broadcast([P, C])).then_inc(ld_vec4, 16)
            ov = out.rearrange("(b p) c -> p b c", p=P)
            for lo, hi in ln_sizes("out3"):
                sp.wait_ge(x_rows, 3 * NB + hi)
                sp.dma_start(ov[:, lo:hi, :], X[:, lo:hi, :]).then_inc(stored, 16)
            sp.wait_ge(stored, 16 * len(ln_sizes("out3")))
            sp.wait_ge(filler_stored, 16)
            for a in range(2):
                sp.wait_ge(kv_stored[a], 16 * NB // 2)

        @block.gpsimd
        def _(pool):
            nc.gpsimd.memset(recs[:, :, :], 0.0).then_inc(consts, 1)
            nc.gpsimd.iota(iota_c[:, :], pattern=[[1, N]], base=0, channel_multiplier=0,
                           allow_small_or_imprecise_dtypes=True).then_inc(consts, 1)
            nc.gpsimd.iota(iota_pi[:, :], pattern=[[0, 1]], base=0, channel_multiplier=1).then_inc(consts, 1)
            nc.gpsimd.iota(iota_g[:, :], pattern=[[GE, NG]], base=0, channel_multiplier=0,
                           allow_small_or_imprecise_dtypes=True).then_inc(consts, 1)
            nc.gpsimd.memset(ones[:, :], 1.0).then_inc(consts, 1)
            pool.wait_ge(consts, 5)
            nc.gpsimd.memset(recs[:, :, 0:1], 1.0).then_inc(filler_made, 1)

            pool.wait_ge(rows_ready, 1)
            pool.wait_ge(attr_put, 1)
            pool.wait_ge(filler_stored, 16)

            def scatter_tiles(t0, a, k):
                nc.gpsimd.tensor_copy(stage_rec[:, a, :, :], rec_src[:, bass.ds(t0, 8), :]).then_inc(staged, 1)
                nc.gpsimd.tensor_copy(stage_row[:, a, :], row_i[:, bass.ds(t0, 8)]).then_inc(staged, 1)
                pool.wait_ge(staged, k)
                pool.sem_inc(pool_go, 1)
                for j in range(8):
                    nc.gpsimd.indirect_dma_start(
                        out=records[:, :], out_offset=bass.IndirectOffsetOnAxis(ap=stage_row[:, a, j:j + 1], axis=0),
                        in_=stage_rec[:, a, j, :], in_offset=None).then_inc(scat[a], 16)

            scatter_tiles(0, 0, 2)
            scatter_tiles(8, 1, 4)
            with pool.Fori(1, EPP // 16) as i:
                for a in range(2):
                    pool.wait_ge(scat[a], i * (16 * 8))
                    scatter_tiles(i * 16 + 8 * a, a, i * 4 + (2 * a + 2))

            pool.wait_ge(bmax_in, 1)
            nc.gpsimd.partition_all_reduce(bmax_all[:, :], bmax[:, :], P, bass.bass_isa.ReduceOp.max).then_inc(bmax_out, 1)
            for a in range(2):
                pool.wait_ge(wt_stored[a], 48)
            nc.gpsimd.memset(HR[:, :, :], 0.0).then_inc(acc_zero, 1)
            nc.gpsimd.memset(Lacc[:, :, :], 0.0).then_inc(acc_zero, 1)

            def gather(g, a, k, wait=True):
                if wait:
                    for j in range(GT):
                        pool.wait_ge(kv_in[a][j], (g - a) * 8)
                nc.gpsimd.tensor_copy(idx[:, a, :], dst_i[:, bass.ds(g * GT, GT)]).then_inc(idx_ready, 1)
                pool.wait_ge(idx_ready, k)
                pool.sem_inc(pool_go, 1)
                for j in range(GT):
                    if wait and j == 0:
                        pool.wait_ge(pv_made, g - 1)
                        pool.sem_inc(pool_go, 1)
                    if wait and j >= DVE_TILES:
                        pool.wait_ge(act_pv_made, (g - 2) * (GT - DVE_TILES) + (j - DVE_TILES + 1))
                        pool.sem_inc(pool_go, 1)
                    nc.gpsimd.indirect_dma_start(
                        out=kvr[a][:, j, :], out_offset=None, in_=kv_table[:, :],
                        in_offset=bass.IndirectOffsetOnAxis(ap=idx[:, a, j:j + 1], axis=0)).then_inc(kv_in[a][j], 16)

            for a in range(2):
                pool.wait_ge(kv_stored[a], 16 * NB // 2)
            pool.wait_ge(recs_int, 1)
            gather(0, 0, 1, wait=False)
            pool.wait_ge(smm, NB * H)
            gather(1, 1, 2, wait=False)
            with pool.Fori(2, NG - 1, 2) as g:
                for a in range(2):
                    gather(g + a, a, g + (a + 1))

            pool.wait_ge(rc_made, 1)
            for b in range(NB):
                last = nc.gpsimd.tensor_tensor(CT[:, b, :], CT[:, b, :], inv_degree[:, :], ALU.mult)
            last.then_inc(cn_ready, 1)
            pool.wait_ge(ld_vec4, 32)
            pool.wait_ge(tile_full, h_tile(3, 0) + 1)
            for b in range(NB):
                nc.gpsimd.tensor_tensor(X[:, b, :], X[:, b, :], VEC[:, 2, :], ALU.add).then_inc(x_biased, 1)

        @block.scalar
        def _(act):
            act.wait_ge(ld_edges, 48)
            nc.scalar.copy(rec_src[:, :, 2:RW], attr.rearrange("p (t h) -> p t h", h=H)).then_inc(attr_put, 1)
            roots = [0]

            def root(lo, hi):
                roots[0] += 1
                act.wait_ge(ln_var, roots[0])
                nc.scalar.activation(std[:, lo:hi], var_e[:, lo:hi], ACT.Sqrt).then_inc(ln_std, 1)

            def drain(n, dest, func=None, **kw):
                act.wait_ge(tile_full, n + 1)
                if func is None:
                    nc.scalar.copy(dest, ps[:, n % NBANK, :]).then_inc(act_drained, 1)
                else:
                    nc.scalar.activation(dest, ps[:, n % NBANK, :], func, **kw).then_inc(act_drained, 1)

            def drain_T(name, dest):
                for m in range(2 * KC):
                    half, k = m // KC, m % KC
                    drain(first[name] + m, dest[:, k, half * HALF:(half + 1) * HALF])

            def drain_weights(lo, hi):
                for m in range(lo, hi):
                    if m >= 8 and m % 4 == 0:
                        act.wait_ge(wt_stored[m // 4 % 2], 16 * (m // 8))
                    drain(wt_tile(m), wtr[m // 4 % 2][:, m % 4, :])

            drain_weights(0, 8)
            root(0, NB // 2)
            drain_weights(8, 12)
            root(NB // 2, NB)
            drain_T("zT", TR)
            drain_weights(12, 16)

            def drain_block_T(name, dest):
                for b in range(NB):
                    n = first[f"{name}{b}"]
                    act.wait_ge(tile_full, n + 1)
                    nc.scalar.copy(dest[:, :, b * P:(b + 1) * P],
                                   ps[:, n % NBANK, :].rearrange("p (k n) -> p k n", k=KC)).then_inc(act_drained, 1)

            drain_block_T("KT", KTr)
            drain_weights(16, 24)
            drain_block_T("QT", QT)

            def distances(g, done, used, at=None):
                if used is not None:
                    act.wait_ge(used, g)
                tiles = recs[:, bass.ds((g if at is None else at) * GT, GT), :]
                for j in range(GT):
                    last = nc.scalar.activation(dist[:, j, :], iota_c[:, 0:P], ACT.Abs, bias=tiles[:, j, 0:1], scale=1.0)
                last.then_inc(done, 1)
                act.wait_ge(done, g + 1)

            act.wait_ge(dve_drained, drains(first[f"Q{NB - 1}"]))

            def count_sources(g, a, wait=True, late=True):
                at = act.value_load(order_i[0:1, bass.ds(g, 1)], min_val=0, max_val=NG - 1)
                act.wait_ge(group_in[a], kv_count(g, a))
                distances(g, csrc_dist, csrc_oh if late else None, at)
                if wait:
                    act.wait_ge(cmm, g - 1)
                nc.scalar.activation(oh_b[:, a, :, :], dist[:, :, :], ACT.Relu, bias=1.0, scale=-1.0).then_inc(csrc_oh, 1)

            count_sources(0, 0, wait=False, late=False)
            count_sources(1, 1, wait=False)
            with act.Fori(2, NG - 1, 2) as g:
                for a in range(2):
                    count_sources(g + a, a)

            def edge_sources(g, a, wait=True, head=False):
                distances(g, src_dist, None if head else oh_made)
                if wait:
                    act.wait_ge(ohf_made, g - 1)
                nc.scalar.activation(oh_b[:, a, :, :], dist[:, :, :], ACT.Relu, bias=1.0, scale=-1.0).then_inc(oh_made, 1)

            def sources_f(g, a, wait=True):
                if wait:
                    act.wait_ge(agg_done, g - 1)
                nc.scalar.copy(oh_f[:, a, :, :], oh_b[:, a, :, :]).then_inc(ohf_made, 1)

            def onehots(g, a):
                act.wait_ge(ohT_ps, g + 1)
                nc.scalar.copy(ohT[:, a, :, :], psb[:, 0:GE].rearrange("p (j n) -> p j n", j=GT)).then_inc(ohT_sb, 1)

            def exps(g, a):
                act.wait_ge(z_made, g + 1)
                nc.scalar.activation(prob[:, a, :, :].rearrange("p j h -> p (j h)"), zsc[:, a, :],
                                     ACT.Exp).then_inc(p_made, 1)

            def act_values(g, a):
                act.wait_ge(p_made, g + 1)
                for j in range(DVE_TILES, GT):
                    for h in range(H):
                        last = nc.scalar.activation(pv[a][:, j, h * D:(h + 1) * D], kvr[a][:, j, C + h * D:C + (h + 1) * D],
                                                    ACT.Copy, scale=prob[:, a, j, h:h + 1])
                    last.then_inc(act_pv_made, 1)

            act.wait_ge(cmm, NG)
            act.wait_ge(csrc_oh, NG)
            edge_sources(0, 0, wait=False, head=True)
            edge_sources(1, 1, wait=False)
            onehots(0, 0)

            def edge_step(g, a, wait=True, copies=True, sources=True):
                if copies:
                    onehots(g + 1, 1 - a)
                sources_f(g, a, wait)
                if sources:
                    edge_sources(g + 2, a)
                exps(g, a)
                act_values(g, a)

            edge_step(0, 0, wait=False)
            edge_step(1, 1, wait=False)
            with act.Fori(2, NG - 3, 2) as g:
                for a in range(2):
                    edge_step(g + a, a)
            edge_step(NG - 2, 0, sources=False)
            edge_step(NG - 1, 1, copies=False, sources=False)

            act.wait_ge(cn_ready, 1)
            drain_T("oT", TR)
            root(0, NB // 2)
            for half in range(2):
                cols = slice(half * HALF, (half + 1) * HALF)
                for k in range(KC):
                    drain(first[f"z2T{half}"] + k, TR[:, k, cols])
                if half == 0:
                    root(NB // 2, NB)
                for k in range(HC):
                    drain(first[f"hidT{half}"] + k, hidT[:, k, cols], ACT.Silu, bias=b1_col[:, k:k + 1])
            for lo, hi in ln_sizes("out"):
                root(lo, hi)
            for layer in (1, 2, 3):
                drain_T(f"aggT{layer}", TR)
                drain_T(f"xT{layer}", XT)
                if layer == 2:
                    for b in range(NB):
                        act.wait_ge(centred, b + 1)
                        nc.scalar.activation(SQ[:, b, :], HR[:, b, :], ACT.Square).then_inc(squared, 1)
                    act.wait_ge(bn_var, 1)
                    nc.scalar.activation(PR[:, 512:1024], PR[:, 0:512], ACT.Sqrt).then_inc(bn_std, 1)
                    for lo, hi in ln_sizes("out2"):
                        root(lo, hi)
                else:
                    for lo, hi in ln_sizes(f"out{layer}"):
                        root(lo, hi)
                        root(lo, hi)

        @block.vector
        def _(dve):
            chain = [0]

            def link(ins):
                chain[0] += 1
                ins.then_inc(dve_chain, 1)
                dve.wait_ge(dve_chain, chain[0])

            vec = nc.vector
            dve.wait_ge(consts, 5)
            link(vec.tensor_copy(iota_p[:, :], iota_pi[:, :]))
            vec.tensor_scalar(ident[:, :], iota_c[:, 0:P], iota_p[:, 0:1], None, ALU.is_equal)
            vec.tensor_scalar(ident_b[:, :], iota_c[:, 0:P], iota_p[:, 0:1], None, ALU.is_equal)
            vec.tensor_scalar(ones_b, iota_c[:, 0:P], 0.0, None, ALU.is_ge)
            vec.tensor_scalar(upto_b, iota_c[:, 0:P], iota_p[:, 0:1], -1.0, ALU.is_le, ALU.mult).then_inc(dve_consts, 1)

            dve.wait_ge(ld_edges, 48)
            srcf = pick[:, 0, :]
            blkf = pick[:, 1, :]
            vec.tensor_copy(rec_src[:, :, 1:2].rearrange("p t o -> p (t o)"), blk_i[:, :])
            link(vec.tensor_copy(srcf, src_i[:, :]))
            link(vec.tensor_scalar(blk_i[:, :], src_i[:, :], 7, None, ALU.arith_shift_right))
            link(vec.tensor_copy(blkf, blk_i[:, :]))
            link(vec.scalar_tensor_tensor(rec_src[:, :, 0:1].rearrange("p t o -> p (t o)"), blkf, float(P), srcf,
                                          ALU.mult, ALU.subtract))
            for b in range(NB):
                last = vec.tensor_scalar(oh8[:, b, :], blkf, float(b), None, ALU.is_equal)
            link(last)
            dve.sem_inc(sort_n, 1)
            dve.wait_ge(sort_mm, 1)
            totals = ps[:, 0:4, :].rearrange("p a c -> p (a c)")
            last8, prev8, n8, tot8, end8, base8, off8 = (small[:, i, :] for i in range(7))
            link(vec.memset(small[:, 7, 0:1], 0.0))
            link(vec.tensor_tensor_scan(cum_f, small[:, 7, 0:1].to_broadcast([P, NB * EPP]), totals, 0.0,
                                        ALU.add, ALU.add))
            link(vec.tensor_copy(last8, cum[:, :, EPP - 1:EPP].rearrange("p b o -> p (b o)")))
            vec.memset(prev8[:, 0:1], 0.0)
            link(vec.tensor_copy(prev8[:, 1:8], last8[:, 0:7]))
            link(vec.tensor_tensor(n8, last8, prev8, ALU.subtract))
            link(vec.tensor_scalar(tot8, n8, float(GE - 1), None, ALU.add))
            link(vec.tensor_copy(pad_i[:, :], tot8))
            link(vec.tensor_scalar(pad_i[:, :], pad_i[:, :], -GE, None, ALU.bitwise_and))
            link(vec.tensor_copy(tot8, pad_i[:, :]))
            link(vec.tensor_tensor_scan(end8, tot8, tot8, 0.0, ALU.add, ALU.max))
            link(vec.tensor_tensor(base8, end8, tot8, ALU.subtract))
            link(vec.tensor_tensor(off8, base8, prev8, ALU.subtract))
            dve.wait_ge(sort_mm, 2)
            link(vec.tensor_tensor(pick_f, ps[:, 4:8, :].rearrange("p a c -> p (a c)"), cum_f, ALU.add))
            for b in range(NB):
                last = vec.scalar_tensor_tensor(pick[:, b, :], pick[:, b, :], off8[:, b:b + 1], oh8[:, b, :],
                                                ALU.add, ALU.mult)
            link(last)
            slot, tif, ppf = (ctf[:, 3072 + i * EPP:3072 + (i + 1) * EPP] for i in range(3))
            link(vec.tensor_reduce(slot, pick.rearrange("p b t -> p t b"), AX.X, ALU.add))
            link(vec.tensor_copy(row_i[:, :], slot))
            link(vec.tensor_scalar(blk_i[:, :], row_i[:, :], 7, None, ALU.arith_shift_right))
            link(vec.tensor_copy(tif, blk_i[:, :]))
            link(vec.tensor_scalar(blk_i[:, :], row_i[:, :], P - 1, None, ALU.bitwise_and))
            link(vec.tensor_copy(ppf, blk_i[:, :]))
            link(vec.scalar_tensor_tensor(ppf, ppf, float(NT), tif, ALU.mult, ALU.add))
            vec.tensor_copy(row_i[:, :], ppf).then_inc(rows_ready, 1)
            roots = [0]

            def ln_stats(source, lo, hi):
                for b in range(lo, hi):
                    last = vec.bn_stats(stats[:, b, :], source[:, b, :])
                link(last)
                for b in range(lo, hi):
                    last = vec.bn_aggr(mv[:, b, :], stats[:, b, :])
                link(last)
                roots[0] += 1
                vec.tensor_scalar(var_e[:, lo:hi], mv[:, lo:hi, 1:2].rearrange("p b o -> p (b o)"), EPS, None,
                                  ALU.add).then_inc(ln_var, 1)
                dve.wait_ge(ln_std, roots[0])
                link(vec.reciprocal(rstd[:, lo:hi], std[:, lo:hi]))

            def ln_apply(dest, source, b):
                return vec.tensor_scalar(dest[:, b, :], source[:, b, :], mv[:, b, 0:1], rstd[:, b:b + 1],
                                         ALU.subtract, ALU.mult)

            def phased(lo, hi, *steps):
                for step in steps[:-1]:
                    for b in range(lo, hi):
                        last = step(b)
                    link(last)
                return steps[-1]

            dve.wait_ge(ld_x, 16)
            dve.wait_ge(ld_vec, 96)
            for lo, hi in ln_sizes("ln1"):
                ln_stats(X, lo, hi)
                last_step = phased(lo, hi,
                                   lambda b: ln_apply(Z, X, b),
                                   lambda b: vec.tensor_tensor(Z[:, b, :], Z[:, b, :], VEC[:, 0, :], ALU.mult),
                                   lambda b: vec.tensor_tensor(Z[:, b, :], Z[:, b, :], VEC[:, 1, :], ALU.add))
                for b in range(lo, hi):
                    last_step(b).then_inc(z_rows, 1)

            vec.tensor_reduce(bmax[:, :], attr.rearrange("p (t h) -> p h t", h=H), AX.X, ALU.max).then_inc(bmax_in, 1)
            link(vec.tensor_scalar(gblk[:, :], iota_g[:, :], end8[:, 0:1], None, ALU.is_ge))
            for b in range(1, NB - 1):
                link(vec.scalar_tensor_tensor(gblk[:, :], iota_g[:, :], end8[:, b:b + 1], gblk[:, :],
                                              ALU.is_ge, ALU.add))
            vec.tensor_copy(gblk_i[:, :], gblk[:, :]).then_inc(gtab, 1)

            dve.wait_ge(attr_put, 1)
            full, step_f = ctf[:, 0:2048], ctf[:, 2048:4096]
            full_bt = full.rearrange("p (b t) -> p b t", b=NB)
            step_tb = step_f.rearrange("p (t b) -> p t b", b=NB)
            zero, one_up, g0, fe8 = small[:, 7, 0:1], small[:, 8, 0:1], small[:, 9, :], small[:, 10, :]
            ord1, ord2 = small[:, 11, 0:1], small[:, 12, 0:1]
            vec.tensor_scalar(one_up, iota_p[:, :], 1.0, None, ALU.add)
            vec.tensor_scalar(g0, base8, 1.0 / GE, -1.0, ALU.mult, ALU.add)
            link(vec.tensor_tensor(full_bt, cum, prev8.unsqueeze(2).to_broadcast([P, NB, EPP]), ALU.subtract))
            link(vec.tensor_copy(step_f.bitcast(i32), full))
            link(vec.tensor_scalar(step_f.bitcast(i32), step_f.bitcast(i32), GE.bit_length() - 1, None,
                                   ALU.arith_shift_right))
            link(vec.tensor_copy(full, step_f.bitcast(i32)))
            link(vec.scalar_tensor_tensor(fe8, full_bt[:, :, EPP - 1:EPP].rearrange("p b o -> p (b o)"), float(GE),
                                          base8, ALU.mult, ALU.add))
            vec.memset(step_tb[:, 0:1, :], 0.0)
            link(vec.tensor_tensor(step_tb.rearrange("p t b -> p b t")[:, :, 1:EPP], full_bt[:, :, 1:EPP],
                                   full_bt[:, :, 0:EPP - 1], ALU.subtract))
            link(vec.tensor_tensor_scan(pick_f, zero.to_broadcast([P, NB * EPP]), step_f, 0.0, ALU.add, ALU.add))
            link(vec.tensor_tensor(full_bt, full_bt, g0.unsqueeze(2).to_broadcast([P, NB, EPP]), ALU.add))
            link(vec.tensor_tensor(cum_f.rearrange("p (t b) -> p t b", b=NB), full_bt.rearrange("p b t -> p t b"),
                                   step_tb, ALU.mult))
            link(vec.tensor_scalar(full, pick_f, one_up, None, ALU.is_equal))
            link(vec.tensor_tensor_reduce(out=step_f, in0=full, in1=cum_f, scale=1.0, scalar=0.0, op0=ALU.mult,
                                          op1=ALU.add, accum_out=ord1))
            rest, place, number = (ctf[:, i * NG:(i + 1) * NG] for i in range(3))
            link(vec.tensor_scalar(rest, iota_g[:, :], base8[:, 0:1], -float(NB - 1), ALU.is_lt, ALU.add))
            for b in range(1, NB):
                link(vec.scalar_tensor_tensor(rest, iota_g[:, :], base8[:, b:b + 1], rest, ALU.is_lt, ALU.add))
            for b in range(NB):
                link(vec.scalar_tensor_tensor(rest, iota_g[:, :], fe8[:, b:b + 1], rest, ALU.is_ge, ALU.add))
            link(vec.tensor_tensor_scan(place, zero.to_broadcast([P, NG]), rest, 0.0, ALU.add, ALU.add))
            link(vec.tensor_scalar(place, place, pick_f[:, NB * EPP - 1:NB * EPP], one_up, ALU.add, ALU.is_equal))
            link(vec.scalar_tensor_tensor(number, iota_g[:, :], 1.0 / GE, rest, ALU.mult, ALU.mult))
            link(vec.tensor_tensor_reduce(out=rest, in0=place, in1=number, scale=1.0, scalar=0.0, op0=ALU.mult,
                                          op1=ALU.add, accum_out=ord2))
            link(vec.tensor_tensor(ord1, ord1, ord2, ALU.add))
            link(vec.tensor_scalar(ord2, ord1, float(GE), None, ALU.mult))
            blk1 = small[:, 13, 0:1]
            link(vec.tensor_scalar(blk1, ord2, end8[:, 0:1], None, ALU.is_ge))
            for b in range(1, NB - 1):
                last = vec.scalar_tensor_tensor(blk1, ord2, end8[:, b:b + 1], blk1, ALU.is_ge, ALU.add)
                if b < NB - 2:
                    link(last)
            last.then_inc(order_made, 1)
            for b in range(NB):
                if b >= 2:
                    dve.wait_ge(kv_stored[b % 2], 16 * (b // 2))
                    dve.wait_ge(tile_full, first[f"KT{b - 2}"] + 1)
                for v, name in enumerate("KV"):
                    n = first[f"{name}{b}"]
                    dve.wait_ge(tile_full, n + 1)
                    vec.tensor_tensor(kvst[:, b % 2, v * C:(v + 1) * C], ps[:, n % NBANK, :], VEC[:, 2 + v, :],
                                      ALU.add).then_inc(dve_drained, 1)
                link(vec.memset(CT[:, b, :], 0.0))
            n = first["order"]
            dve.wait_ge(tile_full, n + 1)
            vec.tensor_copy(order_i[:, :], ps[0:1, n % NBANK, 0:2 * NG]).then_inc(dve_drained, 1)
            dve.wait_ge(filler_stored, 16)
            for b in range(NB):
                n = first[f"Q{b}"]
                q, rest1, rest2 = (tmpq[:, i * C:(i + 1) * C] for i in (b % 2, 2, 3))
                if b >= 2:
                    dve.wait_ge(tile_full, first[f"QT{b - 2}"] + 1)
                dve.wait_ge(tile_full, n + 1)
                vec.tensor_tensor(q, ps[:, n % NBANK, :], VEC[:, 4, :], ALU.add).then_inc(dve_drained, 1)
                dve.wait_ge(dve_drained, drains(n))
                vec.tensor_scalar(q, q, float(D) ** -0.5, None, ALU.mult).then_inc(q_scaled, 1)
                dve.wait_ge(q_scaled, b + 1)
                link(vec.tensor_copy(Qs[:, 0, b, :], q))
                link(vec.tensor_tensor(rest1, q, Qs[:, 0, b, :], ALU.subtract))
                link(vec.tensor_copy(Qs[:, 1, b, :], rest1))
                link(vec.tensor_tensor(rest2, rest1, Qs[:, 1, b, :], ALU.subtract))
                link(vec.tensor_copy(Qs[:, 2, b, :], rest2))
                dve.sem_inc(q_split, 1)

            dve.wait_ge(gtab, 1)
            for a in range(2):
                dve.wait_ge(kv_stored[a], 16 * NB // 2)

            def count_onehots(g, a, wait=True):
                if wait:
                    dve.wait_ge(cmm, g - 1)
                at = dve.value_load(order_i[0:1, bass.ds(g, 1)], min_val=0, max_val=NG - 1)
                dve.wait_ge(group_in[a], kv_count(g, a))
                tiles = recs[:, bass.ds(at * GT, GT), :]
                for j in range(GT):
                    last = vec.tensor_scalar(ohd[a][:, j, :], iota_c[:, :], tiles[:, j, 1:2], None, ALU.is_equal)
                last.then_inc(coh, 1)

            def count_flush(g, a, wait=True):
                at = dve.value_load(order_i[0:1, bass.ds(g + NG, 1)], min_val=0, max_val=NB - 1)
                dve.wait_ge(cmm, g + 1)
                if wait:
                    dve.wait_ge(cflush, g)
                vec.tensor_tensor(CT[:, at, :], CT[:, at, :],
                                  ps[:, 2 * a:2 * a + 2, :].rearrange("p a c -> p (a c)"), ALU.add).then_inc(cflush, 1)

            count_onehots(0, 0, wait=False)
            count_onehots(1, 1, wait=False)
            count_flush(0, 0, wait=False)
            with dve.Fori(1, NG - 2, 2) as g:
                for a in range(2):
                    count_onehots(g + (a + 1), a)
                    count_flush(g + a, 1 - a)
            count_flush(NG - 1, 1)
            dve.wait_ge(cflush, NG)
            dve.sem_inc(ct_ready, 1)
            vec.tensor_copy(dst_i[:, :], recs[:, :, 1:2].rearrange("p t o -> p (t o)")).then_inc(recs_int, 1)

            for b in range(NB):
                if b >= 2:
                    dve.wait_ge(smax, H * (b - 1))
                link(vec.tensor_scalar(mask[:, b % 2, :], CT[:, b, :], 0.0, NEG, ALU.is_equal, ALU.mult))
                for h in range(H):
                    m = b * H + h
                    dve.wait_ge(smm, m + 1)
                    if m >= 2:
                        dve.wait_ge(smax, m - 1)
                    bank = 2 * (m % 3)
                    vec.tensor_tensor_reduce(out=PV[:, (m % 2) * N:(m % 2 + 1) * N], in0=ps[:, bank:bank + 2, :].rearrange("p a c -> p (a c)"),
                                             in1=mask[:, b % 2, :], scale=1.0, scalar=4 * NEG, op0=ALU.add,
                                             op1=ALU.max, accum_out=cmax[:, b, h:h + 1]).then_inc(smax, 1)
            dve.wait_ge(smax, NB * H)
            dve.wait_ge(deg_full, 1)
            vec.tensor_scalar(inv_degree, ps[:, 6:8, :].rearrange("p a c -> p (a c)"), 1.0, None,
                              ALU.max).then_inc(degree_put, 1)
            dve.wait_ge(bmax_out, 1)
            for b in range(NB):
                last = vec.tensor_tensor(shift[:, b, :], cmax[:, b, :], bmax_all[:, :], ALU.add)
            last.then_inc(shift_ready, 1)
            dve.wait_ge(degree_put, 1)
            vec.reciprocal(inv_degree, inv_degree).then_inc(rc_made, 1)

            def edge_scores(g, a, wait=True):
                for half in range(2):
                    dve.wait_ge(q_ps, g * 2 + (half + 1))
                    for j in (2 * half, 2 * half + 1):
                        dve.wait_ge(kv_in[a][j], kv_count(g, a))
                    if wait and half == 0:
                        dve.wait_ge(summed, g)
                    vec.tensor_tensor(prod[:, 2 * half:2 * half + 2, :], ps[:, 2 * half:2 * half + 2, :],
                                      kvr[a][:, 2 * half:2 * half + 2, 0:C], ALU.mult).then_inc(prod_done, 1)
                dve.wait_ge(prod_done, g * 2 + 2)
                vec.tensor_reduce(score[:, a, :], prod_h, AX.X, ALU.add).then_inc(summed, 1)
                dve.wait_ge(summed, g + 1)
                tiles = recs[:, bass.ds(g * GT, GT), :]
                vec.tensor_tensor(score[:, a, :].rearrange("p (j h) -> p j h", j=GT),
                                  score[:, a, :].rearrange("p (j h) -> p j h", j=GT),
                                  tiles[:, :, 2:RW], ALU.add).then_inc(biased, 1)
                dve.wait_ge(biased, g + 1)
                dve.wait_ge(c_ps, g + 1)
                vec.tensor_tensor(zsc[:, a, :], score[:, a, :], shift_ps, ALU.subtract).then_inc(z_made, 1)

            def block_of(g):
                return dve.value_load(gblk_i[0:1, bass.ds(g, 1)], min_val=0, max_val=NB - 1)

            def edge_flush(g, a, at, wait=True):
                dve.wait_ge(agg_done, g + 1)
                if wait:
                    dve.wait_ge(flushed, g)
                    dve.wait_ge(l_flushed, g)
                vec.tensor_tensor(Lacc[:, at, :], Lacc[:, at, :], psum_ps, ALU.add).then_inc(l_flushed, 1)
                vec.tensor_tensor(HR[:, at, :], HR[:, at, :], sums_ps, ALU.add).then_inc(flushed, 1)

            def edge_values(g, a):
                dve.wait_ge(p_made, g + 1)
                n = DVE_TILES
                vec.tensor_tensor(pv[a][:, 0:n, :].rearrange("p j (h d) -> p j h d", d=D),
                                  kvr[a][:, 0:n, C:2 * C].rearrange("p j (h d) -> p j h d", d=D),
                                  prob[:, a, 0:n, :].unsqueeze(3).to_broadcast([P, n, H, D]), ALU.mult).then_inc(pv_made, 1)

            dve.wait_ge(acc_zero, 2)
            at = block_of(0)
            edge_scores(0, 0, wait=False)
            edge_values(0, 0)
            edge_scores(1, 1)
            edge_values(1, 1)
            edge_flush(0, 0, at, wait=False)
            with dve.Fori(2, NG - 1, 2) as g:
                for a in range(2):
                    at = block_of(g + (a - 1))
                    edge_scores(g + a, a)
                    edge_flush(g + (a - 1), 1 - a, at)
                    edge_values(g + a, a)
            edge_flush(NG - 1, 1, block_of(NG - 1))
            dve.wait_ge(flushed, NG)
            dve.wait_ge(l_flushed, NG)

            rl = cmax
            link(vec.tensor_scalar(rl[:, :, :], Lacc[:, :, :], 1.0e-37, None, ALU.max))
            link(vec.reciprocal(rl[:, :, :], rl[:, :, :]))
            for b in range(NB):
                o = HR[:, b, :].rearrange("p (h d) -> p h d", d=D)
                vec.tensor_tensor(o, o, rl[:, b, :].unsqueeze(2).to_broadcast([P, H, D]), ALU.mult).then_inc(onorm, 1)
            dve.wait_ge(ld_vec2, 128)
            for lo, hi in ln_sizes("z2"):
                for b in range(lo, hi):
                    n = first["wo"] + b
                    dve.wait_ge(tile_full, n + 1)
                    last = vec.tensor_tensor(HR[:, b, :], ps[:, n % NBANK, :], X[:, b, :], ALU.add)
                    last.then_inc(dve_drained, 1)
                dve.wait_ge(dve_drained, drains(first["wo"] + hi - 1))
                for b in range(lo, hi):
                    last = vec.tensor_tensor(HR[:, b, :], HR[:, b, :], VEC[:, 5, :], ALU.add)
                link(last)
                ln_stats(HR, lo, hi)
                zh = z2[lo // 4]
                step = phased(lo, hi,
                              lambda b: vec.tensor_scalar(zh[:, b % 4, :], HR[:, b, :], mv[:, b, 0:1], rstd[:, b:b + 1],
                                                          ALU.subtract, ALU.mult),
                              lambda b: vec.tensor_tensor(zh[:, b % 4, :], zh[:, b % 4, :], VEC[:, 6, :], ALU.mult),
                              lambda b: vec.tensor_tensor(zh[:, b % 4, :], zh[:, b % 4, :], VEC[:, 7, :], ALU.add))
                for b in range(lo, hi):
                    step(b).then_inc(z2_rows, 1)
            for b in range(NB):
                last = vec.tensor_tensor(X[:, b, :], X[:, b, :], HR[:, b, :], ALU.add)
            link(last)
            for b in range(NB):
                last = vec.tensor_tensor(X[:, b, :], X[:, b, :], VEC[:, 0, :], ALU.add)
            link(last)
            for lo, hi in ln_sizes("out"):
                for b in range(lo, hi):
                    n = first["ff"] + b
                    dve.wait_ge(tile_full, n + 1)
                    last = vec.tensor_tensor(HR[:, b, :], ps[:, n % NBANK, :], X[:, b, :], ALU.add)
                    last.then_inc(dve_drained, 1)
                dve.wait_ge(dve_drained, drains(first["ff"] + hi - 1))
                ln_stats(HR, lo, hi)
                for b in range(lo, hi):
                    ln_apply(X, HR, b).then_inc(x_rows, 1)

            def gain_relu_add(v_g, v_b, relu, pre):
                steps = list(pre)
                steps.append(lambda b: vec.tensor_tensor(HR[:, b, :], HR[:, b, :], v_g, ALU.mult))
                if v_b is not None:
                    steps.append(lambda b: vec.tensor_tensor(HR[:, b, :], HR[:, b, :], v_b, ALU.add))
                if relu:
                    steps.append(lambda b: vec.scalar_tensor_tensor(HR[:, b, :], HR[:, b, :], 0.0, X[:, b, :],
                                                                    ALU.max, ALU.add))
                else:
                    steps.append(lambda b: vec.tensor_tensor(HR[:, b, :], HR[:, b, :], X[:, b, :], ALU.add))
                return steps

            def whole(lo, hi, steps):
                for step in steps:
                    for b in range(lo, hi):
                        last = step(b)
                    link(last)

            def take_h(layer, lo, hi, v_bias):
                for b in range(lo, hi):
                    n = h_tile(layer, b)
                    dve.wait_ge(tile_full, n + 1)
                    vec.tensor_tensor(HR[:, b, :], ps[:, n % NBANK, :], v_bias, ALU.add).then_inc(dve_drained, 1)
                dve.wait_ge(dve_drained, drains(h_tile(layer, hi - 1)))

            def finish(lo, hi):
                ln_stats(HR, lo, hi)
                for b in range(lo, hi):
                    ln_apply(X, HR, b).then_inc(x_rows, 1)

            def ln_layer(layer, v_bias, v_g, v_b, relu):
                for lo, hi in ln_sizes(f"out{layer}"):
                    take_h(layer, lo, hi, v_bias)
                    ln_stats(HR, lo, hi)
                    if layer == 3:
                        dve.wait_ge(x_biased, hi)
                    whole(lo, hi, gain_relu_add(v_g, v_b, relu, [lambda b: ln_apply(HR, HR, b)]))
                    finish(lo, hi)

            ln_layer(1, VEC[:, 1, :], VEC[:, 2, :], VEC[:, 3, :], True)

            dve.wait_ge(ld_vec3, 48)
            take_h(2, 0, NB, VEC[:, 4, :])
            dve.wait_ge(bn_sums, 1)
            vec.tensor_scalar(PR[:, 0:C], ps[:, first["bn_mean"] % NBANK, :], 1.0 / N, None,
                              ALU.mult).then_inc(mean_drained, 1)
            dve.wait_ge(mean_drained, 1)
            for b in range(NB):
                vec.tensor_tensor(HR[:, b, :], HR[:, b, :], PR[:, 0:C], ALU.subtract).then_inc(centred, 1)
            dve.wait_ge(centred, NB)
            n = first["bn_var"]
            dve.wait_ge(tile_full, n + 1)
            vec.tensor_scalar(PR[:, 0:C], ps[:, n % NBANK, :], 1.0 / N, EPS, ALU.mult, ALU.add).then_inc(dve_drained, 1)
            dve.wait_ge(dve_drained, drains(n))
            dve.sem_inc(bn_var, 1)
            dve.wait_ge(bn_std, 1)
            link(vec.reciprocal(PR[:, 0:C], PR[:, C:2 * C]))
            link(vec.tensor_tensor(PR[:, 0:C], PR[:, 0:C], VEC[:, 5, :], ALU.mult))
            for lo, hi in ln_sizes("out2"):
                whole(lo, hi, gain_relu_add(PR[:, 0:C], VEC[:, 6, :], True, []))
                finish(lo, hi)

            dve.wait_ge(ld_vec4, 32)
            ln_layer(3, VEC[:, 7, :], VEC[:, 1, :], None, False)

        @block.tensor
        def _(pe):
            mm = nc.tensor.matmul

            def free_bank(n):
                if n >= NBANK:
                    pe.wait_ge(drained(n - NBANK), drains(n - NBANK))
                return ps[:, n % NBANK, :]

            def transposes_half(n0, source, rows, count):
                pe.wait_ge(rows, count)
                for k in range(KC):
                    bank = free_bank(n0 + k)
                    for j in range(4):
                        last = nc.tensor.transpose(bank[:, j * P:(j + 1) * P], source[:, j, k * P:(k + 1) * P],
                                                   ident[:, :])
                    last.then_inc(tile_full, 1)

            def transposes(name, source, rows, per):
                for half in range(2):
                    transposes_half(first[name] + half * KC, source[:, 4 * half:4 * half + 4, :], rows,
                                    per + (half + 1) * (NB // 2))

            pe.wait_ge(dve_consts, 1)
            pe.wait_ge(consts, 5)
            pe.wait_ge(sort_n, 1)
            for bank, m in ((0, ones_b), (4, upto_b)):
                for k in range(4):
                    last = mm(ps[:, bank + k, :], m, oh8[:, 2 * k:2 * k + 2, :].rearrange("p b t -> p (b t)"),
                              start=True, stop=True)
                last.then_inc(sort_mm, 1)

            pe.wait_ge(rows_ready, 1)

            def weight_transposes(lo, hi):
                for m in range(lo, hi):
                    pe.wait_ge(wt_loaded[m // 4 % 2], 16 * (m // 8 + 1))
                    bank = free_bank(wt_tile(m))
                    for j in range(4):
                        last = nc.tensor.transpose(bank[:, j * P:(j + 1) * P],
                                                   wnat[m // 4 % 2][:, j, (m % 4) * P:(m % 4 + 1) * P], ident[:, :])
                    last.then_inc(tile_full, 1)

            weight_transposes(0, 12)

            transposes("zT", Z, z_rows, 0)
            weight_transposes(12, 16)
            pe.wait_ge(ld_w, 48)

            def block_transpose(n, rows):
                bank = free_bank(n)
                for k in range(KC):
                    last = nc.tensor.transpose(bank[:, k * P:(k + 1) * P], rows[:, k * P:(k + 1) * P], ident[:, :])
                last.then_inc(tile_full, 1)

            for b in range(NB + KT_LAG):
                if b < NB:
                    pe.wait_ge(act_drained, drains(first["zT"] + KC * (b // 4) + KC - 1))
                    for name, w0 in (("K", 4), ("V", 8)):
                        bank = free_bank(first[f"{name}{b}"])
                        for k in range(KC):
                            last = mm(bank, TR[:, k, b * P:(b + 1) * P], W[:, w0 + k, :], start=k == 0, stop=k == KC - 1)
                        last.then_inc(tile_full, 1)
                if b >= KT_LAG:
                    at = b - KT_LAG
                    pe.wait_ge(dve_drained, drains(first[f"K{at}"]))
                    block_transpose(first[f"KT{at}"], kvst[:, at % 2, 0:C])
            weight_transposes(16, 24)
            pe.wait_ge(order_made, 1)
            bank = free_bank(first["order"])
            for i, column in enumerate((small[:, 11, 0:1], small[:, 13, 0:1])):
                last = mm(bank[0:1, i * NG:(i + 1) * NG], column, ident[:, 0:NG], start=True, stop=True)
            last.then_inc(tile_full, 1)
            for b in range(NB + 1):
                if b < NB:
                    bank = free_bank(first[f"Q{b}"])
                    for k in range(KC):
                        last = mm(bank, TR[:, k, b * P:(b + 1) * P], W[:, k, :], start=k == 0, stop=k == KC - 1)
                    last.then_inc(tile_full, 1)
                if b:
                    pe.wait_ge(q_scaled, b)
                    block_transpose(first[f"QT{b - 1}"], tmpq[:, (b - 1) % 2 * C:((b - 1) % 2 + 1) * C])
            pe.wait_ge(act_drained, drains(first[f"QT{NB - 1}"]))
            pe.wait_ge(dve_drained, drains(first[f"Q{NB - 1}"]))

            def count_mm(g, a, wait=True):
                pe.wait_ge(coh, g + 1)
                pe.wait_ge(csrc_oh, g + 1)
                if wait:
                    pe.wait_ge(cflush, g - 1)
                for j in range(GT):
                    for half in range(2):
                        last = mm(ps[:, 2 * a + half, :], oh_b[:, a, j, :], ohd[a][:, j, half * HALF:(half + 1) * HALF],
                                  start=j == 0, stop=j == GT - 1)
                last.then_inc(cmm, 1)

            count_mm(0, 0, wait=False)
            count_mm(1, 1, wait=False)
            with pe.Fori(2, NG - 1, 2) as g:
                for a in range(2):
                    count_mm(g + a, a)

            pe.wait_ge(ct_ready, 1)
            for b in range(NB):
                for h in range(H):
                    m = b * H + h
                    bank = 2 * (m % 3)
                    if m >= 3:
                        pe.wait_ge(smax, m - 2)
                    lo = D * (h % 2)
                    for half in range(2):
                        last = mm(ps[:, bank + half, :], QT[lo:lo + D, h // 2, b * P:(b + 1) * P],
                                  KTr[lo:lo + D, h // 2, half * HALF:(half + 1) * HALF], start=True, stop=True)
                    last.then_inc(smm, 1)
                    if h % 4 == 3:
                        k = h // 4
                        last = mm(ps[:, 6 + k, :], ones[:, :], CT[:, b, k * HALF:(k + 1) * HALF],
                                  start=b == 0, stop=b == NB - 1)
            last.then_inc(deg_full, 1)
            pe.wait_ge(shift_ready, 1)
            pe.wait_ge(q_split, NB)

            def edge_transposes(g, a, wait=True):
                pe.wait_ge(oh_made, g + 1)
                if wait:
                    pe.wait_ge(ohT_sb, g)
                for j in range(GT):
                    last = nc.tensor.transpose(psb[:, j * P:(j + 1) * P], oh_b[:, a, j, :], ident_b[:, :])
                last.then_inc(ohT_ps, 1)

            def edge_front(g, a, at, wait=True):
                pe.wait_ge(ohT_sb, g + 1)
                for half in range(2):
                    if wait:
                        pe.wait_ge(prod_done, g * 2 + (half - 1))
                    for j in (2 * half, 2 * half + 1):
                        for s in range(3):
                            last = mm(ps[:, j, :], ohT[:, a, j, :], Qs[:, s, at, :], start=s == 0, stop=s == 2)
                    last.then_inc(q_ps, 1)
                if wait:
                    pe.wait_ge(z_made, g)
                for j in range(GT):
                    last = mm(shift_ps[:, j * H:(j + 1) * H], ohT[:, a, j, :], shift[:, at, :], start=True, stop=True)
                last.then_inc(c_ps, 1)

            def edge_back(g, a, wait=True):
                pe.wait_ge(p_made, g + 1)
                if wait:
                    pe.wait_ge(l_flushed, g)
                    pe.wait_ge(flushed, g)
                for j in range(GT):
                    mm(psum_ps, oh_f[:, a, j, :], prob[:, a, j, :], start=j == 0, stop=j == GT - 1)
                for j in range(GT):
                    if j == 0:
                        pe.wait_ge(pv_made, g + 1)
                    if j >= DVE_TILES:
                        pe.wait_ge(act_pv_made, g * (GT - DVE_TILES) + (j - DVE_TILES + 1))
                    last = mm(sums_ps, oh_f[:, a, j, :], pv[a][:, j, :], start=j == 0, stop=j == GT - 1)
                last.then_inc(agg_done, 1)

            def block_of(g):
                return pe.value_load(gblk_i[0:1, bass.ds(g, 1)], min_val=0, max_val=NB - 1)

            pe.wait_ge(gtab, 1)
            edge_transposes(0, 0, wait=False)
            edge_front(0, 0, block_of(0), wait=False)
            edge_transposes(1, 1)
            edge_front(1, 1, block_of(1))
            edge_transposes(2, 0)
            edge_back(0, 0, wait=False)
            with pe.Fori(1, NG - 4, 2) as g:
                for a in range(2):
                    at = block_of(g + (a + 1))
                    edge_front(g + (a + 1), a, at)
                    edge_transposes(g + (a + 2), 1 - a)
                    edge_back(g + a, 1 - a)
            edge_front(NG - 2, 0, block_of(NG - 2))
            edge_transposes(NG - 1, 1)
            edge_back(NG - 3, 1)
            edge_front(NG - 1, 1, block_of(NG - 1))
            edge_back(NG - 2, 0)
            edge_back(NG - 1, 1)

            pe.wait_ge(flushed, NG)
            pe.wait_ge(l_flushed, NG)
            transposes("oT", HR, onorm, 0)
            pe.wait_ge(ld_wo, 16)
            for b in range(NB):
                n = first["wo"] + b
                pe.wait_ge(act_drained, drains(first["oT"] + KC * (b // 4) + KC - 1))
                bank = free_bank(n)
                for k in range(KC):
                    last = mm(bank, TR[:, k, b * P:(b + 1) * P], W[:, k, :], start=k == 0, stop=k == KC - 1)
                last.then_inc(tile_full, 1)
            pe.wait_ge(ld_w1, 16)
            w1 = W[:, 4:12, :].rearrange("p (k a) c -> p k (a c)", k=KC)
            for half in range(2):
                transposes_half(first[f"z2T{half}"], z2[half], z2_rows, (half + 1) * (NB // 2))
                pe.wait_ge(act_drained, drains(first[f"z2T{half}"] + KC - 1))
                for o in range(HC):
                    bank = free_bank(first[f"hidT{half}"] + o)
                    for k in range(KC):
                        last = mm(bank, w1[:, k, o * P:(o + 1) * P], TR[:, k, half * HALF:(half + 1) * HALF],
                                  start=k == 0, stop=k == KC - 1)
                    last.then_inc(tile_full, 1)
            pe.wait_ge(ld_w2a, 16)
            pe.wait_ge(ld_w2b, 16)
            for b in range(NB):
                n = first["ff"] + b
                pe.wait_ge(act_drained, drains(first[f"hidT{b // 4}"] + HC - 1))
                bank = free_bank(n)
                for k in range(HC):
                    last = mm(bank, hidT[:, k, b * P:(b + 1) * P], W[:, (12 + k) % 16, :], start=k == 0, stop=k == HC - 1)
                last.then_inc(tile_full, 1)

            pe.wait_ge(cn_ready, 1)
            for layer, (ws, wn) in ((1, (4, 8)), (2, (12, 0)), (3, (4, 8))):
                for lo in range(0, NB, 2):
                    pe.wait_ge(x_rows, (layer - 1) * NB + lo + 2)
                    for m in range(2 * KC):
                        n = first[f"aggT{layer}"] + m
                        bank = free_bank(n) if lo == 0 else ps[:, n % NBANK, :]
                        cols = slice(m // KC * HALF, (m // KC + 1) * HALF)
                        for b in (lo, lo + 1):
                            last = mm(bank, X[:, b, m % KC * P:(m % KC + 1) * P], CT[:, b, cols],
                                      start=b == 0, stop=b == NB - 1)
                        if lo + 2 == NB:
                            last.then_inc(tile_full, 1)
                transposes(f"xT{layer}", X, x_rows, (layer - 1) * NB)
                pe.wait_ge(ld_l[layer - 1], 32)

                def mean_step(b):
                    pe.wait_ge(dve_drained, drains(h_tile(2, b)))
                    last = mm(free_bank(first["bn_mean"]), ones[:, :], HR[:, b, :], start=b == 0, stop=b == NB - 1)
                    if b == NB - 1:
                        last.then_inc(bn_sums, 1)

                for b in range(NB):
                    n = h_tile(layer, b)
                    pe.wait_ge(act_drained, drains(first[f"xT{layer}"] + KC * (b // 4) + KC - 1))
                    bank = free_bank(n)
                    for k in range(KC):
                        mm(bank, TR[:, k, b * P:(b + 1) * P], W[:, wn + k, :], start=k == 0, stop=False)
                    for k in range(KC):
                        last = mm(bank, XT[:, k, b * P:(b + 1) * P], W[:, ws + k, :], start=False, stop=k == KC - 1)
                    last.then_inc(tile_full, 2 if layer == 2 and b == 0 else 1)
                    if layer == 2 and b:
                        mean_step(b - 1)
                if layer == 2:
                    mean_step(NB - 1)
                    bank = free_bank(first["bn_var"])
                    for b in range(NB):
                        pe.wait_ge(squared, b + 1)
                        last = mm(bank, ones[:, :], SQ[:, b, :], start=b == 0, stop=b == NB - 1)
                    last.then_inc(tile_full, 1)


_INS = ['x', 'src', 'dst', 'edge_attr_8', 'L0_gnn_Wq', 'L0_gnn_bq', 'L0_gnn_Wk', 'L0_gnn_bk', 'L0_gnn_Wv', 'L0_gnn_bv',
        'L0_gnn_Wo', 'L0_gnn_bo', 'L0_gnn_ln1_g', 'L0_gnn_ln1_b', 'L0_gnn_ln2_g', 'L0_gnn_ln2_b', 'L0_gnn_W1',
        'L0_gnn_b1', 'L0_gnn_W2', 'L0_gnn_b2', 'L1_gnn_w_self', 'L1_gnn_w_neigh', 'L1_gnn_bias', 'L1_gnn_gamma',
        'L1_gnn_beta', 'L2_gnn_W_l', 'L2_gnn_b_l', 'L2_gnn_W_r', 'L2_gnn_gamma', 'L2_gnn_beta', 'L3_gnn_W_self',
        'L3_gnn_W_neigh', 'L3_gnn_bias', 'L3_gnn_gamma', 'L3_gnn_beta']


def kernel(**inputs):
    import numpy as _np
    import concourse.bacc as _bacc
    from concourse import mybir as _mybir
    from concourse.bass_utils import run_bass_kernel_spmd as _run

    nc = _bacc.Bacc("TRN2", target_bir_lowering=False, num_devices=1)
    f32 = _mybir.dt.float32
    arrays, args = {}, []
    for name in _INS:
        a = _np.ascontiguousarray(inputs[name])
        arrays[f"in_{name}"] = a
        args.append(nc.dram_tensor(f"in_{name}", a.shape, _mybir.dt.from_np(a.dtype), kind="ExternalInput").ap())
    args.append(nc.dram_tensor("kv_table", (N, 2 * C), f32).ap())
    args.append(nc.dram_tensor("records", (P * NT, RW), f32).ap())
    args.append(nc.dram_tensor("weights_t", (6, C, C), f32).ap())
    args.append(nc.dram_tensor("out", (N, C), f32, kind="ExternalOutput").ap())
    gnn(nc, *args)
    r = _run(nc, [arrays], core_ids=[0])
    return r.results[0]["out"]
```
